# Optimizing a Trainium2 kernel written in Bass

```python
import numpy as np
import jax
import jax.numpy as jnp

def _softmax(x, axis=-1):
    return jax.nn.softmax(x, axis=axis)

def _gelu(x):
    return jax.nn.gelu(x, approximate=True)

def _silu(x):
    return jax.nn.silu(x)

def _sigmoid(x):
    return jax.nn.sigmoid(x)

def _layernorm(x, axis=-1, eps=1e-05):
    m = jnp.mean(x, axis=axis, keepdims=True)
    v = jnp.var(x, axis=axis, keepdims=True)
    return (x - m) / jnp.sqrt(v + eps)

def _scatter_add(tgt, idx, src, axis=0):
    return tgt.at[idx].add(src)

def _segment_sum(src, seg, n):
    return jax.ops.segment_sum(src, seg, n)
kernel_name = 'mk_metaformer_d4_conv_nchw512_r4_a529e8'

def setup_inputs(seed: int=0):
    np.random.seed(seed)
    _w = jnp.asarray

    def _rec_inputs():
        import jax
        import jax.numpy as jnp
        _gk = jax.random.key(seed)
        x = 7.22e-05 + 1 * jax.random.normal(jax.random.fold_in(_gk, 1), (4, 128, 16, 16), jnp.float32)
        return x
    x = _rec_inputs()

    def _L0_conv_setup():
        import jax, jax.numpy as jnp
        import numpy as np
        B, C, OUT_C, PAB, H, W = (4, 128, 128, 16, 16, 16)

        def _conv(x, w, b, pad):
            y = jax.lax.conv_general_dilated(x, w, window_strides=(1, 1), padding=[(pad, pad), (pad, pad)], dimension_numbers=('NCHW', 'OIHW', 'NCHW'))
            return y + b[None, :, None, None]
        key = jax.random.key(seed)
        ks = jax.random.split(key, 9)
        s = 0.02
        return {'x': jax.random.normal(ks[0], (B, C, H, W), dtype=jnp.float32), 'w_top': jax.random.normal(ks[1], (PAB, C, 1, 1), dtype=jnp.float32) * s, 'b_top': jnp.zeros((PAB,), dtype=jnp.float32), 'w_center': jax.random.normal(ks[2], (PAB, C, 1, 1), dtype=jnp.float32) * s, 'b_center': jnp.zeros((PAB,), dtype=jnp.float32), 'w_bottom': jax.random.normal(ks[3], (C, C, 3, 3), dtype=jnp.float32) * s, 'b_bottom': jnp.zeros((C,), dtype=jnp.float32), 'w_out': jax.random.normal(ks[4], (OUT_C, C, 3, 3), dtype=jnp.float32) * s, 'b_out': jnp.zeros((OUT_C,), dtype=jnp.float32)}
    _L0_conv_all = _L0_conv_setup()
    _L0_conv_in = {k: v for k, v in _L0_conv_all.items() if k in ('w_top', 'b_top', 'w_center', 'b_center', 'w_bottom', 'b_bottom', 'w_out', 'b_out')}
    del _L0_conv_all

    def _L0_ffn_setup():
        import jax, jax.numpy as jnp
        import numpy as np
        SINKHORN_ITERS = 8
        TEMPERATURE = 1.0
        EPS = 1e-10

        def sinkhorn(gates):
            t = jnp.log(jnp.clip(gates, EPS)) / TEMPERATURE

            def body(t, _):
                t = t - jax.nn.logsumexp(t, axis=-2, keepdims=True)
                t = t - jax.nn.logsumexp(t, axis=-1, keepdims=True)
                return (t, None)
            t, _ = jax.lax.scan(body, t, None, length=SINKHORN_ITERS)
            return jnp.exp(t)
        key = jax.random.key(seed)
        k1, k2, k3 = jax.random.split(key, 3)
        b, n, d, e, h = (4, 2048, 128, 8, 1)
        x = jax.random.normal(k1, (b, n, d), dtype=jnp.float32)
        gate_w = jax.random.normal(k2, (h, d, e), dtype=jnp.float32)
        experts = jax.random.normal(k3, (e, d, d), dtype=jnp.float32) / np.sqrt(d)
        return {'x': x, 'gate_w': gate_w, 'experts': experts}
    _L0_ffn_all = _L0_ffn_setup()
    _L0_ffn_in = {k: v for k, v in _L0_ffn_all.items() if k in ('gate_w', 'experts')}
    del _L0_ffn_all

    def _L1_conv_setup():
        import jax, jax.numpy as jnp
        import numpy as np
        B, C, H, W, K = (16, 128, 16, 16, 7)
        LN_EPS = 1e-05
        key = jax.random.key(seed)
        ks = jax.random.split(key, 6)
        x = jax.random.normal(ks[0], (B, C, H, W), dtype=jnp.float32)
        K_w = jax.random.normal(ks[1], (K * K, C), dtype=jnp.float32) * 0.02
        K_b = jnp.zeros((K * K,), dtype=jnp.float32)
        conv0_w = jax.random.normal(ks[2], (C, C), dtype=jnp.float32) * 0.02
        conv0_b = jnp.zeros((C,), dtype=jnp.float32)
        ln_w = jnp.ones((C, K, K), dtype=jnp.float32)
        ln_b = jnp.zeros((C, K, K), dtype=jnp.float32)
        conv1_w = jax.random.normal(ks[3], (C, C), dtype=jnp.float32) * 0.02
        conv1_b = jnp.zeros((C,), dtype=jnp.float32)
        return {'x': x, 'K_w': K_w, 'K_b': K_b, 'conv0_w': conv0_w, 'conv0_b': conv0_b, 'ln_w': ln_w, 'ln_b': ln_b, 'conv1_w': conv1_w, 'conv1_b': conv1_b}
    _L1_conv_all = _L1_conv_setup()
    _L1_conv_in = {k: v for k, v in _L1_conv_all.items() if k in ('K_w', 'K_b', 'conv0_w', 'conv0_b', 'ln_w', 'ln_b', 'conv1_w', 'conv1_b')}
    del _L1_conv_all

    def _L1_ffn_setup():
        import jax, jax.numpy as jnp
        import numpy as np
        D_MODEL = 128
        D_FF = 512
        NUM_EXPERTS = 8
        TOP_K = 2
        key = jax.random.key(seed)
        k_x, k_g, k_w1, k_w2 = jax.random.split(key, 4)
        x = jax.random.normal(k_x, (8, 1024, D_MODEL), dtype=jnp.float32)
        Wg = jax.random.normal(k_g, (D_MODEL, NUM_EXPERTS), dtype=jnp.float32) * (1.0 / np.sqrt(D_MODEL))
        W1 = jax.random.normal(k_w1, (NUM_EXPERTS, D_MODEL, D_FF), dtype=jnp.float32) * (1.0 / np.sqrt(D_MODEL))
        W2 = jax.random.normal(k_w2, (NUM_EXPERTS, D_FF, D_MODEL), dtype=jnp.float32) * (1.0 / np.sqrt(D_FF))
        return {'x': x, 'Wg': Wg, 'W1': W1, 'W2': W2}
    _L1_ffn_all = _L1_ffn_setup()
    _L1_ffn_in = {k: v for k, v in _L1_ffn_all.items() if k in ('Wg', 'W1', 'W2')}
    del _L1_ffn_all

    def _L2_conv_setup():
        import jax, jax.numpy as jnp
        import numpy as np
        from jax import lax
        key = jax.random.key(seed)
        k1, k2, k3 = jax.random.split(key, 3)
        B, C, H, W = (32, 128, 56, 56)
        K = 3
        x = jax.random.normal(k1, (B, C, H, W), dtype=jnp.float32)
        w_offset = jax.random.normal(k2, (K, 1, K), dtype=jnp.float32) * 0.1
        w_deform = jax.random.normal(k3, (1, 1, K), dtype=jnp.float32) * 0.5
        b_deform = jnp.zeros((1,), dtype=jnp.float32)
        return {'x': x, 'w_offset': w_offset, 'w_deform': w_deform, 'b_deform': b_deform}
    _L2_conv_all = _L2_conv_setup()
    _L2_conv_in = {k: v for k, v in _L2_conv_all.items() if k in ('w_offset', 'w_deform', 'b_deform')}
    del _L2_conv_all

    def _L2_ffn_setup():
        import jax, jax.numpy as jnp
        import numpy as np
        B, L, D, H, E, K = (8, 2048, 128, 512, 8, 2)
        SCALE = 0.02
        key = jax.random.key(seed)
        ks = jax.random.split(key, 6)
        return {'x': jax.random.normal(ks[0], (B, L, D), dtype=jnp.float32), 'Wg': jax.random.normal(ks[1], (D, E), dtype=jnp.float32) * SCALE, 'W1': jax.random.normal(ks[2], (E, D, H), dtype=jnp.float32) * SCALE, 'b1': jax.random.normal(ks[3], (E, H), dtype=jnp.float32) * SCALE, 'W2': jax.random.normal(ks[4], (E, H, D), dtype=jnp.float32) * SCALE, 'b2': jax.random.normal(ks[5], (E, D), dtype=jnp.float32) * SCALE}
    _L2_ffn_all = _L2_ffn_setup()
    _L2_ffn_in = {k: v for k, v in _L2_ffn_all.items() if k in ('Wg', 'W1', 'b1', 'W2', 'b2')}
    del _L2_ffn_all

    def _L3_conv_setup():
        import jax, jax.numpy as jnp
        import numpy as np
        TH = 0.01
        H = 56
        W = 56
        key = jax.random.key(seed)
        k1, k2 = jax.random.split(key)
        x = jax.random.uniform(k1, (32, 128, 56, 56), dtype=jnp.float32)
        conv_w = jax.random.normal(k2, (128, 1, 1, 1), dtype=jnp.float32)
        scale = jnp.ones((1,), dtype=jnp.float32)
        wf = jnp.ones((1,), dtype=jnp.float32)
        return {'x': x, 'conv_w': conv_w, 'scale': scale, 'wf': wf}
    _L3_conv_all = _L3_conv_setup()
    _L3_conv_in = {k: v for k, v in _L3_conv_all.items() if k in ('conv_w', 'scale', 'wf')}
    del _L3_conv_all

    def _L3_ffn_setup():
        import jax, jax.numpy as jnp
        import numpy as np
        NUM_EXPERTS = 8
        TOP_K = 2
        key = jax.random.key(seed)
        ks = jax.random.split(key, 4)
        B, S, D, F, E = (4, 1024, 128, 256, NUM_EXPERTS)
        x = jax.random.normal(ks[0], (B, S, D), dtype=jnp.float32)
        w1 = jax.random.normal(ks[1], (E, D, F), dtype=jnp.float32) * 0.02
        b1 = jnp.zeros((E, F), dtype=jnp.float32)
        w2 = jax.random.normal(ks[2], (E, F, D), dtype=jnp.float32) * 0.02
        b2 = jnp.zeros((E, D), dtype=jnp.float32)
        wg = jax.random.normal(ks[3], (D, E), dtype=jnp.float32) * 0.02
        bg = jnp.zeros((E,), dtype=jnp.float32)
        return {'x': x, 'w1': w1, 'b1': b1, 'w2': w2, 'b2': b2, 'wg': wg, 'bg': bg}
    _L3_ffn_all = _L3_ffn_setup()
    _L3_ffn_in = {k: v for k, v in _L3_ffn_all.items() if k in ('w1', 'b1', 'w2', 'b2', 'wg', 'bg')}
    del _L3_ffn_all
    return {'x': x, 'L0_conv_w_top': _L0_conv_in['w_top'], 'L0_conv_b_top': _L0_conv_in['b_top'], 'L0_conv_w_center': _L0_conv_in['w_center'], 'L0_conv_b_center': _L0_conv_in['b_center'], 'L0_conv_w_bottom': _L0_conv_in['w_bottom'], 'L0_conv_b_bottom': _L0_conv_in['b_bottom'], 'L0_conv_w_out': _L0_conv_in['w_out'], 'L0_conv_b_out': _L0_conv_in['b_out'], 'L0_ffn_gate_w': _L0_ffn_in['gate_w'], 'L0_ffn_experts': _L0_ffn_in['experts'], 'L1_conv_K_w': _L1_conv_in['K_w'], 'L1_conv_K_b': _L1_conv_in['K_b'], 'L1_conv_conv0_w': _L1_conv_in['conv0_w'], 'L1_conv_conv0_b': _L1_conv_in['conv0_b'], 'L1_conv_ln_w': _L1_conv_in['ln_w'], 'L1_conv_ln_b': _L1_conv_in['ln_b'], 'L1_conv_conv1_w': _L1_conv_in['conv1_w'], 'L1_conv_conv1_b': _L1_conv_in['conv1_b'], 'L1_ffn_Wg': _L1_ffn_in['Wg'], 'L1_ffn_W1': _L1_ffn_in['W1'], 'L1_ffn_W2': _L1_ffn_in['W2'], 'L2_conv_w_offset': _L2_conv_in['w_offset'], 'L2_conv_w_deform': _L2_conv_in['w_deform'], 'L2_conv_b_deform': _L2_conv_in['b_deform'], 'L2_ffn_Wg': _L2_ffn_in['Wg'], 'L2_ffn_W1': _L2_ffn_in['W1'], 'L2_ffn_b1': _L2_ffn_in['b1'], 'L2_ffn_W2': _L2_ffn_in['W2'], 'L2_ffn_b2': _L2_ffn_in['b2'], 'L3_conv_conv_w': _L3_conv_in['conv_w'], 'L3_conv_scale': _L3_conv_in['scale'], 'L3_conv_wf': _L3_conv_in['wf'], 'L3_ffn_w1': _L3_ffn_in['w1'], 'L3_ffn_b1': _L3_ffn_in['b1'], 'L3_ffn_w2': _L3_ffn_in['w2'], 'L3_ffn_b2': _L3_ffn_in['b2'], 'L3_ffn_wg': _L3_ffn_in['wg'], 'L3_ffn_bg': _L3_ffn_in['bg']}

def reference(x, L0_conv_w_top, L0_conv_b_top, L0_conv_w_center, L0_conv_b_center, L0_conv_w_bottom, L0_conv_b_bottom, L0_conv_w_out, L0_conv_b_out, L0_ffn_gate_w, L0_ffn_experts, L1_conv_K_w, L1_conv_K_b, L1_conv_conv0_w, L1_conv_conv0_b, L1_conv_ln_w, L1_conv_ln_b, L1_conv_conv1_w, L1_conv_conv1_b, L1_ffn_Wg, L1_ffn_W1, L1_ffn_W2, L2_conv_w_offset, L2_conv_w_deform, L2_conv_b_deform, L2_ffn_Wg, L2_ffn_W1, L2_ffn_b1, L2_ffn_W2, L2_ffn_b2, L3_conv_conv_w, L3_conv_scale, L3_conv_wf, L3_ffn_w1, L3_ffn_b1, L3_ffn_w2, L3_ffn_b2, L3_ffn_wg, L3_ffn_bg):
    import jax
    import jax.numpy as jnp

    def _L0_conv_ref(x, w_top, b_top, w_center, b_center, w_bottom, b_bottom, w_out, b_out):
        import jax, jax.numpy as jnp
        import numpy as np
        B, C, OUT_C, PAB, H, W = (4, 128, 128, 16, 16, 16)

        def _conv(x, w, b, pad):
            y = jax.lax.conv_general_dilated(x, w, window_strides=(1, 1), padding=[(pad, pad), (pad, pad)], dimension_numbers=('NCHW', 'OIHW', 'NCHW'))
            return y + b[None, :, None, None]
        bsz, c, h, w = x.shape
        hw = h * w
        x_top = _conv(x, w_top, b_top, 0).reshape(bsz, -1, hw)
        x_center = _conv(x, w_center, b_center, 0).reshape(bsz, -1, hw)
        x_bottom = _conv(x, w_bottom, b_bottom, 1).reshape(bsz, c, hw)
        x_center = jnp.swapaxes(x_center, 1, 2)
        x_bottom = jnp.swapaxes(x_bottom, 1, 2)
        sp_map = jnp.einsum('bnp,bpm->bnm', x_center, x_top)
        sp_map = jax.nn.softmax(sp_map.reshape(bsz, -1), axis=1).reshape(bsz, hw, hw)
        sp_map = jnp.einsum('bnm,bmc->bnc', sp_map, x_bottom)
        sp_map = sp_map.reshape(bsz, c, h, w)
        return _conv(x + sp_map, w_out, b_out, 1)

    def _L0_ffn_ref(x, gate_w, experts):
        import jax, jax.numpy as jnp
        import numpy as np
        SINKHORN_ITERS = 8
        TEMPERATURE = 1.0
        EPS = 1e-10

        def sinkhorn(gates):
            t = jnp.log(jnp.clip(gates, EPS)) / TEMPERATURE

            def body(t, _):
                t = t - jax.nn.logsumexp(t, axis=-2, keepdims=True)
                t = t - jax.nn.logsumexp(t, axis=-1, keepdims=True)
                return (t, None)
            t, _ = jax.lax.scan(body, t, None, length=SINKHORN_ITERS)
            return jnp.exp(t)
        b, n, d = x.shape
        h = gate_w.shape[0]
        e = experts.shape[0]
        N = b * n
        m = n // e
        x4 = x[:, None]
        gates = jnp.einsum('bhnd,hde->bhne', x4, gate_w)
        xf = jnp.transpose(x4, (1, 0, 2, 3)).reshape(h, N, d)
        gf = jnp.transpose(gates, (1, 0, 2, 3)).reshape(h, N, e)
        cg = sinkhorn(gf)
        vals, idx = jax.lax.top_k(jnp.transpose(cg, (0, 2, 1)), m)
        gate_values = (vals > 0.5).astype(x.dtype)
        gate_values = jnp.transpose(gate_values, (0, 2, 1))
        idx = jnp.transpose(idx, (0, 2, 1))
        routed = xf[jnp.arange(h)[:, None, None], idx]
        outputs = jnp.einsum('hmei,eio->hmeo', routed, experts)
        outputs = outputs * gate_values[..., None]
        o_dim = outputs.shape[-1]
        src = outputs.reshape(h, m * e, o_dim)
        idx_flat = idx.reshape(h, m * e)

        def combine(idxf, srcf):
            s = jnp.zeros((N, o_dim), srcf.dtype).at[idxf].add(srcf)
            c = jnp.zeros((N,), srcf.dtype).at[idxf].add(1.0)
            return s / (c + 1.0)[:, None]
        out = jax.vmap(combine)(idx_flat, src)
        out = out.reshape(h, b, n, o_dim)
        out = jnp.transpose(out, (1, 0, 2, 3))[:, 0]
        return out

    def _L1_conv_ref(x, K_w, K_b, conv0_w, conv0_b, ln_w, ln_b, conv1_w, conv1_b):
        import jax, jax.numpy as jnp
        import numpy as np
        B, C, H, W, K = (16, 128, 16, 16, 7)
        LN_EPS = 1e-05
        b, c, h, w = x.shape
        kk = K_w.shape[0]
        k = int(round(kk ** 0.5))
        hw = h * w
        query = x.reshape(b, c, hw)
        key = jnp.einsum('bchw,oc->bohw', x, K_w) + K_b[None, :, None, None]
        key = key.reshape(b, kk, hw).transpose(0, 2, 1)
        key = jax.nn.softmax(key, axis=1)
        filters = jnp.einsum('bcn,bnk->bck', query, key).reshape(b, c, k, k)
        filters = jnp.einsum('bcij,oc->boij', filters, conv0_w) + conv0_b[None, :, None, None]
        mean = jnp.mean(filters, axis=(1, 2, 3), keepdims=True)
        var = jnp.var(filters, axis=(1, 2, 3), keepdims=True)
        filters = (filters - mean) * jax.lax.rsqrt(var + LN_EPS)
        filters = filters * ln_w[None] + ln_b[None]
        filters = jax.nn.relu(filters)
        filters = jnp.einsum('bcij,oc->boij', filters, conv1_w) + conv1_b[None, :, None, None]
        wgt = filters.reshape(b * c, 1, k, k)
        x_r = x.reshape(1, b * c, h, w)
        pad = k // 2
        out = jax.lax.conv_general_dilated(x_r, wgt, window_strides=(1, 1), padding=[(pad, pad), (pad, pad)], feature_group_count=b * c, dimension_numbers=('NCHW', 'OIHW', 'NCHW'))
        return out.reshape(b, c, h, w)

    def _L1_ffn_ref(x, Wg, W1, W2):
        import jax, jax.numpy as jnp
        import numpy as np
        D_MODEL = 128
        D_FF = 512
        NUM_EXPERTS = 8
        TOP_K = 2
        B, S, D = x.shape
        E = Wg.shape[-1]
        router_logits = jnp.einsum('bsd,de->bse', x, Wg)
        top_logits, top_idx = jax.lax.top_k(router_logits, TOP_K)
        top_w = jax.nn.softmax(top_logits, axis=-1)
        combine = jnp.sum(jax.nn.one_hot(top_idx, E, dtype=x.dtype) * top_w[..., None], axis=-2)
        xt = x.reshape(B * S, D)
        cw = combine.reshape(B * S, E)
        out = jnp.zeros_like(xt)
        for e in range(E):
            h = jax.nn.silu(xt @ W1[e]) @ W2[e]
            out = out + cw[:, e:e + 1] * h
        return out.reshape(B, S, D)

    def _L2_conv_ref(x, w_offset, w_deform, b_deform):
        import jax, jax.numpy as jnp
        import numpy as np
        from jax import lax
        B, C, H, W = x.shape
        K = w_offset.shape[0]
        pad = (K - 1) // 2
        pooled = jnp.mean(x, axis=(2, 3))
        seq = pooled[:, None, :]
        offset = lax.conv_general_dilated(seq, w_offset, window_strides=(1,), padding=[(pad, pad)], dimension_numbers=('NCH', 'OIH', 'NCH'))
        i_idx = jnp.arange(C, dtype=jnp.float32)
        k_idx = jnp.arange(K, dtype=jnp.float32)
        base = i_idx[None, :] + k_idx[:, None] - pad
        p = jnp.clip(base[None] + offset, 0.0, C - 1.0)
        p0 = jnp.floor(p)
        frac = p - p0
        idx0 = p0.astype(jnp.int32)
        idx1 = jnp.minimum(idx0 + 1, C - 1)
        pooled_b = pooled[:, None, :]
        g0 = jnp.take_along_axis(jnp.broadcast_to(pooled_b, p.shape), idx0, axis=2)
        g1 = jnp.take_along_axis(jnp.broadcast_to(pooled_b, p.shape), idx1, axis=2)
        samp = g0 * (1.0 - frac) + g1 * frac
        out = jnp.einsum('bkc,k->bc', samp, w_deform[0, 0]) + b_deform[0]
        gate = jax.nn.sigmoid(out)[:, :, None, None]
        return x * gate

    def _L2_ffn_ref(x, Wg, W1, b1, W2, b2):
        import jax, jax.numpy as jnp
        import numpy as np
        B, L, D, H, E, K = (8, 2048, 128, 512, 8, 2)
        SCALE = 0.02
        b, l, d = x.shape
        xt = x.reshape(-1, d)
        T = xt.shape[0]
        gate = jax.nn.softmax(xt @ Wg, axis=-1)
        topv, topi = jax.lax.top_k(gate, K)
        topv = topv / (jnp.sum(topv, axis=-1, keepdims=True) + 1e-06)
        scores = jnp.zeros((T, E), dtype=xt.dtype).at[jnp.arange(T)[:, None], topi].set(topv)
        out = jnp.zeros_like(xt)
        for e in range(E):
            h = jax.nn.gelu(xt @ W1[e] + b1[e], approximate=False)
            ye = h @ W2[e] + b2[e]
            out = out + ye * scores[:, e:e + 1]
        return out.reshape(b, l, d)

    def _L3_conv_ref(x, conv_w, scale, wf):
        import jax, jax.numpy as jnp
        import numpy as np
        TH = 0.01
        H = 56
        W = 56
        B, C, _, _ = x.shape
        alpha = jnp.sum(x, axis=(2, 3)) / (H * W)
        sal = jnp.einsum('bchw,bc->bhw', x, alpha) / C
        w = conv_w.reshape(1, -1, 1, 1)
        fm = sal[:, None, :, :] * w
        fm = jax.nn.relu(fm)
        fm = jnp.where(fm > TH, fm, 0.0)
        return 1.0 - wf * jax.nn.sigmoid(scale * fm)

    def _L3_ffn_ref(x, w1, b1, w2, b2, wg, bg):
        import jax, jax.numpy as jnp
        import numpy as np
        NUM_EXPERTS = 8
        TOP_K = 2
        B, S, D = x.shape
        E = wg.shape[1]
        xf = x.reshape(-1, D)
        logits = xf @ wg + bg
        top_vals, top_idx = jax.lax.top_k(logits, TOP_K)
        gate_w = jax.nn.softmax(top_vals, axis=-1)
        onehot = jax.nn.one_hot(top_idx, E, dtype=x.dtype)
        combine = jnp.einsum('tke,tk->te', onehot, gate_w)
        h = jax.nn.relu(jnp.einsum('td,edf->etf', xf, w1) + b1[:, None, :])
        y = jnp.einsum('etf,efd->etd', h, w2) + b2[:, None, :]
        out = jnp.einsum('etd,te->td', y, combine)
        return out.reshape(B, S, D)

    def _gn(v, G=32, eps=1e-05):
        B_, C_, H_, W_ = v.shape
        g = v.reshape(B_, G, C_ // G, H_, W_)
        m = jnp.mean(g, axis=(2, 3, 4), keepdims=True)
        s = jnp.var(g, axis=(2, 3, 4), keepdims=True)
        return ((g - m) / jnp.sqrt(s + eps)).reshape(v.shape)

    def _ln_c(v, eps=1e-06):
        m = jnp.mean(v, axis=1, keepdims=True)
        s = jnp.var(v, axis=1, keepdims=True)
        return (v - m) / jnp.sqrt(s + eps)

    def _ln_t(v, eps=1e-05):
        m = jnp.mean(v, axis=-1, keepdims=True)
        s = jnp.var(v, axis=-1, keepdims=True)
        return (v - m) / jnp.sqrt(s + eps)

    def _to_tokens(v):
        B_, C_, H_, W_ = v.shape
        return v.reshape(B_, C_, H_ * W_).transpose(0, 2, 1)

    def _from_tokens(t, like):
        B_, C_, H_, W_ = like.shape
        return t.transpose(0, 2, 1).reshape(B_, C_, H_, W_)
    x = x + _L0_conv_ref(_ln_c(x), L0_conv_w_top, L0_conv_b_top, L0_conv_w_center, L0_conv_b_center, L0_conv_w_bottom, L0_conv_b_bottom, L0_conv_w_out, L0_conv_b_out)
    t = _to_tokens(x)
    t = t + _L0_ffn_ref(_ln_t(t), L0_ffn_gate_w, L0_ffn_experts)
    x = _from_tokens(t, x)
    x = x + _L1_conv_ref(_ln_c(x), L1_conv_K_w, L1_conv_K_b, L1_conv_conv0_w, L1_conv_conv0_b, L1_conv_ln_w, L1_conv_ln_b, L1_conv_conv1_w, L1_conv_conv1_b)
    t = _to_tokens(x)
    t = t + _L1_ffn_ref(_ln_t(t), L1_ffn_Wg, L1_ffn_W1, L1_ffn_W2)
    x = _from_tokens(t, x)
    x = x + _L2_conv_ref(_ln_c(x), L2_conv_w_offset, L2_conv_w_deform, L2_conv_b_deform)
    t = _to_tokens(x)
    t = t + _L2_ffn_ref(_ln_t(t), L2_ffn_Wg, L2_ffn_W1, L2_ffn_b1, L2_ffn_W2, L2_ffn_b2)
    x = _from_tokens(t, x)
    x = x + _L3_conv_ref(_ln_c(x), L3_conv_conv_w, L3_conv_scale, L3_conv_wf)
    t = _to_tokens(x)
    t = t + _L3_ffn_ref(_ln_t(t), L3_ffn_w1, L3_ffn_b1, L3_ffn_w2, L3_ffn_b2, L3_ffn_wg, L3_ffn_bg)
    x = _from_tokens(t, x)
    return x

_drawn_inputs = setup_inputs


def setup_inputs(seed=0):
    import zlib

    import numpy as np

    out = dict(_drawn_inputs(seed))
    spreads = {'L0_conv_b_top': (0.0, 0.8),
     'L0_conv_b_center': (0.0, 0.8),
     'L0_conv_b_bottom': (0.0, 0.8),
     'L0_conv_b_out': (0.0, 0.1),
     'L1_conv_K_b': (0.0, 2.0),
     'L1_conv_conv0_b': (0.0, 0.1),
     'L1_conv_ln_w': (1.0, 0.2),
     'L1_conv_ln_b': (0.0, 0.1),
     'L1_conv_conv1_b': (0.0, 0.1),
     'L3_ffn_b1': (0.0, 0.8),
     'L3_ffn_b2': (0.0, 0.278),
     'L3_ffn_bg': (0.0, 0.337)}
    factors = {'L0_conv_w_top': 8.0,
     'L0_conv_w_center': 8.0,
     'L0_conv_w_bottom': 8.0,
     'L2_conv_w_offset': 7.558,
     'L2_ffn_Wg': 3.537,
     'L2_ffn_W1': 3.397,
     'L2_ffn_b1': 8.0,
     'L2_ffn_W2': 3.317,
     'L2_ffn_b2': 8.0,
     'L3_conv_conv_w': 64.0,
     'L3_ffn_w1': 4.192,
     'L3_ffn_w2': 3.297}
    for name, (base, spread) in spreads.items():
        noise = np.random.default_rng([zlib.crc32(name.encode()), seed]).standard_normal(out[name].shape)
        drawn = base * np.exp(spread * noise) if base else spread * noise
        out[name] = jnp.asarray(drawn.astype(out[name].dtype))
    for name, factor in factors.items():
        out[name] = (out[name] * factor).astype(out[name].dtype)
    return out
```

```python
from contextlib import ExitStack

import numpy as np

import concourse.bass as bass
from concourse import mybir

F32 = mybir.dt.float32
F32R = mybir.dt.float32r
BF16 = mybir.dt.bfloat16
ALU = mybir.AluOpType
ACT = mybir.ActivationFunctionType
AX = mybir.AxisListType

C = 128
B = 4
SIDE = 16
PIX = SIDE * SIDE
N = B * PIX
HALF = N // 2
TT = N // C
PAD = SIDE + 2
PAB = 16
E = 8
TOPK0 = N // B // E
KW = 7
KK = KW * KW
PARTS = 3
TH = 0.01
SALIENCY_AREA = 56 * 56
BIG = 3.0e38

GRID = SIDE + KW // 2
FREQ = (GRID * GRID - 1) // 2
QF = -(-(1 + 3 * FREQ) // C)

PARAM = {}
for _name, _cols in [
    ("b_bottom", 1), ("b_out", 1), ("b_top", 1), ("b_center", 1), ("w_top", PAB), ("w_center", PAB),
    ("gate_w", E), ("K_w", KK), ("K_b", 1), ("conv0_w", C), ("conv0_b", 1), ("ln_w", KK), ("ln_b", KK),
    ("conv1_w", C), ("conv1_b", C), ("Wg1", E), ("w_offset", 9), ("w_deform", 3), ("b_deform", 1),
    ("Wg2", E), ("L2_b1", E * 4), ("L2_b2", E), ("conv_w", 1), ("scale", 1), ("wf", 1),
    ("wg3", E), ("bg3", E), ("L3_b1", E * 2), ("L3_b2", E),
]:
    PARAM[_name] = (sum(c for _, c in PARAM.values()), _cols)
PARAM_COLS = sum(c for _, c in PARAM.values())

CONST = {}
for _name, _cols in [("center", C), ("mean", C), ("ident", C), ("ones", C), ("shift", 3 * C), ("base", 3 * C),
                     ("rev", E), ("minus_i", 1), ("eps6", 1), ("eps5", 1), ("one", 1)]:
    CONST[_name] = (sum(c for _, c in CONST.values()), _cols)
CONST_COLS = sum(c for _, c in CONST.values())

UNITS = 2 * E
MOE = [
    dict(layer=1, ln=3, q=4, act="Silu", router="Wg1", b1=None, b2=None),
    dict(layer=2, ln=5, q=4, act="Gelu", router="Wg2", b1="L2_b1", b2="L2_b2"),
    dict(layer=3, ln=7, q=2, act="Relu", router="wg3", b1="L3_b1", b2="L3_b2"),
]
LN_EPS = ["eps6", "eps5"] * 4

SIGNALS = [
    "x_loaded", "params_loaded", "consts_loaded", "wb_loaded", "wo_loaded", "we_loaded", "dft_loaded", "sel_loaded",
    "moe1_loaded", "moe2_loaded", "moe3_loaded", "stored",
    "borders_zero", "routes_zero", "wb_split", "wo_split", "we_split", "pool_step",
    "centered", "squared", "variance", "log_var", "rstd", "normed", "norm_hi", "norm_lo",
    "dve_step",
    "proj_done", "top_ready", "center_ready", "scores_done", "score_max", "max_turned", "max_diag", "max_spread",
    "neg_max", "exp_done", "exp_summed", "exp_recip",
    "bottom_done", "bottom_biased", "bottom_turned", "bottom_ready", "mixed", "mix_added", "mix_hi", "mix_lo",
    "out_conv_done", "x1_ready",
    "gates_done", "expert_out", "expert_kept", "sink_in", "sink_sum", "plan_turned", "plan_ready",
    "picked", "picked_turned", "combined", "combined_turned", "x2_ready",
    "keys_done", "key_max", "key_exp", "key_soft", "key_turned", "key_ready", "img_turned", "img_ready",
    "filt_done", "filt_in", "filt0_done", "stat_in", "stat_sum", "filt_rstd_ln", "filt_rstd", "filt_act", "filt1_done", "filt1_ready",
    "img_freq", "img_freq_kept", "filt_freq", "freq_mult", "img_back", "x3_ready",
    "pooled_in", "offset_done", "pos_ready", "dist_done", "hat_ready", "deform_done", "deform_gate", "x5_ready",
    "alpha_in", "sal_done", "sal_ready", "sal_sig", "x7_ready",
    "logits_done", "exp_in", "exp_out", "route_parts", "route_turned", "route_ready",
    "w1_split", "w2_split", "hidden_sums", "score_sums", "bias_kept", "hidden", "hidden_hi_act", "hidden_hi_dve", "hidden_lo", "score_kept", "part_sums", "scaled",
    "state_added",
]


def metaformer(nc, dram, out):
    ctx = ExitStack()
    with ctx:
        def sb(name, shape, dt=F32, scope=ctx):
            return scope.enter_context(nc.sbuf_tensor(name, shape, dt))

        s = {name: ctx.enter_context(nc.semaphore(name)) for name in SIGNALS}

        x = sb("x", [C, N])
        xn = sb("xn", [C, N])
        xh = sb("xh", [C, N], F32R)
        xl = sb("xl", [C, N], F32R)
        sq = sb("sq", [C, N])
        rstd = sb("rstd", [C, N])
        par = sb("par", [C, PARAM_COLS])
        cst = sb("cst", [C, CONST_COLS])
        sel = sb("sel", [C, E + 1, C], BF16)
        routes = sb("routes", [C, N], BF16)
        wa = sb("wa", [C, E, 1024])
        wb = sb("wb", [C, E, 1024])
        dft_x = sb("dft_x", [C, 2, QF * C])
        dft_k = sb("dft_k", [KK, QF * C])
        dft_o = sb("dft_o", [C, QF, PIX])
        shiftw = sb("shiftw", [C, 3, C])
        small = sb("small", [C, 1024])
        cparts = sb("cparts", [C, TT, PARTS * E], BF16)
        ps = ctx.enter_context(nc.psum_tensor("ps", [C, 8, 512], F32))

        with ExitStack() as scope:
            xp = sb("xp", [C, B, PAD, PAD], scope=scope)
            xph = sb("xph", [C, B, PAD, PAD], F32R, scope)
            xpl = sb("xpl", [C, B, PAD, PAD], F32R, scope)
            yp = sb("yp", [C, B, PAD, PAD], scope=scope)
            w33 = sb("w33", [C, 2, 9 * C], scope=scope)
            w33h = sb("w33h", [C, 2, 9 * C], F32R, scope)
            w33l = sb("w33l", [C, 2, 9 * C], F32R, scope)
            expo = sb("expo", [C, B, 2, PIX], scope=scope)
            bot = sb("bot", [C, N], scope=scope)
            bot_t = sb("bot_t", [C, TT, C], scope=scope)
            top = sb("top", [PAB, N], scope=scope)
            cen = sb("cen", [PAB, N], scope=scope)
            we = sb("we", [C, E * C], scope=scope)
            weh = sb("weh", [C, E * C], F32R, scope)
            wel = sb("wel", [C, E * C], F32R, scope)
        picked = bot[0:E, :]
        with ExitStack() as scope:
            img_t = sb("img_t", [C, TT, C], scope=scope)
            keys = sb("keys", [KK, N], scope=scope)
            keye = sb("keye", [KK, N], scope=scope)
            key_t = sb("key_t", [C, TT, KK], scope=scope)
            filt = sb("filt", [C, 4, B, KK], scope=scope)
            filt_t = sb("filt_t", [KK, B * C], scope=scope)
            img_f = sb("img_f", [C, QF, B * C], scope=scope)
            prod_f = sb("prod_f", [C, QF, B * C], scope=scope)
        pos = img_f[:, 0:3, :].rearrange("p a (b c) -> p (a b) c", b=4)
        hat = prod_f[:, 0:3, :].rearrange("p a (b c) -> p (a b) c", b=4)
        spread = img_t[:, 0:4, :]
        fm = sq
        with ExitStack() as scope:
            hid = sb("hid", [C, 2, 4, 512], scope=scope)
            hidh = sb("hidh", [C, 2, 4, 512], F32R, scope)
            hidl = sb("hidl", [C, 2, 4, 512], F32R, scope)
            wst_h = sb("wst_h", [C, 2, 1024], F32R, scope)
            wst_l = sb("wst_l", [C, 2, 1024], F32R, scope)
        score = sq
        parts = rstd

        at = [0]

        def piece(cols, rows=C):
            at[0] += cols
            assert at[0] <= 1024
            return small[0:rows, at[0] - cols:at[0]]

        mx, mx4, mxd, nmx, es, rs = piece(4), piece(1, B), piece(4, B), piece(4), piece(4), piece(4)
        plan, r8, r8b, top8 = piece(64), piece(8), piece(8), piece(8, E)
        pick_w, cnt = piece(64), piece(8)
        kmx, kes, krs = piece(4, KK), piece(4, KK), piece(4, KK)
        st, mean4 = piece(4), piece(4)
        pool4, wpool, gate4 = piece(4), piece(12), piece(4)
        lg, lg2, ew, oh1, oh2, wgt, rem, m8 = [piece(64) for _ in range(7)] + [piece(8)]
        neg_wf, bias1 = piece(1), piece(4)

        def p(name, rows=C):
            at0, cols = PARAM[name]
            return par[0:rows, at0:at0 + cols]

        def k(name, rows=C):
            at0, cols = CONST[name]
            return cst[0:rows, at0:at0 + cols]

        ident = k("ident")

        def half(t, h):
            return t[:, h * HALF:(h + 1) * HALF]

        def bank(n, rows=C, cols=512, first=0):
            return ps[0:rows, n, first:first + cols]

        def f32(t):
            return t.bitcast(F32)

        def tiles(t):
            return t.rearrange("p (t e) -> p t e", e=E)

        def over(t, n):
            return t.unsqueeze(2).to_broadcast([t.shape[0], t.shape[1], n])

        def again(t, n):
            return t.unsqueeze(1).to_broadcast([t.shape[0], n, t.shape[1]])

        def inside(t, b):
            return t[:, b, 1:1 + SIDE, 1:1 + SIDE]

        def x_ready(eng, version, h):
            if version == 0:
                eng.wait_ge(s["x_loaded"], 32)
            elif version in (4, 6, 8):
                eng.wait_ge(s["state_added"], UNITS * (version // 2 - 1) - 1 + h)
            else:
                eng.wait_ge(s[f"x{version}_ready"], h + 1)

        def wait_count(eng, name, value):
            if not isinstance(value, int) or value > 0:
                eng.wait_ge(s[name], value)

        CHUNKS = [sum(MOE[j]["q"] for j in range(m)) * UNITS for m in range(3)]

        block = ctx.enter_context(nc.Block())

        @block.sync
        def _(sp):
            sp.dma_start(cst[:], dram["consts"]).then_inc(s["consts_loaded"], 16)
            for h in range(2):
                sp.dma_start(half(x, h).rearrange("p (b n) -> p b n", b=2),
                             dram["x"][2 * h:2 * h + 2].rearrange("b c n -> c b n")).then_inc(s["x_loaded"], 16)
            sp.dma_start(par[:], dram["params"]).then_inc(s["params_loaded"], 16)
            sp.dma_start(w33[:, 0], dram["w_bottom"]).then_inc(s["wb_loaded"], 16)
            sp.dma_start(w33[:, 1], dram["w_out"]).then_inc(s["wo_loaded"], 16)
            sp.dma_start(we[:], dram["w_experts"]).then_inc(s["we_loaded"], 16)
            sp.dma_start(wa[:], dram["moe1"]).then_inc(s["moe1_loaded"], 16)
            sp.dma_start(dft_x[:], dram["dft_x"]).then_inc(s["dft_loaded"], 16)
            sp.dma_start(dft_k[:], dram["dft_k"]).then_inc(s["dft_loaded"], 16)
            sp.dma_start(dft_o[:], dram["dft_o"]).then_inc(s["dft_loaded"], 16)
            sp.dma_start(sel[:], dram["sel"]).then_inc(s["sel_loaded"], 16)
            sp.wait_ge(s["x2_ready"], 2)
            sp.dma_start(wb[:], dram["moe2"]).then_inc(s["moe2_loaded"], 16)
            sp.wait_ge(s["w2_split"], E)
            sp.dma_start(wa[:, :, 0:512], dram["moe3"]).then_inc(s["moe3_loaded"], 16)
            for h in range(2):
                x_ready(sp, 8, h)
                sp.dma_start(out[2 * h:2 * h + 2].rearrange("b c n -> c b n"),
                             half(x, h).rearrange("p (b n) -> p b n", b=2)).then_inc(s["stored"], 16)
            sp.wait_ge(s["stored"], 32)

        @block.gpsimd
        def _(pool):
            pool.memset(xp[:], 0.0).then_inc(s["borders_zero"], 1)
            pool.memset(yp[:], 0.0).then_inc(s["borders_zero"], 1)
            pool.memset(routes[:], 0.0).then_inc(s["routes_zero"], 1)

            def split(hi, lo, src, done, n):
                pool.tensor_copy(hi, src).then_inc(s["pool_step"], 1)
                pool.wait_ge(s["pool_step"], n)
                pool.tensor_tensor(lo, src, f32(hi), ALU.subtract).then_inc(done, 1)

            pool.wait_ge(s["wb_loaded"], 16)
            split(w33h[:, 0], w33l[:, 0], w33[:, 0], s["wb_split"], 1)
            pool.wait_ge(s["wo_loaded"], 16)
            split(w33h[:, 1], w33l[:, 1], w33[:, 1], s["wo_split"], 2)
            pool.wait_ge(s["we_loaded"], 16)
            split(weh[:], wel[:], we[:], s["we_split"], 3)

            for m, spec in enumerate(MOE):
                src = wb if spec["layer"] == 2 else wa
                unit0 = UNITS * m
                if m == 0:
                    x_ready(pool, 2, 1)
                pool.wait_ge(s[f"moe{spec['layer']}_loaded"], 16)

                def split_half(e, q, first, done):
                    at0, at1 = first * spec["q"] * C, (first + 1) * spec["q"] * C
                    pool.tensor_copy(wst_h[:, q, at0:at1], src[:, e, at0:at1])
                    pool.drain()
                    pool.tensor_tensor(wst_l[:, q, at0:at1], src[:, e, at0:at1], f32(wst_h[:, q, at0:at1]),
                                       ALU.subtract).then_inc(s[done], 1)

                def split_first(e, q):
                    wait_count(pool, "hidden_sums", e * (2 * spec["q"]) + (CHUNKS[m] - 2 * spec["q"]))
                    split_half(e, q, 0, "w1_split")

                def split_second(e, q):
                    wait_count(pool, "part_sums", e * 2 + (unit0 - 2))
                    split_half(e, q, 1, "w2_split")

                def add_parts(e):
                    for h in range(2):
                        pool.wait_ge(s["scaled"], e * 2 + (unit0 + h + 1))
                        pool.tensor_tensor(half(x, h), half(x, h), half(parts, h), ALU.add).then_inc(s["state_added"], 1)

                for q in range(2):
                    split_first(q, q)
                    split_second(q, q)
                with pool.Fori(0, E // 2 - 1) as i:
                    for q in range(2):
                        split_first(i * 2 + (q + 2), q)
                        add_parts(i * 2 + q)
                        split_second(i * 2 + (q + 2), q)
                for q in range(2):
                    add_parts(E - 2 + q)

        @block.tensor
        def _(pe):
            def mm3(o, wh, wl, xhi, xlo, start=True, stop=True):
                pe.matmul(o, wh, xhi, start=start, stop=False)
                pe.matmul(o, wl, xhi, start=False, stop=False)
                return pe.matmul(o, wh, xlo, start=False, stop=stop)

            def norm(n):
                for h in range(2):
                    x_ready(pe, n, h)
                    pe.matmul(bank(h), k("center"), half(x, h), start=True, stop=True).then_inc(s["centered"], 1)
                for h in range(2):
                    pe.wait_ge(s["squared"], 2 * n + h + 1)
                    pe.matmul(bank(2 + h), k("mean"), half(sq, h), start=True, stop=True).then_inc(s["variance"], 1)

            pe.wait_ge(s["consts_loaded"], 16)
            norm(0)
            pe.wait_ge(s["params_loaded"], 16)
            for h in range(2):
                pe.wait_ge(s["normed"], h + 1)
                window = xp[:, 2 * h:2 * h + 2, 1:1 + SIDE, 1:1 + SIDE]
                for w, b0 in (("w_top", 0), ("w_center", 2)):
                    pe.matmul(bank(b0 + h, PAB), p(w), window, start=True, stop=True).then_inc(s["proj_done"], 1)

            def conv33(which, hi, lo, hi_done, lo_done, n0, done, halves=(0, 1)):
                for h in halves:
                    pe.wait_ge(hi_done, n0 + h + 1)
                    pe.wait_ge(lo_done, n0 + h + 1)
                    for t in range(9):
                        dy, dx = divmod(t, 3)
                        wh = w33h[:, which, t * C:(t + 1) * C]
                        wl = w33l[:, which, t * C:(t + 1) * C]
                        win = (slice(None), slice(2 * h, 2 * h + 2), slice(dy, dy + SIDE), slice(dx, dx + SIDE))
                        last = mm3(bank(4 + h), wh, wl, hi[win], lo[win], start=(t == 0), stop=(t == 8))
                    last.then_inc(done, 1)

            for b in range(B):
                if b % 2 == 0:
                    pe.wait_ge(s["top_ready"], 2)
                    pe.wait_ge(s["center_ready"], 2)
                for j in range(2):
                    last = pe.matmul(bank(b, cols=PIX, first=j * PIX), top[:, b * PIX + j * C:b * PIX + (j + 1) * C],
                                     cen[:, b * PIX:(b + 1) * PIX], start=True, stop=True)
                last.then_inc(s["scores_done"], 1)
            pe.wait_ge(s["wb_split"], 1)
            conv33(0, xph, xpl, s["norm_hi"], s["norm_lo"], 0, s["bottom_done"], halves=(0,))
            pe.wait_ge(s["score_max"], B)
            pe.transpose(bank(6, B, C), mx, ident).then_inc(s["max_turned"], 1)
            pe.wait_ge(s["max_diag"], 1)
            pe.matmul(bank(6, cols=B, first=256), k("ones", B), mxd, start=True, stop=True).then_inc(s["max_spread"], 1)
            conv33(0, xph, xpl, s["norm_hi"], s["norm_lo"], 0, s["bottom_done"], halves=(1,))
            pe.wait_ge(s["neg_max"], 1)
            for t in range(TT):
                if t % 4 == 0:
                    pe.wait_ge(s["bottom_biased"], t // 4 + 1)
                last = pe.transpose(bank(6 + t // 4, cols=C, first=t % 4 * C), bot[:, t * C:(t + 1) * C], ident)
                if t % 4 == 3:
                    last.then_inc(s["bottom_turned"], 1)
            pe.wait_ge(s["exp_done"], B)
            pe.matmul(bank(4, cols=B), k("ones"), es, start=True, stop=True).then_inc(s["exp_summed"], 1)
            pe.wait_ge(s["bottom_ready"], 2)
            for b in range(B):
                for par_ in range(2):
                    for j in range(2):
                        last = pe.matmul(bank(6 + b // 2, cols=C, first=(b % 2) * PIX + par_ * C),
                                         expo[:, b, j, par_::2], bot_t[:, 2 * b + j, :], start=(j == 0), stop=(j == 1))
                last.then_inc(s["mixed"], 1)
            pe.wait_ge(s["wo_split"], 1)
            pe.wait_ge(s["exp_recip"], 1)
            conv33(1, xph, xpl, s["mix_hi"], s["mix_lo"], 0, s["out_conv_done"])

            norm(1)
            pe.wait_ge(s["normed"], 4)
            for t in range(TT):
                last = pe.matmul(bank(4, cols=E, first=t * E), xn[:, t * C:(t + 1) * C], p("gate_w"), start=True, stop=True)
            last.then_inc(s["gates_done"], 1)
            pe.wait_ge(s["norm_hi"], 4)
            pe.wait_ge(s["norm_lo"], 4)
            pe.wait_ge(s["we_split"], 1)
            ring = [0, 1, 6, 7]

            def expert_rows(n):
                t, g = divmod(n, 2)
                if n >= 4:
                    pe.wait_ge(s["expert_kept"], n - 3)
                o = bank(ring[n % 4])
                cols, ecols = slice(t * C, (t + 1) * C), slice(g * 512, (g + 1) * 512)
                pe.matmul(o, xh[:, cols], weh[:, ecols], start=True, stop=False)
                pe.matmul(o, xh[:, cols], wel[:, ecols], start=False, stop=False)
                pe.matmul(o, xl[:, cols], weh[:, ecols], start=False, stop=True).then_inc(s["expert_out"], 1)

            for it in range(8):
                pe.wait_ge(s["sink_in"], it + 1)
                pe.matmul(bank(5, cols=64), k("ones"), plan, start=True, stop=True).then_inc(s["sink_sum"], 1)
                expert_rows(2 * it)
                expert_rows(2 * it + 1)
            pe.wait_ge(s["sink_in"], 9)
            for t in range(TT):
                last = pe.transpose(bank(2 + t // 4, E, C, t % 4 * C), plan[:, t * E:(t + 1) * E], ident)
            last.then_inc(s["plan_turned"], 1)
            pe.wait_ge(s["picked"], 1)
            for t in range(TT):
                last = pe.transpose(bank(4, cols=E, first=64 + t * E), picked[:, t * C:(t + 1) * C], ident[0:E, 0:E])
            last.then_inc(s["picked_turned"], 1)
            for t in range(TT):
                pe.wait_ge(s["combined"], t + 1)
                last = pe.transpose(bank(t // 4, cols=C, first=t % 4 * C), sq[:, t * C:(t + 1) * C], ident)
                if t % 4 == 3:
                    last.then_inc(s["combined_turned"], 1)

            norm(2)
            for h in range(2):
                pe.wait_ge(s["normed"], 5 + h)
                pe.matmul(bank(4 + h, KK), p("K_w"), half(xn, h), start=True, stop=True).then_inc(s["keys_done"], 1)
            for t in range(TT):
                last = pe.transpose(bank(6 + t // 4, cols=C, first=t % 4 * C), xn[:, t * C:(t + 1) * C], ident)
                if t % 4 == 3:
                    last.then_inc(s["img_turned"], 1)
            pe.wait_ge(s["img_ready"], 2)
            pe.wait_ge(s["dft_loaded"], 48)
            for q in range(QF):
                if q == 4:
                    pe.wait_ge(s["img_freq_kept"], 1)
                for j in range(2):
                    last = pe.matmul(bank(q % 4), dft_x[:, j, q * C:(q + 1) * C],
                                     img_t.rearrange("p (b j) c -> p j b c", j=2)[:, j], start=(j == 0), stop=(j == 1))
                last.then_inc(s["img_freq"], 1)
            pe.wait_ge(s["key_soft"], 1)
            for t in range(TT):
                last = pe.transpose(bank(4, cols=KK, first=t * KK), keys[:, t * C:(t + 1) * C], ident[0:KK, 0:KK])
            last.then_inc(s["key_turned"], 1)
            pe.wait_ge(s["key_ready"], 1)
            for b in range(B):
                for j in range(2):
                    last = pe.matmul(bank(5, cols=KK, first=b * KK), img_t[:, 2 * b + j, :], key_t[:, 2 * b + j, :],
                                     start=(j == 0), stop=(j == 1))
            last.then_inc(s["filt_done"], 1)
            pe.wait_ge(s["filt_in"], 1)
            pe.matmul(bank(6, cols=B * KK), p("conv0_w"), filt[:, 0].rearrange("p b k -> p (b k)"),
                      start=True, stop=True).then_inc(s["filt0_done"], 1)
            for i in range(2):
                pe.wait_ge(s["stat_in"], i + 1)
                pe.matmul(bank(7, cols=B, first=B * i), k("ones"), st, start=True, stop=True).then_inc(s["stat_sum"], 1)
            pe.wait_ge(s["filt_act"], 1)
            for b in range(B):
                pe.matmul(bank(4, KK, C, b * C), filt[:, 3, b, :], p("conv1_w"), start=True, stop=False)
                last = pe.matmul(bank(4, KK, C, b * C), k("ones", 1)[:, 0:KK], p("conv1_b", 1), start=False, stop=True)
            last.then_inc(s["filt1_done"], 1)
            pe.wait_ge(s["filt1_ready"], 1)
            fring = [5, 6, 7]
            for q in range(QF):
                if q >= 3:
                    pe.wait_ge(s["freq_mult"], q - 2)
                pe.matmul(bank(fring[q % 3]), dft_k[:, q * C:(q + 1) * C], filt_t[:], start=True, stop=True).then_inc(s["filt_freq"], 1)
            pe.wait_ge(s["img_freq_kept"], QF)
            pe.wait_ge(s["freq_mult"], QF)
            for b in range(B):
                for q in range(QF):
                    last = pe.matmul(bank(b // 2, cols=PIX, first=b % 2 * PIX), prod_f[:, q, b * C:(b + 1) * C],
                                     dft_o[:, q, :], start=(q == 0), stop=(q == QF - 1))
                if b % 2:
                    last.then_inc(s["img_back"], 1)

            def mixture(m):
                spec = MOE[m]
                q_n, n = spec["q"], spec["ln"]
                norm(n)
                for h in range(2):
                    pe.wait_ge(s["normed"], 2 * n + h + 1)
                    for t in range(4 * h, 4 * h + 4):
                        last = pe.matmul(bank(4, cols=E, first=t * E), xn[:, t * C:(t + 1) * C], p(spec["router"]),
                                         start=True, stop=True)
                last.then_inc(s["logits_done"], 1)

                def front(e, h, q, peeled=False):
                    if h == 0:
                        pe.wait_ge(s["w1_split"], e + (E * m + 1))
                    for f in range(q_n):
                        if not peeled:
                            wait_count(pe, "hidden", e * (2 * q_n) + (CHUNKS[m] + q_n * (h - 1) + f + 1))
                        mm3(bank(f), wst_h[:, q, f * C:(f + 1) * C], wst_l[:, q, f * C:(f + 1) * C],
                            half(xh, h), half(xl, h)).then_inc(s["hidden_sums"], 1)

                def weights(e, h, peeled=False):
                    if not peeled:
                        wait_count(pe, "score_kept", e * 2 + (UNITS * m + h - 1))
                    pe.matmul(bank(4 + h), sel[:, e, :], half(routes, h), start=True, stop=True).then_inc(s["score_sums"], 1)

                def back(e, h, q):
                    wait_count(pe, "scaled", e * 2 + (UNITS * m + h - 1))
                    if h == 0:
                        pe.wait_ge(s["w2_split"], e + (E * m + 1))
                    for f in range(q_n):
                        pe.wait_ge(s["hidden_lo"], e * (2 * q_n) + (CHUNKS[m] + q_n * h + f + 1))
                        first = (q_n + f) * C
                        last = mm3(bank(6 + h), wst_h[:, q, first:first + C], wst_l[:, q, first:first + C],
                                   hidh[:, h, f, :], hidl[:, h, f, :], start=(f == 0), stop=(f == q_n - 1))
                    last.then_inc(s["part_sums"], 1)

                def expert(e, q):
                    front(e, 1, q)
                    weights(e, 1)
                    back(e, 0, q)
                    front(e + 1, 0, 1 - q)
                    weights(e + 1, 0)
                    back(e, 1, q)

                pe.wait_ge(s["norm_hi"], 4 + 2 * m + 1)
                pe.wait_ge(s["norm_lo"], 4 + 2 * m + 1)
                front(0, 0, 0, peeled=True)
                pe.wait_ge(s["norm_hi"], 4 + 2 * m + 2)
                pe.wait_ge(s["norm_lo"], 4 + 2 * m + 2)
                front(0, 1, 0)
                back(0, 0, 0)
                pe.wait_ge(s["route_parts"], m + 1)
                for t in range(TT):
                    last = pe.transpose(ps[0:PARTS * E, 5, :].bitcast(BF16)[:, t * C:(t + 1) * C], cparts[:, t, :],
                                        sel[:, E, :])
                last.then_inc(s["route_turned"], 1)
                pe.wait_ge(s["route_ready"], m + 1)
                weights(0, 0, peeled=True)
                weights(0, 1, peeled=True)
                front(1, 0, 1)
                weights(1, 0)
                back(0, 1, 0)
                with pe.Fori(0, E // 2 - 1) as i:
                    for q in range(2):
                        expert(i * 2 + (1 + q), 1 - q)
                front(E - 1, 1, 1)
                weights(E - 1, 1)
                back(E - 1, 0, 1)
                back(E - 1, 1, 1)

            pe.wait_ge(s["sel_loaded"], 16)
            mixture(0)

            norm(4)
            for b in range(B):
                pe.wait_ge(s["pooled_in"], 1)
                pe.matmul(bank(b, cols=3 * C), spread[:, b, :], shiftw.rearrange("p k i -> p (k i)"),
                          start=True, stop=True).then_inc(s["offset_done"], 1)
            for b in range(B):
                pe.wait_ge(s["hat_ready"], b + 1)
                for j in range(3):
                    last = pe.matmul(bank(4, cols=1, first=b), hat[:, 3 * b + j, :], wpool[:, 3 * b + j:3 * b + j + 1],
                                     start=(j == 0), stop=(j == 2))
            last.then_inc(s["deform_done"], 1)
            mixture(1)

            norm(6)
            pe.wait_ge(s["alpha_in"], 1)
            for b in range(B):
                last = pe.matmul(bank(b // 2, cols=PIX, first=b % 2 * PIX), spread[:, b, :],
                                 xn[:, b * PIX:(b + 1) * PIX], start=True, stop=True)
                if b % 2:
                    last.then_inc(s["sal_done"], 1)
            mixture(2)

        @block.scalar
        def _(act):
            def norm(n, split=None):
                if n == 0:
                    act.wait_ge(s["consts_loaded"], 16)
                if n in (0, 4, 5, 6):
                    act.preload_act_table_set("natural_log_exp_and_others")
                for h in range(2):
                    act.wait_ge(s["centered"], 2 * n + h + 1)
                    act.activation(half(sq, h), bank(h), ACT.Square).then_inc(s["squared"], 1)
                for h in range(2):
                    act.wait_ge(s["variance"], 2 * n + h + 1)
                    act.activation(half(rstd, h), bank(2 + h), ACT.Ln, bias=k(LN_EPS[n])).then_inc(s["log_var"], 1)
                    act.wait_ge(s["log_var"], 2 * n + h + 1)
                    act.activation(half(rstd, h), half(rstd, h), ACT.Exp, scale=-0.5).then_inc(s["rstd"], 1)
                if split is not None:
                    for h in range(2):
                        act.wait_ge(s["normed"], 2 * n + h + 1)
                        act.activation(half(xh, h), half(xn, h), ACT.Copy).then_inc(s["norm_hi"], 1)

            norm(0)
            for h in range(2):
                act.wait_ge(s["normed"], h + 1)
                act.activation(xph[:, 2 * h:2 * h + 2].rearrange("p b y x -> p (b y x)"),
                               xp[:, 2 * h:2 * h + 2].rearrange("p b y x -> p (b y x)"), ACT.Copy).then_inc(s["norm_hi"], 1)
            for h in range(2):
                act.wait_ge(s["proj_done"], 2 * h + 1)
                act.activation(half(top, h), bank(h, PAB), ACT.Identity, bias=p("b_top", PAB)).then_inc(s["top_ready"], 1)
            def bottom_bias(h):
                act.wait_ge(s["bottom_done"], h + 1)
                act.activation(half(bot, h), bank(4 + h), ACT.Identity, bias=p("b_bottom")).then_inc(s["bottom_biased"], 1)

            bottom_bias(0)
            for b in range(B):
                act.wait_ge(s["neg_max"], 1)
                act.activation(expo[:, b].rearrange("p j n -> p (j n)"), bank(b), ACT.Exp, bias=nmx[:, b:b + 1],
                               accum_out=es[:, b:b + 1]).then_inc(s["exp_done"], 1)
            bottom_bias(1)
            for h in range(2):
                act.wait_ge(s["mix_added"], 2 * h + 2)
                act.activation(xph[:, 2 * h:2 * h + 2].rearrange("p b y x -> p (b y x)"),
                               yp[:, 2 * h:2 * h + 2].rearrange("p b y x -> p (b y x)"), ACT.Copy).then_inc(s["mix_hi"], 1)
            norm(1, split=1)
            for n in range(2 * TT):
                act.wait_ge(s["expert_out"], n + 1)
                t, g = divmod(n, 2)
                act.activation(wb[:, t, g * 512:(g + 1) * 512], bank([0, 1, 6, 7][n % 4]), ACT.Copy).then_inc(s["expert_kept"], 1)
            norm(2)
            for g in range(2):
                act.wait_ge(s["img_turned"], g + 1)
                act.activation(img_t[:, 4 * g:4 * g + 4, :].rearrange("p t c -> p (t c)"), bank(6 + g), ACT.Copy).then_inc(s["img_ready"], 1)
            for b in range(B):
                act.wait_ge(s["key_max"], 1)
                act.activation(keye[:, b * PIX:(b + 1) * PIX], keys[:, b * PIX:(b + 1) * PIX], ACT.Exp, bias=kmx[:, b:b + 1],
                               accum_out=kes[:, b:b + 1]).then_inc(s["key_exp"], 1)
            for q in range(QF):
                act.wait_ge(s["img_freq"], q + 1)
                act.activation(img_f[:, q, :], bank(q % 4), ACT.Copy).then_inc(s["img_freq_kept"], 1)
            act.wait_ge(s["stat_sum"], 2)
            act.activation(st, bank(7, cols=B, first=B), ACT.Ln, bias=k("eps5"), scale=1.0 / (C * KK)).then_inc(s["filt_rstd_ln"], 1)
            act.wait_ge(s["filt_rstd_ln"], 1)
            act.activation(st, st, ACT.Exp, scale=-0.5).then_inc(s["filt_rstd"], 1)

            def mixture(m):
                spec = MOE[m]
                q_n, n = spec["q"], spec["ln"]
                func = {"Silu": ACT.Silu, "Gelu": ACT.Gelu, "Relu": ACT.Relu}[spec["act"]]
                norm(n, split=1)
                act.wait_ge(s["exp_in"], m + 1)
                act.activation(ew, lg2, ACT.Exp).then_inc(s["exp_out"], 1)

                def front(e, h):
                    hidden(e, h)
                    keep_score(e, h)

                def hidden(e, h):
                    if spec["b1"] and h == 0:
                        act.wait_ge(s["hidden"], e * (2 * q_n) + CHUNKS[m])
                        act.activation(bias1[:, 0:q_n], p(spec["b1"]).rearrange("p (e f) -> p e f", f=q_n)[:, e, :],
                                       ACT.Copy).then_inc(s["bias_kept"], 1)
                        act.wait_ge(s["bias_kept"], e + (E * (m - 1) + 1))
                    wait_count(act, "part_sums", e * 2 + (UNITS * m + h - 1))
                    for f in range(q_n):
                        chunk = e * (2 * q_n) + (CHUNKS[m] + q_n * h + f + 1)
                        act.wait_ge(s["hidden_sums"], chunk)
                        bias = 0.0
                        if spec["b1"]:
                            bias = bias1[:, f:f + 1]
                        act.activation(hid[:, h, f, :], bank(f), func, bias=bias).then_inc(s["hidden"], 1)
                        if f % 2 == 0:
                            act.wait_ge(s["hidden"], chunk)
                            act.activation(hidh[:, h, f, :], hid[:, h, f, :], ACT.Copy).then_inc(s["hidden_hi_act"], 1)

                def keep_score(e, h):
                    act.wait_ge(s["score_sums"], e * 2 + (UNITS * m + h + 1))
                    wait_count(act, "scaled", e * 2 + (UNITS * m + h - 1))
                    act.activation(half(score, h), bank(4 + h), ACT.Copy).then_inc(s["score_kept"], 1)

                hidden(0, 0)
                hidden(0, 1)
                keep_score(0, 0)
                keep_score(0, 1)
                with act.Fori(0, E - 1) as i:
                    for h in range(2):
                        front(i + 1, h)

            mixture(0)
            norm(4)
            for b in range(B):
                act.wait_ge(s["pos_ready"], b + 1)
                seg = pos[:, 3 * b:3 * b + 3, :].rearrange("p a c -> p (a c)")
                act.activation(seg, seg, ACT.Abs, bias=k("minus_i")).then_inc(s["dist_done"], 1)
                act.wait_ge(s["dist_done"], b + 1)
                act.activation(hat[:, 3 * b:3 * b + 3, :].rearrange("p a c -> p (a c)"), seg, ACT.Relu,
                               bias=1.0, scale=-1.0).then_inc(s["hat_ready"], 1)
            act.wait_ge(s["deform_done"], 1)
            act.activation(gate4, bank(4, cols=B), ACT.Sigmoid, bias=p("b_deform")).then_inc(s["deform_gate"], 1)
            mixture(1)
            norm(6)
            for h in range(2):
                act.wait_ge(s["sal_ready"], h + 1)
                act.activation(half(fm, h), half(fm, h), ACT.Sigmoid, scale=p("scale")).then_inc(s["sal_sig"], 1)
            mixture(2)

        @block.vector
        def _(dve):
            steps = [0]

            def step(ins):
                steps[0] += 1
                ins.then_inc(s["dve_step"], 1)
                dve.wait_ge(s["dve_step"], steps[0])

            def norm(n, split=None):
                for h in range(2):
                    dve.wait_ge(s["rstd"], 2 * n + h + 1)
                    if n == 0:
                        dve.wait_ge(s["borders_zero"], 1)
                        dve.tensor_tensor(xp[:, 2 * h:2 * h + 2, 1:1 + SIDE, 1:1 + SIDE],
                                          bank(h).rearrange("p (b y x) -> p b y x", b=2, y=SIDE),
                                          half(rstd, h).rearrange("p (b y x) -> p b y x", b=2, y=SIDE),
                                          ALU.mult).then_inc(s["normed"], 1)
                    else:
                        dve.tensor_tensor(half(xn, h), bank(h), half(rstd, h), ALU.mult).then_inc(s["normed"], 1)
                if split is not None:
                    for h in range(2):
                        dve.wait_ge(s["norm_hi"], split + h + 1)
                        dve.wait_ge(s["normed"], 2 * n + h + 1)
                        dve.tensor_tensor(half(xl, h), half(xn, h), f32(half(xh, h)), ALU.subtract).then_inc(s["norm_lo"], 1)

            dve.wait_ge(s["consts_loaded"], 16)
            dve.wait_ge(s["params_loaded"], 16)
            shifts = k("shift").rearrange("p (d i) -> p d i", d=3)
            woff = p("w_offset")
            for j in range(3):
                step(dve.tensor_scalar(shiftw[:, j, :], shifts[:, 0, :], woff[:, 3 * j:3 * j + 1], None, ALU.mult))
                for d in range(1, 3):
                    step(dve.scalar_tensor_tensor(shiftw[:, j, :], shifts[:, d, :], woff[:, 3 * j + d:3 * j + d + 1],
                                                  shiftw[:, j, :], ALU.mult, ALU.add))
            step(dve.tensor_scalar(neg_wf, p("wf"), -1.0, None, ALU.mult))

            norm(0)
            for h in range(2):
                dve.wait_ge(s["norm_hi"], h + 1)
                dve.wait_ge(s["normed"], h + 1)
                seg = [t[:, 2 * h:2 * h + 2].rearrange("p b y x -> p (b y x)") for t in (xpl, xp, xph)]
                dve.tensor_tensor(seg[0], seg[1], f32(seg[2]), ALU.subtract).then_inc(s["norm_lo"], 1)
            for h in range(2):
                dve.wait_ge(s["proj_done"], 2 * h + 2)
                dve.tensor_scalar(half(cen, h), bank(2 + h, PAB), p("b_center", PAB), None, ALU.add).then_inc(s["center_ready"], 1)
            for b in range(B):
                dve.wait_ge(s["scores_done"], b + 1)
                dve.tensor_reduce(mx[:, b:b + 1], bank(b), AX.X, ALU.max).then_inc(s["score_max"], 1)
            dve.wait_ge(s["max_turned"], 1)
            step(dve.tensor_reduce(mx4, bank(6, B, C), AX.X, ALU.max))
            dve.tensor_scalar(mxd, ident[0:B, 0:B], mx4, -1.0, ALU.mult, ALU.mult).then_inc(s["max_diag"], 1)
            dve.wait_ge(s["max_spread"], 1)
            dve.tensor_copy(nmx, bank(6, cols=B, first=256)).then_inc(s["neg_max"], 1)
            for g in range(2):
                dve.wait_ge(s["bottom_turned"], g + 1)
                dve.tensor_copy(bot_t[:, 4 * g:4 * g + 4, :].rearrange("p t c -> p (t c)"), bank(6 + g)).then_inc(s["bottom_ready"], 1)
            dve.wait_ge(s["exp_summed"], 1)
            dve.reciprocal(rs, bank(4, cols=B)).then_inc(s["exp_recip"], 1)
            dve.wait_ge(s["exp_recip"], 1)
            dve.wait_ge(s["borders_zero"], 2)
            for b in range(B):
                dve.wait_ge(s["mixed"], b // 2 * 2 + 2)
                dve.scalar_tensor_tensor(inside(yp, b), bank(6 + b // 2, cols=PIX, first=b % 2 * PIX).rearrange("p (y x) -> p y x", y=SIDE),
                                         rs[:, b:b + 1], inside(xp, b), ALU.mult, ALU.add).then_inc(s["mix_added"], 1)
            for h in range(2):
                dve.wait_ge(s["mix_hi"], h + 1)
                dve.wait_ge(s["mix_added"], 2 * h + 2)
                seg = [t[:, 2 * h:2 * h + 2].rearrange("p b y x -> p (b y x)") for t in (xpl, yp, xph)]
                dve.tensor_tensor(seg[0], seg[1], f32(seg[2]), ALU.subtract).then_inc(s["mix_lo"], 1)
            for h in range(2):
                dve.wait_ge(s["out_conv_done"], h + 1)
                dve.scalar_tensor_tensor(half(x, h), bank(4 + h), p("b_out"), half(x, h), ALU.add, ALU.add).then_inc(s["x1_ready"], 1)

            norm(1, split=2)
            dve.wait_ge(s["gates_done"], 1)
            dve.tensor_scalar(plan, bank(4, cols=64), 1e-10, None, ALU.max).then_inc(s["sink_in"], 1)
            plan3 = tiles(plan)
            for it in range(8):
                dve.wait_ge(s["sink_sum"], it + 1)
                dve.wait_ge(s["sink_in"], it + 1)
                step(dve.tensor_reduce(r8, bank(5, cols=64).rearrange("p (t e) -> p e t", e=E), AX.X, ALU.add))
                step(dve.reciprocal(r8b, r8))
                step(dve.tensor_tensor(plan3, plan3, again(r8b, TT), ALU.mult))
                step(dve.tensor_reduce(r8, plan3, AX.X, ALU.add))
                step(dve.reciprocal(r8b, r8))
                dve.tensor_tensor(plan3, plan3, over(r8b, E), ALU.mult).then_inc(s["sink_in"], 1)
            dve.wait_ge(s["plan_turned"], 1)
            src = ps[0:E, 2:4, :].rearrange("p g n -> p (g n)")
            for r in range(TOPK0 // 8):
                step(dve.max(top8, src))
                last = dve.match_replace(picked, top8, src, -1.0)
                if r < TOPK0 // 8 - 1:
                    step(last)
                src = picked
            last.then_inc(s["picked"], 1)
            dve.wait_ge(s["picked_turned"], 1)
            step(dve.tensor_scalar(pick_w, bank(4, cols=64, first=64), 0.0, None, ALU.is_lt))
            step(dve.tensor_reduce(cnt, tiles(pick_w), AX.X, ALU.add))
            step(dve.tensor_scalar(cnt, cnt, 1.0, None, ALU.add))
            step(dve.reciprocal(r8, cnt))
            dve.wait_ge(s["sink_in"], 9)
            step(dve.scalar_tensor_tensor(pick_w, plan, 0.5, pick_w, ALU.is_gt, ALU.mult))
            step(dve.tensor_tensor(tiles(pick_w), tiles(pick_w), over(r8, E), ALU.mult))
            dve.wait_ge(s["expert_kept"], 2 * TT)
            sqt = sq.rearrange("p (t c) -> p t c", c=C)
            for e in range(E):
                for t in range(TT):
                    w = pick_w[:, t * E + e:t * E + e + 1]
                    y = wb[:, t, e * C:(e + 1) * C]
                    if e == 0:
                        last = dve.tensor_scalar(sqt[:, t, :], y, w, None, ALU.mult)
                    else:
                        last = dve.scalar_tensor_tensor(sqt[:, t, :], y, w, sqt[:, t, :], ALU.mult, ALU.add)
                    if e == E - 1:
                        last.then_inc(s["combined"], 1)
                    else:
                        last.then_inc(s["dve_step"], 1)
                        steps[0] += 1
                        if t == TT - 1:
                            dve.wait_ge(s["dve_step"], steps[0])
            for h in range(2):
                dve.wait_ge(s["combined_turned"], h + 1)
                dve.tensor_tensor(half(x, h), bank(h), half(x, h), ALU.add).then_inc(s["x2_ready"], 1)

            norm(2)
            for h in range(2):
                dve.wait_ge(s["keys_done"], h + 1)
                step(dve.tensor_scalar(half(keys, h), bank(4 + h, KK), p("K_b", KK), None, ALU.add))
            step(dve.tensor_reduce(kmx, keys.rearrange("p (b n) -> p b n", b=B), AX.X, ALU.max))
            dve.tensor_scalar(kmx, kmx, -1.0, None, ALU.mult).then_inc(s["key_max"], 1)
            dve.wait_ge(s["key_exp"], B)
            step(dve.reciprocal(krs, kes))
            for b in range(B):
                last = dve.tensor_scalar(keys[:, b * PIX:(b + 1) * PIX], keye[:, b * PIX:(b + 1) * PIX], krs[:, b:b + 1], None, ALU.mult)
            last.then_inc(s["key_soft"], 1)
            dve.wait_ge(s["key_turned"], 1)
            dve.tensor_copy(key_t.rearrange("p t k -> p (t k)"), bank(4, cols=TT * KK)).then_inc(s["key_ready"], 1)
            dve.wait_ge(s["filt_done"], 1)
            f0, f1, f2, f3 = [filt[:, j] for j in range(4)]

            def flat(t):
                return t.rearrange("p b k -> p (b k)")

            dve.tensor_copy(flat(f0), bank(5, cols=B * KK)).then_inc(s["filt_in"], 1)
            dve.wait_ge(s["filt0_done"], 1)
            step(dve.tensor_scalar(flat(f1), bank(6, cols=B * KK), p("conv0_b"), None, ALU.add))
            dve.tensor_reduce(st, f1, AX.X, ALU.add).then_inc(s["stat_in"], 1)
            dve.wait_ge(s["stat_sum"], 1)
            step(dve.tensor_scalar(mean4, bank(7, cols=B), 1.0 / (C * KK), None, ALU.mult))
            step(dve.tensor_tensor(f1, f1, over(mean4, KK), ALU.subtract))
            step(dve.tensor_tensor(f2, f1, f1, ALU.mult))
            dve.tensor_reduce(st, f2, AX.X, ALU.add).then_inc(s["stat_in"], 1)
            dve.wait_ge(s["filt_rstd"], 1)
            step(dve.tensor_tensor(f1, f1, over(st, KK), ALU.mult))
            step(dve.tensor_tensor(f1, f1, again(p("ln_w"), B), ALU.mult))
            step(dve.tensor_tensor(f1, f1, again(p("ln_b"), B), ALU.add))
            dve.tensor_scalar(flat(f3), flat(f1), 0.0, None, ALU.max).then_inc(s["filt_act"], 1)
            dve.wait_ge(s["filt1_done"], 1)
            dve.tensor_copy(filt_t[:], bank(4, KK)).then_inc(s["filt1_ready"], 1)
            for q in range(QF):
                dve.wait_ge(s["filt_freq"], q + 1)
                dve.wait_ge(s["img_freq_kept"], q + 1)
                dve.tensor_tensor(prod_f[:, q, :], bank([5, 6, 7][q % 3]), img_f[:, q, :], ALU.mult).then_inc(s["freq_mult"], 1)
            for h in range(2):
                dve.wait_ge(s["img_back"], h + 1)
                dve.tensor_tensor(half(x, h), bank(h), half(x, h), ALU.add).then_inc(s["x3_ready"], 1)

            def mixture(m):
                spec = MOE[m]
                q_n, n = spec["q"], spec["ln"]
                def front(e, h):
                    for f in range(q_n):
                        pair = e * q_n + (CHUNKS[m] // 2 + (q_n * h + f) // 2 + 1)
                        if f % 2 == 1:
                            dve.wait_ge(s["hidden"], e * (2 * q_n) + (CHUNKS[m] + q_n * h + f + 1))
                            dve.tensor_copy(hidh[:, h, f, :], hid[:, h, f, :]).then_inc(s["hidden_hi_dve"], 1)
                            dve.wait_ge(s["hidden_hi_dve"], pair)
                        else:
                            dve.wait_ge(s["hidden_hi_act"], pair)
                        dve.tensor_tensor(hidl[:, h, f, :], hid[:, h, f, :], f32(hidh[:, h, f, :]),
                                          ALU.subtract).then_inc(s["hidden_lo"], 1)

                norm(n, split=4 + 2 * m)
                dve.wait_ge(s["logits_done"], m + 1)
                if spec["layer"] == 3:
                    step(dve.tensor_tensor(tiles(lg), tiles(bank(4, cols=64)), again(p("bg3"), TT), ALU.add))
                else:
                    step(dve.tensor_copy(lg, bank(4, cols=64)))
                step(dve.tensor_reduce(m8, tiles(lg), AX.X, ALU.max))
                dve.tensor_tensor(tiles(lg2), tiles(lg), over(m8, E), ALU.subtract).then_inc(s["exp_in"], 1)
                front(0, 0)
                dve.wait_ge(s["exp_out"], m + 1)
                if spec["layer"] == 2:
                    step(dve.tensor_reduce(r8, tiles(ew), AX.X, ALU.add))
                    step(dve.reciprocal(r8b, r8))
                    step(dve.tensor_tensor(tiles(lg), tiles(ew), over(r8b, E), ALU.mult))
                    step(dve.tensor_copy(ew, lg))
                    step(dve.tensor_reduce(m8, tiles(lg), AX.X, ALU.max))
                rev = again(k("rev"), TT)
                for pick in (oh1, oh2):
                    step(dve.tensor_tensor(tiles(pick), tiles(lg), over(m8, E), ALU.is_equal))
                    step(dve.tensor_tensor(tiles(pick), tiles(pick), rev, ALU.mult))
                    step(dve.tensor_reduce(r8, tiles(pick), AX.X, ALU.max))
                    step(dve.tensor_tensor(tiles(pick), tiles(pick), over(r8, E), ALU.is_equal))
                    if pick is oh1:
                        step(dve.scalar_tensor_tensor(lg, oh1, -BIG, lg, ALU.mult, ALU.add))
                        step(dve.tensor_reduce(m8, tiles(lg), AX.X, ALU.max))
                step(dve.tensor_tensor(oh1, oh1, oh2, ALU.add))
                step(dve.tensor_tensor(wgt, ew, oh1, ALU.mult))
                step(dve.tensor_reduce(r8, tiles(wgt), AX.X, ALU.add))
                if spec["layer"] == 2:
                    step(dve.tensor_scalar(r8, r8, 1e-6, None, ALU.add))
                step(dve.reciprocal(r8b, r8))
                step(dve.tensor_tensor(tiles(wgt), tiles(wgt), over(r8b, E), ALU.mult))
                step(dve.tensor_copy(cparts[:, :, 0:E], tiles(wgt)))
                step(dve.tensor_tensor(tiles(rem), tiles(wgt), cparts[:, :, 0:E], ALU.subtract))
                step(dve.tensor_copy(cparts[:, :, E:2 * E], tiles(rem)))
                step(dve.tensor_tensor(tiles(rem), tiles(rem), cparts[:, :, E:2 * E], ALU.subtract))
                dve.tensor_copy(cparts[:, :, 2 * E:3 * E], tiles(rem)).then_inc(s["route_parts"], 1)
                dve.wait_ge(s["route_turned"], m + 1)
                dve.wait_ge(s["routes_zero"], 1)
                dve.tensor_copy(routes[0:PARTS * E, :], ps[0:PARTS * E, 5, :].bitcast(BF16)).then_inc(s["route_ready"], 1)

                def back(e, h):
                    unit = e * 2 + (UNITS * m + h + 1)
                    dve.wait_ge(s["part_sums"], unit)
                    dve.wait_ge(s["score_kept"], unit)
                    wait_count(dve, "state_added", e * 2 + (UNITS * m + h - 1))
                    if spec["b2"]:
                        dve.scalar_tensor_tensor(half(parts, h), bank(6 + h), p(spec["b2"])[:, bass.ds(e, 1)], half(score, h),
                                                 ALU.add, ALU.mult).then_inc(s["scaled"], 1)
                    else:
                        dve.tensor_tensor(half(parts, h), bank(6 + h), half(score, h), ALU.mult).then_inc(s["scaled"], 1)

                def expert(e):
                    front(e, 1)
                    back(e, 0)
                    front(e + 1, 0)
                    back(e, 1)

                expert(0)
                with dve.Fori(0, E - 2) as i:
                    expert(i + 1)
                front(E - 1, 1)
                back(E - 1, 0)
                back(E - 1, 1)

            mixture(0)

            norm(4)
            dve.wait_ge(s["normed"], 10)
            step(dve.tensor_reduce(pool4, xn.rearrange("p (b n) -> p b n", b=B), AX.X, ALU.add))
            step(dve.tensor_scalar(pool4, pool4, 1.0 / PIX, None, ALU.mult))
            step(dve.tensor_tensor(wpool.rearrange("p (b k) -> p b k", b=B), over(pool4, 3), again(p("w_deform"), B), ALU.mult))
            dve.tensor_copy(spread, over(pool4, C)).then_inc(s["pooled_in"], 1)
            for b in range(B):
                dve.wait_ge(s["offset_done"], b + 1)
                seg = pos[:, 3 * b:3 * b + 3, :].rearrange("p a c -> p (a c)")
                step(dve.tensor_tensor(seg, bank(b, cols=3 * C), k("base"), ALU.add))
                dve.tensor_scalar(seg, seg, 0.0, C - 1.0, ALU.max, ALU.min).then_inc(s["pos_ready"], 1)
            dve.wait_ge(s["deform_gate"], 1)
            for b in range(B):
                cols = slice(b * PIX, (b + 1) * PIX)
                last = dve.scalar_tensor_tensor(x[:, cols], xn[:, cols], gate4[:, b:b + 1], x[:, cols], ALU.mult, ALU.add)
                if b % 2:
                    last.then_inc(s["x5_ready"], 1)
            mixture(1)

            norm(6)
            dve.wait_ge(s["normed"], 14)
            step(dve.tensor_reduce(pool4, xn.rearrange("p (b n) -> p b n", b=B), AX.X, ALU.add))
            step(dve.tensor_scalar(pool4, pool4, 1.0 / SALIENCY_AREA, 1.0 / C, ALU.mult, ALU.mult))
            dve.tensor_copy(spread, over(pool4, C)).then_inc(s["alpha_in"], 1)
            for h in range(2):
                dve.wait_ge(s["sal_done"], h + 1)
                step(dve.tensor_scalar(half(fm, h), bank(h), p("conv_w"), 0.0, ALU.mult, ALU.max))
                dve.scalar_tensor_tensor(half(fm, h), half(fm, h), TH, half(fm, h), ALU.is_gt, ALU.mult).then_inc(s["sal_ready"], 1)
            for h in range(2):
                dve.wait_ge(s["sal_sig"], h + 1)
                step(dve.tensor_scalar(half(fm, h), half(fm, h), neg_wf, 1.0, ALU.mult, ALU.add))
                dve.tensor_tensor(half(x, h), half(x, h), half(fm, h), ALU.add).then_inc(s["x7_ready"], 1)
            mixture(2)


def constants():
    cols = {
        "center": np.eye(C) - 1.0 / C, "mean": np.full((C, C), 1.0 / C), "ident": np.eye(C), "ones": np.ones((C, C)),
        "shift": np.concatenate([np.eye(C, k=1 - d) for d in range(3)], 1),
        "base": np.broadcast_to((np.arange(C)[None, :] + np.arange(3)[:, None] - 1).reshape(-1), (C, 3 * C)),
        "rev": np.broadcast_to(np.arange(E, 0, -1), (C, E)), "minus_i": -np.arange(C)[:, None],
        "eps6": np.full((C, 1), 1e-6), "eps5": np.full((C, 1), 1e-5), "one": np.ones((C, 1)),
    }
    packed = np.concatenate([cols[n] for n in CONST], 1).astype(np.float32)
    sel = np.zeros((C, E + 1, C), np.float32)
    for e in range(E):
        sel[e:PARTS * E:E, e, :] = 1.0
    sel[:, E, :] = np.eye(C)

    freqs = [(u, v) for u in range(GRID) for v in range(GRID)
             if (u, v) != (0, 0) and (u, v) < ((-u) % GRID, (-v) % GRID)]
    assert len(freqs) == FREQ
    fu, fv = (np.array([f[i] for f in freqs], np.float64) for i in range(2))
    y, xx = np.divmod(np.arange(PIX), SIDE)
    i, j = np.divmod(np.arange(KK), KW)
    angle = 2 * np.pi / GRID
    ta = angle * (np.outer(y, fu) + np.outer(xx, fv))
    tk = angle * (np.outer(i - KW // 2, fu) + np.outer(j - KW // 2, fv))
    ar, ai, br, bi = np.cos(ta), -np.sin(ta), np.cos(tk), np.sin(tk)
    pad = QF * C - 1 - 3 * FREQ

    def rows(first, a, b, c):
        n = first.shape[0]
        return np.concatenate([first, a, b, c, np.zeros((n, pad))], 1)

    to_x = rows(np.ones((PIX, 1)), ar + ai, ar, ai)
    to_k = rows(np.ones((KK, 1)), br, bi - br, br + bi)
    re, im = 2 * ar, 2 * ai
    back = rows(np.ones((PIX, 1)), re + im, im, -re).T / GRID ** 2
    f32 = np.float32
    return {
        "consts": packed,
        "sel": sel,
        "dft_x": np.ascontiguousarray(to_x.reshape(2, C, QF * C).transpose(1, 0, 2)).astype(f32),
        "dft_k": np.ascontiguousarray(to_k).astype(f32),
        "dft_o": np.ascontiguousarray(back.reshape(QF, C, PIX).transpose(1, 0, 2)).astype(f32),
    }


def laid_out(a):
    def col(v, rows=C):
        m = np.zeros((C, v.shape[-1] if v.ndim > 1 else 1), np.float32)
        m[:v.shape[0]] = v.reshape(v.shape[0], -1)
        return m

    def every(v):
        v = np.asarray(v).reshape(1, -1)
        return np.broadcast_to(v, (C, v.shape[1]))

    par = {
        "b_bottom": col(a["L0_conv_b_bottom"]), "b_out": col(a["L0_conv_b_out"]),
        "b_top": col(a["L0_conv_b_top"]), "b_center": col(a["L0_conv_b_center"]),
        "w_top": a["L0_conv_w_top"][:, :, 0, 0].T, "w_center": a["L0_conv_w_center"][:, :, 0, 0].T,
        "gate_w": a["L0_ffn_gate_w"][0], "K_w": a["L1_conv_K_w"].T, "K_b": col(a["L1_conv_K_b"]),
        "conv0_w": a["L1_conv_conv0_w"].T, "conv0_b": col(a["L1_conv_conv0_b"]),
        "ln_w": a["L1_conv_ln_w"].reshape(C, KK), "ln_b": a["L1_conv_ln_b"].reshape(C, KK),
        "conv1_w": a["L1_conv_conv1_w"].T, "conv1_b": every(a["L1_conv_conv1_b"]), "Wg1": a["L1_ffn_Wg"],
        "w_offset": every(a["L2_conv_w_offset"]), "w_deform": every(a["L2_conv_w_deform"]),
        "b_deform": every(a["L2_conv_b_deform"]), "Wg2": a["L2_ffn_Wg"],
        "L2_b1": a["L2_ffn_b1"].reshape(E * 4, C).T, "L2_b2": a["L2_ffn_b2"].T,
        "conv_w": col(a["L3_conv_conv_w"].reshape(C, 1)), "scale": every(a["L3_conv_scale"]), "wf": every(a["L3_conv_wf"]),
        "wg3": a["L3_ffn_wg"], "bg3": every(a["L3_ffn_bg"]),
        "L3_b1": a["L3_ffn_b1"].reshape(E * 2, C).T, "L3_b2": a["L3_ffn_b2"].T,
    }

    def experts(w1, w2, q):
        return np.concatenate([w1.transpose(1, 0, 2), w2.reshape(E, q, C, C).transpose(2, 0, 1, 3).reshape(C, E, q * C)], 2)

    return {
        "x": a["x"].reshape(B, C, PIX),
        "params": np.concatenate([par[n] for n in PARAM], 1),
        "w_bottom": a["L0_conv_w_bottom"].transpose(1, 2, 3, 0).reshape(C, 9 * C),
        "w_out": a["L0_conv_w_out"].transpose(1, 2, 3, 0).reshape(C, 9 * C),
        "w_experts": a["L0_ffn_experts"].transpose(1, 0, 2).reshape(C, E * C),
        "moe1": experts(a["L1_ffn_W1"], a["L1_ffn_W2"], 4),
        "moe2": experts(a["L2_ffn_W1"], a["L2_ffn_W2"], 4),
        "moe3": experts(a["L3_ffn_w1"], a["L3_ffn_w2"], 2),
    }


def kernel(**inputs):
    import ml_dtypes
    import concourse.bacc as bacc
    from concourse.bass_utils import run_bass_kernel_spmd as run

    nc = bacc.Bacc("TRN2", target_bir_lowering=False, num_devices=1)
    arrays, dram = {}, {}
    given = {**laid_out({n: np.asarray(v) for n, v in inputs.items()}), **constants()}
    given["sel"] = given["sel"].astype(ml_dtypes.bfloat16)
    for name, v in given.items():
        v = np.ascontiguousarray(v)
        arrays[f"in_{name}"] = v
        dram[name] = nc.dram_tensor(f"in_{name}", v.shape, mybir.dt.from_np(v.dtype), kind="ExternalInput").ap()
    out = nc.dram_tensor("out_0", (B, C, PIX), F32, kind="ExternalOutput").ap()
    metaformer(nc, dram, out)
    r = run(nc, [arrays], core_ids=[0])
    return r.results[0]["out_0"].reshape(B, C, SIDE, SIDE)
```

```python
from contextlib import ExitStack

import numpy as np

import concourse.bass as bass
from concourse import mybir

F32 = mybir.dt.float32
F32R = mybir.dt.float32r
BF16 = mybir.dt.bfloat16
ALU = mybir.AluOpType
ACT = mybir.ActivationFunctionType
AX = mybir.AxisListType

C = 128
B = 4
SIDE = 16
PIX = SIDE * SIDE
N = B * PIX
HALF = N // 2
TT = N // C
PAD = SIDE + 2
PAB = 16
E = 8
TOPK0 = N // B // E
KW = 7
KK = KW * KW
PARTS = 3
POOL_T = 5
TH = 0.01
SALIENCY_AREA = 56 * 56
BIG = 3.0e38

GRID = SIDE + KW // 2
FREQ = (GRID * GRID - 1) // 2
QF = -(-(1 + 3 * FREQ) // C)

PARAM = {}
for _name, _cols in [
    ("b_bottom", 1), ("b_out", 1), ("b_top", 1), ("b_center", 1), ("w_top", PAB), ("w_center", PAB),
    ("gate_w", E), ("K_w", KK), ("K_b", 1), ("conv0_w", C), ("conv0_b", 1), ("ln_w", KK), ("ln_b", KK),
    ("conv1_w", C), ("conv1_b", C), ("Wg1", E), ("w_offset", 9), ("w_deform", 3), ("b_deform", 1),
    ("Wg2", E), ("L2_b1", E * 4), ("L2_b2", E), ("conv_w", C), ("scale", 1), ("wf", 1),
    ("wg3", E), ("bg3", E), ("L3_b1", E * 2), ("L3_b2", E),
]:
    PARAM[_name] = (sum(c for _, c in PARAM.values()), _cols)
PARAM_COLS = sum(c for _, c in PARAM.values())

CONST = {}
for _name, _cols in [("center", C), ("mean", C), ("eps6", 1), ("eps5", 1), ("ident", C), ("ones", C),
                     ("minus_i", 1), ("shift", 3 * C), ("base", 3 * C)]:
    CONST[_name] = (sum(c for _, c in CONST.values()), _cols)
NORM_CONSTS = CONST["ident"][0]
CONST_COLS = sum(c for _, c in CONST.values())

UNITS = 2 * E
MOE = [
    dict(layer=1, ln=3, q=4, act="Silu", router="Wg1", b1=None, b2=None),
    dict(layer=2, ln=5, q=4, act="Gelu", router="Wg2", b1="L2_b1", b2="L2_b2"),
    dict(layer=3, ln=7, q=2, act="Relu", router="wg3", b1="L3_b1", b2="L3_b2"),
]
START_CLOCK = 7
STAGGERED = (1,)
LN_EPS = ["eps6", "eps5"] * 4

SIGNALS = [
    "x0_loaded", "x1_loaded", "params_loaded", "norm_consts_loaded", "consts_loaded", "wb_loaded", "wo_loaded", "we_loaded", "dft_loaded", "sel_loaded",
    "moe1_loaded", "moe2_loaded", "moe3_loaded", "stored",
    "borders_zero", "routes_zero", "wb_split", "wo_split", "we_split", "pool_step",
    "centered", "squared", "variance", "log_var", "rstd", "normed", "norm_hi", "norm_lo",
    "dve_step",
    "proj_done", "top_ready", "center_ready", "scores_done", "score_max", "max_turned", "max_diag", "max_spread",
    "neg_max", "exp_done", "exp_summed", "exp_recip",
    "bottom_done", "bottom_biased", "bottom_turned", "bottom_ready", "mixed", "mix_added", "mix_hi", "mix_lo",
    "out_conv_done", "x1_ready",
    "gates_done", "expert_out", "expert_kept", "sink_in", "sink_sum", "plan_turned", "plan_ready",
    "gate_ready", "gated", "gated_sum", "pool_gated", "pool_sum",
    "picked", "picked_turned", "combined", "combined_turned", "x2_ready",
    "keys_done", "key_max", "key_exp", "key_diag", "key_turned", "key_ready", "img_turned", "img_ready_act", "img_ready_dve",
    "filt_done", "filt_in", "filt0_done", "stat_in", "stat_sum", "filt_rstd_ln", "filt_rstd", "filt_act", "filt1_done", "filt1_ready",
    "img_freq", "img_freq_kept", "filt_freq", "freq_mult", "img_back", "x3_ready",
    "pooled_in", "offset_done", "pos_ready", "dist_done", "hat_ready", "deform_done", "deform_exp", "x5_ready",
    "alpha_in", "one_added", "sal_done", "sal_rectified", "sal_ready", "sal_sig", "x7_ready",
    "logits_done", "exp_in", "exp_out", "route_parts", "route_turned", "route_ready",
    "w1_split", "w2_split", "hidden_sums", "score_sums", "bias_kept", "hidden", "hidden_hi_act", "hidden_hi_dve", "hidden_lo", "score_kept", "part_sums", "scaled",
    "state_added",
]


def metaformer(nc, dram, out):
    ctx = ExitStack()
    with ctx:
        def sb(name, shape, dt=F32, scope=ctx):
            return scope.enter_context(nc.sbuf_tensor(name, shape, dt))

        s = {name: ctx.enter_context(nc.semaphore(name)) for name in SIGNALS}

        x = sb("x", [C, N])
        xn = sb("xn", [C, N])
        xh = sb("xh", [C, N], F32R)
        xl = sb("xl", [C, N], F32R)
        sq = sb("sq", [C, N])
        rstd = sb("rstd", [C, N])
        par = sb("par", [C, PARAM_COLS])
        cst = sb("cst", [C, CONST_COLS])
        sel = sb("sel", [C, E + 1, C], BF16)
        routes = sb("routes", [C, N], BF16)
        wa = sb("wa", [C, E, 1024])
        wb = sb("wb", [C, E, 1024])
        dft_x = sb("dft_x", [C, 2, QF * C])
        dft_k = sb("dft_k", [KK, QF * C])
        dft_o = sb("dft_o", [C, QF, PIX])
        shiftw = sb("shiftw", [C, 3, C])
        small = sb("small", [C, 1024])
        cparts = sb("cparts", [C, TT, PARTS * E], BF16)
        ps = ctx.enter_context(nc.psum_tensor("ps", [C, 8, 512], F32))

        with ExitStack() as scope:
            xp = sb("xp", [C, B, PAD, PAD], scope=scope)
            xph = sb("xph", [C, B, PAD, PAD], F32R, scope)
            xpl = sb("xpl", [C, B, PAD, PAD], F32R, scope)
            yp = sb("yp", [C, B, PAD, PAD], scope=scope)
            w33 = sb("w33", [C, 2, 9 * C], scope=scope)
            w33h = sb("w33h", [C, 2, 9 * C], F32R, scope)
            w33l = sb("w33l", [C, 2, 9 * C], F32R, scope)
            expo = sb("expo", [C, B, 2, PIX], scope=scope)
            bot = sb("bot", [C, N], scope=scope)
            bot_t = sb("bot_t", [C, TT, C], scope=scope)
            top = sb("top", [PAB, N], scope=scope)
            cen = sb("cen", [PAB, N], scope=scope)
            we = sb("we", [C, E * C], scope=scope)
            weh = sb("weh", [C, E * C], F32R, scope)
            wel = sb("wel", [C, E * C], F32R, scope)
        picked = bot[0:E, :]
        with ExitStack() as scope:
            img_t = sb("img_t", [C, TT, C], scope=scope)
            key_d = sb("key_d", [KK, B, KK], scope=scope)
            keye = sb("keye", [KK, N], scope=scope)
            key_t = sb("key_t", [C, TT, KK], scope=scope)
            filt = sb("filt", [C, 4, B, KK], scope=scope)
            filt_t = sb("filt_t", [KK, B * C], scope=scope)
            img_f = sb("img_f", [C, QF, B * C], scope=scope)
            prod_f = sb("prod_f", [C, QF, B * C], scope=scope)
        pos = img_f[:, 0:3, :].rearrange("p a (b c) -> p (a b) c", b=4)
        hat = prod_f[:, 0:3, :].rearrange("p a (b c) -> p (a b) c", b=4)
        spread = img_t[:, 0:4, :]
        fm = sq
        with ExitStack() as scope:
            hid = sb("hid", [C, 2, 4, 512], scope=scope)
            hidh = sb("hidh", [C, 2, 4, 512], F32R, scope)
            hidl = sb("hidl", [C, 2, 4, 512], F32R, scope)
            wst_h = sb("wst_h", [C, 2, 1024], F32R, scope)
            wst_l = sb("wst_l", [C, 2, 1024], F32R, scope)
        score = sq
        parts = rstd

        at = [0]

        def piece(cols, rows=C):
            at[0] += cols
            assert at[0] <= 1024
            return small[0:rows, at[0] - cols:at[0]]

        mx, mx4, mxd, nmx, es, rs = piece(4), piece(1, B), piece(4, B), piece(4), piece(4), piece(4)
        plan, r8, r8b, top8 = piece(64), piece(8), piece(8), piece(8, E)
        pick_w, cnt = piece(64), piece(8)
        kmx, kbias, kes, krs = [piece(4, KK) for _ in range(4)]
        st = piece(4)
        pool4, wpool, gate4 = piece(4), piece(12), piece(4)
        lg, lg2, ew, oh1, oh2, wgt, rem, tops, pair, m8 = [piece(64) for _ in range(9)] + [piece(8)]
        neg_wf, neg_b, bias1 = piece(1), piece(1), piece(4)
        gate, share = oh1, oh2

        def p(name, rows=C):
            at0, cols = PARAM[name]
            return par[0:rows, at0:at0 + cols]

        def k(name, rows=C):
            at0, cols = CONST[name]
            return cst[0:rows, at0:at0 + cols]

        ident = k("ident")

        def half(t, h):
            return t[:, h * HALF:(h + 1) * HALF]

        def bank(n, rows=C, cols=512, first=0):
            return ps[0:rows, n, first:first + cols]

        def f32(t):
            return t.bitcast(F32)

        def tiles(t):
            return t.rearrange("p (t e) -> p t e", e=E)

        def over(t, n):
            return t.unsqueeze(2).to_broadcast([t.shape[0], t.shape[1], n])

        def again(t, n):
            return t.unsqueeze(1).to_broadcast([t.shape[0], n, t.shape[1]])

        def inside(t, b):
            return t[:, b, 1:1 + SIDE, 1:1 + SIDE]

        def x_ready(eng, version, h):
            if version == 0:
                eng.wait_ge(s[f"x{h}_loaded"], 16)
            elif version in (4, 6, 8):
                eng.wait_ge(s["state_added"], UNITS * (version // 2 - 1) - 1 + h)
            else:
                eng.wait_ge(s[f"x{version}_ready"], h + 1)

        def wait_count(eng, name, value):
            if not isinstance(value, int) or value > 0:
                eng.wait_ge(s[name], value)

        CHUNKS = [sum(MOE[j]["q"] for j in range(m)) * UNITS for m in range(3)]

        block = ctx.enter_context(nc.Block())

        @block.sync
        def _(sp):
            sp.dma_start(cst[:, 0:NORM_CONSTS], dram["consts"][:, 0:NORM_CONSTS]).then_inc(s["norm_consts_loaded"], 16)
            for h in range(2):
                sp.dma_start(half(x, h).rearrange("p (b n) -> p b n", b=2),
                             dram["x"][2 * h:2 * h + 2].rearrange("b c n -> c b n")).then_inc(s[f"x{h}_loaded"], 16)
            sp.dma_start(par[:], dram["params"]).then_inc(s["params_loaded"], 16)
            sp.dma_start(w33[:, 0], dram["w_bottom"]).then_inc(s["wb_loaded"], 16)
            sp.dma_start(cst[:, NORM_CONSTS:], dram["consts"][:, NORM_CONSTS:]).then_inc(s["consts_loaded"], 16)
            sp.dma_start(w33[:, 1], dram["w_out"]).then_inc(s["wo_loaded"], 16)
            sp.dma_start(we[:], dram["w_experts"]).then_inc(s["we_loaded"], 16)
            sp.dma_start(wa[:], dram["moe1"]).then_inc(s["moe1_loaded"], 16)
            sp.dma_start(dft_x[:], dram["dft_x"]).then_inc(s["dft_loaded"], 16)
            sp.dma_start(dft_k[:], dram["dft_k"]).then_inc(s["dft_loaded"], 16)
            sp.dma_start(dft_o[:], dram["dft_o"]).then_inc(s["dft_loaded"], 16)
            sp.dma_start(sel[:], dram["sel"]).then_inc(s["sel_loaded"], 16)
            sp.wait_ge(s["x2_ready"], 2)
            sp.dma_start(wb[:], dram["moe2"]).then_inc(s["moe2_loaded"], 16)
            sp.wait_ge(s["w2_split"], E)
            sp.dma_start(wa[:, :, 0:512], dram["moe3"]).then_inc(s["moe3_loaded"], 16)
            for h in range(2):
                x_ready(sp, 8, h)
                sp.dma_start(out[2 * h:2 * h + 2].rearrange("b c n -> c b n"),
                             half(x, h).rearrange("p (b n) -> p b n", b=2)).then_inc(s["stored"], 16)
            sp.wait_ge(s["stored"], 32)

        @block.gpsimd
        def _(pool):
            pool.memset(routes[:], 0.0).then_inc(s["routes_zero"], 1)
            pool.memset(xp[:], 0.0).then_inc(s["borders_zero"], 1)
            pool.memset(yp[:], 0.0).then_inc(s["borders_zero"], 1)

            def split(hi, lo, src, done, n):
                pool.tensor_copy(hi, src).then_inc(s["pool_step"], 1)
                pool.wait_ge(s["pool_step"], n)
                pool.tensor_tensor(lo, src, f32(hi), ALU.subtract).then_inc(done, 1)

            pool.wait_ge(s["wb_loaded"], 16)
            split(w33h[:, 0], w33l[:, 0], w33[:, 0], s["wb_split"], 1)
            pool.wait_ge(s["wo_loaded"], 16)
            split(w33h[:, 1], w33l[:, 1], w33[:, 1], s["wo_split"], 2)
            pool.wait_ge(s["we_loaded"], 16)
            split(weh[:], wel[:], we[:], s["we_split"], 3)

            gated = wb[:, POOL_T:TT]
            pool.wait_ge(s["expert_kept"], 2 * TT)
            pool.wait_ge(s["gate_ready"], 1)
            for t in range(POOL_T, TT):
                tile = wb[:, t, :].rearrange("p (e c) -> p e c", c=C)
                pool.tensor_tensor(tile, tile, over(gate[:, t * E:(t + 1) * E], C), ALU.mult).then_inc(s["pool_gated"], 1)
            pool.wait_ge(s["pool_gated"], TT - POOL_T)
            for i, w in enumerate((4 * C, 2 * C)):
                pool.tensor_tensor(gated[:, :, 0:w], gated[:, :, 0:w], gated[:, :, w:2 * w], ALU.add).then_inc(s["pool_sum"], 1)
                pool.wait_ge(s["pool_sum"], i + 1)
            pool.tensor_tensor(sq.rearrange("p (t c) -> p t c", c=C)[:, POOL_T:TT, :], gated[:, :, 0:C],
                               gated[:, :, C:2 * C], ALU.add).then_inc(s["pool_sum"], 1)

            for m, spec in enumerate(MOE):
                src = wb if spec["layer"] == 2 else wa
                unit0 = UNITS * m
                if m == 0:
                    x_ready(pool, 2, 1)
                pool.wait_ge(s[f"moe{spec['layer']}_loaded"], 16)

                def split_half(e, q, first, done):
                    at0, at1 = first * spec["q"] * C, (first + 1) * spec["q"] * C
                    pool.tensor_copy(wst_h[:, q, at0:at1], src[:, e, at0:at1])
                    pool.drain()
                    pool.tensor_tensor(wst_l[:, q, at0:at1], src[:, e, at0:at1], f32(wst_h[:, q, at0:at1]),
                                       ALU.subtract).then_inc(s[done], 1)

                def split_first(e, q):
                    wait_count(pool, "hidden_sums", e * (2 * spec["q"]) + (CHUNKS[m] - 2 * spec["q"]))
                    split_half(e, q, 0, "w1_split")

                def split_second(e, q):
                    wait_count(pool, "part_sums", e * 2 + (unit0 - 2))
                    split_half(e, q, 1, "w2_split")

                def add_parts(e, halves=(0, 1)):
                    for h in halves:
                        pool.wait_ge(s["scaled"], e * 2 + (unit0 + h + 1))
                        pool.tensor_tensor(half(x, h), half(x, h), half(parts, h), ALU.add).then_inc(s["state_added"], 1)

                for q in range(2):
                    split_first(q, q)
                    split_second(q, q)
                with pool.Fori(0, E // 2 - 1) as i:
                    for q in range(2):
                        split_first(i * 2 + (q + 2), q)
                        add_parts(i * 2 + q)
                        split_second(i * 2 + (q + 2), q)
                add_parts(E - 2)
                add_parts(E - 1, halves=(0,))

        @block.tensor
        def _(pe):
            def mm3(o, wh, wl, xhi, xlo, start=True, stop=True):
                pe.matmul(o, wh, xhi, start=start, stop=False)
                pe.matmul(o, wl, xhi, start=False, stop=False)
                return pe.matmul(o, wh, xlo, start=False, stop=stop)

            def center(n, h):
                x_ready(pe, n, h)
                pe.matmul(bank(h), k("center"), half(x, h), start=True, stop=True).then_inc(s["centered"], 1)

            def variance(n, h):
                pe.wait_ge(s["squared"], 2 * n + h + 1)
                pe.matmul(bank(2 + h), k("mean"), half(sq, h), start=True, stop=True).then_inc(s["variance"], 1)

            def norm(n):
                if n in STAGGERED:
                    for h in range(2):
                        if (n, h) != (1, 0):
                            center(n, h)
                            variance(n, h)
                else:
                    for h in range(2):
                        center(n, h)
                    for h in range(2):
                        variance(n, h)

            def keep_clock(n, b, weights=sel[:, 0, :], cols=sel[:, 0:4, :]):
                for _ in range(n):
                    pe.matmul(bank(b), weights, cols, start=True, stop=True)

            pe.wait_ge(s["routes_zero"], 1)
            keep_clock(START_CLOCK, 7, routes[:, 0:C], routes[:, 0:512])
            pe.wait_ge(s["norm_consts_loaded"], 16)
            norm(0)
            pe.wait_ge(s["params_loaded"], 16)
            for h in range(2):
                pe.wait_ge(s["normed"], h + 1)
                window = xp[:, 2 * h:2 * h + 2, 1:1 + SIDE, 1:1 + SIDE]
                for w, b0 in (("w_top", 0), ("w_center", 2)):
                    pe.matmul(bank(b0 + h, PAB), p(w), window, start=True, stop=True).then_inc(s["proj_done"], 1)

            def conv33(which, hi, lo, hi_done, lo_done, n0, done, halves=(0, 1), between={}):
                for h in halves:
                    pe.wait_ge(hi_done, n0 + h + 1)
                    pe.wait_ge(lo_done, n0 + h + 1)
                    for t in range(9):
                        if (h, t) in between:
                            between[h, t]()
                        dy, dx = divmod(t, 3)
                        wh = w33h[:, which, t * C:(t + 1) * C]
                        wl = w33l[:, which, t * C:(t + 1) * C]
                        win = (slice(None), slice(2 * h, 2 * h + 2), slice(dy, dy + SIDE), slice(dx, dx + SIDE))
                        last = mm3(bank(4 + h), wh, wl, hi[win], lo[win], start=(t == 0), stop=(t == 8))
                    last.then_inc(done, 1)

            def scores(b):
                pe.wait_ge(s["top_ready"], b // 2 + 1)
                pe.wait_ge(s["center_ready"], b // 2 + 1)
                if b == 0:
                    pe.wait_ge(s["top_ready"], 2)
                    pe.wait_ge(s["center_ready"], 2)
                for j in range(2):
                    last = pe.matmul(bank(b, cols=PIX, first=j * PIX), top[:, b * PIX + j * C:b * PIX + (j + 1) * C],
                                     cen[:, b * PIX:(b + 1) * PIX], start=True, stop=True)
                last.then_inc(s["scores_done"], 1)

            def turn_max():
                pe.wait_ge(s["consts_loaded"], 16)
                pe.wait_ge(s["score_max"], B)
                pe.transpose(bank(6, B, C), mx, ident).then_inc(s["max_turned"], 1)

            def spread_max():
                pe.wait_ge(s["max_diag"], 1)
                pe.matmul(bank(6, cols=B, first=256), k("ones", B), mxd, start=True, stop=True).then_inc(s["max_spread"], 1)

            pe.wait_ge(s["wb_split"], 1)
            conv33(0, xph, xpl, s["norm_hi"], s["norm_lo"], 0, s["bottom_done"],
                   between={**{(0, 3 + b): lambda b=b: scores(b) for b in range(B)}, (1, 0): turn_max, (1, 1): spread_max})
            pe.wait_ge(s["neg_max"], 1)
            for t in range(TT):
                if t % 4 == 0:
                    pe.wait_ge(s["bottom_biased"], t // 4 + 1)
                last = pe.transpose(bank(6 + t // 4, cols=C, first=t % 4 * C), bot[:, t * C:(t + 1) * C], ident)
                if t % 4 == 3:
                    last.then_inc(s["bottom_turned"], 1)
            pe.wait_ge(s["exp_done"], B)
            pe.matmul(bank(4, cols=B), k("ones"), es, start=True, stop=True).then_inc(s["exp_summed"], 1)
            pe.wait_ge(s["bottom_ready"], 2)
            for b in range(B):
                for par_ in range(2):
                    for j in range(2):
                        last = pe.matmul(bank(6 + b // 2, cols=C, first=(b % 2) * PIX + par_ * C),
                                         expo[:, b, j, par_::2], bot_t[:, 2 * b + j, :], start=(j == 0), stop=(j == 1))
                last.then_inc(s["mixed"], 1)
            def gates(h):
                pe.wait_ge(s["normed"], 3 + h)
                if h == 0:
                    pe.wait_ge(s["x1_ready"], 1)
                for t in range(4 * h, 4 * h + 4):
                    last = pe.matmul(bank(4, cols=E, first=t * E), xn[:, t * C:(t + 1) * C], p("gate_w"), start=True, stop=True)
                return last

            pe.wait_ge(s["wo_split"], 1)
            pe.wait_ge(s["exp_recip"], 1)
            conv33(1, xph, xpl, s["mix_hi"], s["mix_lo"], 0, s["out_conv_done"],
                   between={(1, 2): lambda: center(1, 0), (1, 4): lambda: variance(1, 0)})

            gates(0)
            norm(1)
            gates(1).then_inc(s["gates_done"], 1)
            pe.wait_ge(s["norm_hi"], 4)
            pe.wait_ge(s["norm_lo"], 4)
            pe.wait_ge(s["we_split"], 1)
            ring = [0, 1, 6, 7]

            def expert_rows(n):
                t, g = divmod(n, 2)
                if n >= 4:
                    pe.wait_ge(s["expert_kept"], n - 3)
                o = bank(ring[n % 4])
                cols, ecols = slice(t * C, (t + 1) * C), slice(g * 512, (g + 1) * 512)
                pe.matmul(o, xh[:, cols], weh[:, ecols], start=True, stop=False)
                pe.matmul(o, xh[:, cols], wel[:, ecols], start=False, stop=False)
                pe.matmul(o, xl[:, cols], weh[:, ecols], start=False, stop=True).then_inc(s["expert_out"], 1)

            for it in range(8):
                pe.wait_ge(s["sink_in"], it + 1)
                pe.matmul(bank(5, cols=64), k("ones"), plan, start=True, stop=True).then_inc(s["sink_sum"], 1)
                expert_rows(2 * it)
                expert_rows(2 * it + 1)
            pe.wait_ge(s["sink_in"], 9)
            for t in range(TT):
                last = pe.transpose(bank(2 + t // 4, E, C, t % 4 * C), plan[:, t * E:(t + 1) * E], ident)
            last.then_inc(s["plan_turned"], 1)
            pe.wait_ge(s["sel_loaded"], 16)
            pe.wait_ge(s["expert_kept"], 2 * TT)
            for e in range(E):
                if e == E - 1:
                    pe.wait_ge(s["picked"], 1)
                    for t in range(TT):
                        last = pe.transpose(bank(4, cols=E, first=64 + t * E), picked[:, t * C:(t + 1) * C], ident[0:E, 0:E])
                    last.then_inc(s["picked_turned"], 1)
                pe.wait_ge(s["gated"], e + 1)
                pe.matmul(bank(0), ident, wb[:, 0:4, e * C:(e + 1) * C], start=(e == 0), stop=(e == E - 1))
                last = pe.matmul(bank(1, cols=C), ident, wb[:, 4, e * C:(e + 1) * C], start=(e == 0), stop=(e == E - 1))
            last.then_inc(s["gated_sum"], 1)
            keep_clock(2, 5)
            for t in range(TT):
                if t % 4 == 0:
                    pe.wait_ge(s["combined"], 1 + t // 2)
                last = pe.transpose(bank(6 + t // 4, cols=C, first=t % 4 * C), sq[:, t * C:(t + 1) * C], ident)
                if t % 4 == 3:
                    last.then_inc(s["combined_turned"], 1)

            keep_clock(3, 5)
            norm(2)
            for h in range(2):
                pe.wait_ge(s["normed"], 5 + h)
                pe.matmul(bank(4 + h, KK), p("K_w"), half(xn, h), start=True, stop=True).then_inc(s["keys_done"], 1)
            for t in range(TT):
                last = pe.transpose(bank(6 + t // 4, cols=C, first=t % 4 * C), xn[:, t * C:(t + 1) * C], ident)
                if t % 4 == 3:
                    last.then_inc(s["img_turned"], 1)
            def img_pieces(*numbers):
                for n in numbers:
                    q, j = divmod(n, 2)
                    if n == 8:
                        pe.wait_ge(s["img_freq_kept"], 1)
                    ins = pe.matmul(bank(q % 4), dft_x[:, j, q * C:(q + 1) * C],
                                    img_t.rearrange("p (b j) c -> p j b c", j=2)[:, j], start=(j == 0), stop=(j == 1))
                    if j == 1:
                        ins.then_inc(s["img_freq"], 1)

            keep_clock(3, 3)
            pe.wait_ge(s["img_ready_act"], 1)
            pe.wait_ge(s["img_ready_dve"], 1)
            pe.wait_ge(s["dft_loaded"], 48)
            img_pieces(0)
            pe.wait_ge(s["key_diag"], 1)
            for t in range(TT):
                last = pe.matmul(bank(4, cols=KK, first=t * KK), keye[:, t * C:(t + 1) * C], key_d[:, t // 2, :],
                                 start=True, stop=True)
            last.then_inc(s["key_turned"], 1)
            img_pieces(1)
            pe.wait_ge(s["key_ready"], 1)
            for b in range(B):
                for j in range(2):
                    last = pe.matmul(bank(5, cols=KK, first=b * KK), img_t[:, 2 * b + j, :], key_t[:, 2 * b + j, :],
                                     start=(j == 0), stop=(j == 1))
            last.then_inc(s["filt_done"], 1)
            img_pieces(2)
            pe.wait_ge(s["filt_in"], 1)
            pe.matmul(bank(6, cols=B * KK), p("conv0_w"), filt[:, 0].rearrange("p b k -> p (b k)"),
                      start=True, stop=True).then_inc(s["filt0_done"], 1)
            for i, numbers in enumerate([(3,), (4, 5)]):
                img_pieces(*numbers)
                pe.wait_ge(s["stat_in"], i + 1)
                pe.matmul(bank(7, cols=B, first=B * i), k("ones"), st, start=True, stop=True).then_inc(s["stat_sum"], 1)
            img_pieces(6, 7)
            pe.wait_ge(s["filt_act"], 1)
            for b in range(B):
                last = pe.matmul(bank(4, KK, C, b * C), filt[:, 3, b, :], p("conv1_w"), start=True, stop=True)
            last.then_inc(s["filt1_done"], 1)
            img_pieces(8, 9)
            pe.wait_ge(s["filt1_ready"], 1)
            fring = [5, 6, 7]

            def filt_freq(q):
                if q >= 3:
                    pe.wait_ge(s["freq_mult"], q - 2)
                pe.matmul(bank(fring[q % 3]), dft_k[:, q * C:(q + 1) * C], filt_t[:], start=True, stop=True).then_inc(s["filt_freq"], 1)

            filt_freq(0)
            filt_freq(1)
            pe.wait_ge(s["img_freq_kept"], QF)
            for q in range(QF):
                if q + 2 < QF:
                    filt_freq(q + 2)
                pe.wait_ge(s["freq_mult"], q + 1)
                for b in range(B):
                    last = pe.matmul(bank(b, cols=PIX), prod_f[:, q, b * C:(b + 1) * C], dft_o[:, q, :],
                                     start=(q == 0), stop=(q == QF - 1))
                    if q == QF - 1 and b % 2:
                        last.then_inc(s["img_back"], 1)

            def mixture(m):
                spec = MOE[m]
                q_n, n = spec["q"], spec["ln"]
                norm(n)
                for h in range(2):
                    pe.wait_ge(s["normed"], 2 * n + h + 1)
                    for t in range(4 * h, 4 * h + 4):
                        last = pe.matmul(bank(4, cols=E, first=t * E), xn[:, t * C:(t + 1) * C], p(spec["router"]),
                                         start=True, stop=True)
                last.then_inc(s["logits_done"], 1)

                def front(e, h, q, peeled=False):
                    if h == 0:
                        pe.wait_ge(s["w1_split"], e + (E * m + 1))
                    for f in range(q_n):
                        if not peeled:
                            wait_count(pe, "hidden", e * (2 * q_n) + (CHUNKS[m] + q_n * (h - 1) + f + 1))
                        mm3(bank(f), wst_h[:, q, f * C:(f + 1) * C], wst_l[:, q, f * C:(f + 1) * C],
                            half(xh, h), half(xl, h)).then_inc(s["hidden_sums"], 1)

                def weights(e, h, peeled=False):
                    if not peeled:
                        wait_count(pe, "score_kept", e * 2 + (UNITS * m + h - 1))
                    pe.matmul(bank(4 + h), sel[:, e, :], half(routes, h), start=True, stop=True).then_inc(s["score_sums"], 1)

                def back(e, h, q):
                    wait_count(pe, "scaled", e * 2 + (UNITS * m + h - 1))
                    if h == 0:
                        pe.wait_ge(s["w2_split"], e + (E * m + 1))
                    for f in range(q_n):
                        pe.wait_ge(s["hidden_lo"], e * (2 * q_n) + (CHUNKS[m] + q_n * h + f + 1))
                        first = (q_n + f) * C
                        last = mm3(bank(6 + h), wst_h[:, q, first:first + C], wst_l[:, q, first:first + C],
                                   hidh[:, h, f, :], hidl[:, h, f, :], start=(f == 0), stop=(f == q_n - 1))
                    last.then_inc(s["part_sums"], 1)

                def expert(e, q):
                    front(e, 1, q)
                    weights(e, 1)
                    back(e, 0, q)
                    front(e + 1, 0, 1 - q)
                    weights(e + 1, 0)
                    back(e, 1, q)

                pe.wait_ge(s["norm_hi"], 4 + 2 * m + 1)
                pe.wait_ge(s["norm_lo"], 4 + 2 * m + 1)
                front(0, 0, 0, peeled=True)
                pe.wait_ge(s["norm_hi"], 4 + 2 * m + 2)
                pe.wait_ge(s["norm_lo"], 4 + 2 * m + 2)
                front(0, 1, 0)
                pe.wait_ge(s["route_parts"], m + 1)
                for t in range(TT):
                    last = pe.transpose(ps[0:PARTS * E, 5, :].bitcast(BF16)[:, t * C:(t + 1) * C], cparts[:, t, :],
                                        sel[:, E, :])
                last.then_inc(s["route_turned"], 1)
                back(0, 0, 0)
                pe.wait_ge(s["route_ready"], m + 1)
                weights(0, 0, peeled=True)
                weights(0, 1, peeled=True)
                front(1, 0, 1)
                weights(1, 0)
                back(0, 1, 0)
                with pe.Fori(0, E // 2 - 1) as i:
                    for q in range(2):
                        expert(i * 2 + (1 + q), 1 - q)
                front(E - 1, 1, 1)
                weights(E - 1, 1)
                back(E - 1, 0, 1)
                back(E - 1, 1, 1)

            mixture(0)

            norm(4)
            keep_clock(14, 7)
            for b in range(B):
                pe.wait_ge(s["pooled_in"], 1)
                pe.matmul(bank(b, cols=3 * C), spread[:, b, :], shiftw.rearrange("p k i -> p (k i)"),
                          start=True, stop=True).then_inc(s["offset_done"], 1)
            for b in range(B):
                if b:
                    keep_clock(3, 7)
                pe.wait_ge(s["hat_ready"], b + 1)
                for j in range(3):
                    last = pe.matmul(bank(4, cols=1, first=b), hat[:, 3 * b + j, :], wpool[:, 3 * b + j:3 * b + j + 1],
                                     start=(j == 0), stop=(j == 2))
            last.then_inc(s["deform_done"], 1)
            keep_clock(6, 7)
            mixture(1)

            norm(6)
            keep_clock(12, 7)
            pe.wait_ge(s["alpha_in"], 1)
            for b in range(B):
                last = pe.matmul(bank(b // 2, cols=PIX, first=b % 2 * PIX), spread[:, b, :],
                                 xn[:, b * PIX:(b + 1) * PIX], start=True, stop=True)
                if b % 2:
                    last.then_inc(s["sal_done"], 1)
            keep_clock(7, 7)
            mixture(2)

        @block.scalar
        def _(act):
            def norm(n, split=None):
                if n == 0:
                    act.wait_ge(s["norm_consts_loaded"], 16)
                if n in (0, 4, 6, 7):
                    act.preload_act_table_set("natural_log_exp_and_others")
                def square(h):
                    act.wait_ge(s["centered"], 2 * n + h + 1)
                    act.activation(half(sq, h), bank(h), ACT.Square).then_inc(s["squared"], 1)

                def inverse_root(h):
                    act.wait_ge(s["variance"], 2 * n + h + 1)
                    act.activation(half(rstd, h), bank(2 + h), ACT.Ln, bias=k(LN_EPS[n])).then_inc(s["log_var"], 1)
                    act.wait_ge(s["log_var"], 2 * n + h + 1)
                    act.activation(half(rstd, h), half(rstd, h), ACT.Exp, scale=-0.5).then_inc(s["rstd"], 1)

                def high_part(h):
                    if split is not None:
                        act.wait_ge(s["normed"], 2 * n + h + 1)
                        act.activation(half(xh, h), half(xn, h), ACT.Copy).then_inc(s["norm_hi"], 1)

                if n in STAGGERED:
                    for h in range(2):
                        square(h)
                        inverse_root(h)
                        high_part(h)
                else:
                    for work in (square, inverse_root, high_part):
                        for h in range(2):
                            work(h)

            norm(0)
            for h in range(2):
                act.wait_ge(s["normed"], h + 1)
                act.activation(xph[:, 2 * h:2 * h + 2].rearrange("p b y x -> p (b y x)"),
                               xp[:, 2 * h:2 * h + 2].rearrange("p b y x -> p (b y x)"), ACT.Copy).then_inc(s["norm_hi"], 1)
            for h in range(2):
                act.wait_ge(s["proj_done"], 2 * h + 1)
                act.activation(half(top, h), bank(h, PAB), ACT.Identity, bias=p("b_top", PAB)).then_inc(s["top_ready"], 1)
            def bottom_bias(h):
                act.wait_ge(s["bottom_done"], h + 1)
                act.activation(half(bot, h), bank(4 + h), ACT.Identity, bias=p("b_bottom")).then_inc(s["bottom_biased"], 1)

            bottom_bias(0)
            for b in range(B):
                act.wait_ge(s["neg_max"], 1)
                act.activation(expo[:, b].rearrange("p j n -> p (j n)"), bank(b), ACT.Exp, bias=nmx[:, b:b + 1],
                               accum_out=es[:, b:b + 1]).then_inc(s["exp_done"], 1)
            bottom_bias(1)
            for h in range(2):
                act.wait_ge(s["mix_added"], 2 * h + 2)
                act.activation(xph[:, 2 * h:2 * h + 2].rearrange("p b y x -> p (b y x)"),
                               yp[:, 2 * h:2 * h + 2].rearrange("p b y x -> p (b y x)"), ACT.Copy).then_inc(s["mix_hi"], 1)
            norm(1, split=1)
            for n in range(2 * TT):
                act.wait_ge(s["expert_out"], n + 1)
                t, g = divmod(n, 2)
                act.activation(wb[:, t, g * 512:(g + 1) * 512], bank([0, 1, 6, 7][n % 4]), ACT.Copy).then_inc(s["expert_kept"], 1)
            act.wait_ge(s["expert_kept"], 2 * TT)
            act.wait_ge(s["gate_ready"], 1)
            for e in range(E):
                for t in range(POOL_T):
                    y = wb[:, t, e * C:(e + 1) * C]
                    last = act.activation(y, y, ACT.Copy, scale=gate[:, t * E + e:t * E + e + 1])
                last.then_inc(s["gated"], 1)
            norm(2)
            for b in range(B):
                if b % 2 == 0:
                    act.wait_ge(s["key_max"], b // 2 + 1)
                act.activation(keye[:, b * PIX:(b + 1) * PIX], bank(4 + b // 2, KK, PIX, b % 2 * PIX), ACT.Exp,
                               bias=kbias[:, b:b + 1], accum_out=kes[:, b:b + 1]).then_inc(s["key_exp"], 1)
                if b == 1:
                    act.wait_ge(s["img_turned"], 1)
                    act.activation(img_t[:, 0:4, :].rearrange("p t c -> p (t c)"), bank(6), ACT.Copy).then_inc(s["img_ready_act"], 1)
            for q in range(QF):
                act.wait_ge(s["img_freq"], q + 1)
                act.activation(img_f[:, q, :], bank(q % 4), ACT.Copy).then_inc(s["img_freq_kept"], 1)
                if q == 2:
                    act.wait_ge(s["stat_sum"], 2)
                    act.activation(st, bank(7, cols=B, first=B), ACT.Ln, bias=k("eps5"), scale=1.0 / (C * KK)).then_inc(s["filt_rstd_ln"], 1)
                    act.wait_ge(s["filt_rstd_ln"], 1)
                    act.activation(st, st, ACT.Exp, scale=-0.5).then_inc(s["filt_rstd"], 1)

            def mixture(m):
                spec = MOE[m]
                q_n, n = spec["q"], spec["ln"]
                func = {"Silu": ACT.Silu, "Gelu": ACT.Gelu, "Relu": ACT.Relu}[spec["act"]]
                norm(n, split=1)
                act.wait_ge(s["exp_in"], m + 1)
                act.activation(ew, lg2, ACT.Exp).then_inc(s["exp_out"], 1)

                def front(e, h):
                    hidden(e, h)
                    keep_score(e, h)

                def hidden(e, h):
                    if spec["b1"] and h == 0:
                        act.wait_ge(s["hidden"], e * (2 * q_n) + CHUNKS[m])
                        act.activation(bias1[:, 0:q_n], p(spec["b1"]).rearrange("p (e f) -> p e f", f=q_n)[:, e, :],
                                       ACT.Copy).then_inc(s["bias_kept"], 1)
                        act.wait_ge(s["bias_kept"], e + (E * (m - 1) + 1))
                    wait_count(act, "part_sums", e * 2 + (UNITS * m + h - 1))
                    for f in range(q_n):
                        chunk = e * (2 * q_n) + (CHUNKS[m] + q_n * h + f + 1)
                        act.wait_ge(s["hidden_sums"], chunk)
                        bias = 0.0
                        if spec["b1"]:
                            bias = bias1[:, f:f + 1]
                        act.activation(hid[:, h, f, :], bank(f), func, bias=bias).then_inc(s["hidden"], 1)
                        if f % 2 == 0:
                            act.wait_ge(s["hidden"], chunk)
                            act.activation(hidh[:, h, f, :], hid[:, h, f, :], ACT.Copy).then_inc(s["hidden_hi_act"], 1)

                def keep_score(e, h):
                    act.wait_ge(s["score_sums"], e * 2 + (UNITS * m + h + 1))
                    wait_count(act, "scaled", e * 2 + (UNITS * m + h - 1))
                    act.activation(half(score, h), bank(4 + h), ACT.Copy).then_inc(s["score_kept"], 1)

                hidden(0, 0)
                hidden(0, 1)
                keep_score(0, 0)
                keep_score(0, 1)
                with act.Fori(0, E - 1) as i:
                    for h in range(2):
                        front(i + 1, h)

            mixture(0)
            norm(4)
            for b in range(B):
                act.wait_ge(s["pos_ready"], b + 1)
                seg = pos[:, 3 * b:3 * b + 3, :].rearrange("p a c -> p (a c)")
                act.activation(seg, seg, ACT.Abs, bias=k("minus_i")).then_inc(s["dist_done"], 1)
                act.wait_ge(s["dist_done"], b + 1)
                act.activation(hat[:, 3 * b:3 * b + 3, :].rearrange("p a c -> p (a c)"), seg, ACT.Relu,
                               bias=1.0, scale=-1.0).then_inc(s["hat_ready"], 1)
            act.wait_ge(s["deform_done"], 1)
            act.activation(gate4, bank(4, cols=B), ACT.Exp, bias=neg_b, scale=-1.0).then_inc(s["deform_exp"], 1)
            mixture(1)
            norm(6)
            act.preload_act_table_set("sigmoid_and_others")
            for h in range(2):
                act.wait_ge(s["sal_done"], h + 1)
                act.activation(half(fm, h), bank(h), ACT.Relu).then_inc(s["sal_rectified"], 1)
            for h in range(2):
                act.wait_ge(s["sal_ready"], h + 1)
                act.activation(half(fm, h), half(fm, h), ACT.Sigmoid, scale=p("scale")).then_inc(s["sal_sig"], 1)
            mixture(2)

        @block.vector
        def _(dve):
            steps = [0]

            def step(ins):
                steps[0] += 1
                ins.then_inc(s["dve_step"], 1)
                dve.wait_ge(s["dve_step"], steps[0])

            def norm(n, split=None):
                for h in range(2):
                    norm_half(n, h)
                if split is not None:
                    for h in range(2):
                        norm_low(n, h, split)

            def norm_half(n, h):
                dve.wait_ge(s["rstd"], 2 * n + h + 1)
                if n == 0:
                    dve.wait_ge(s["borders_zero"], 1)
                    dve.tensor_tensor(xp[:, 2 * h:2 * h + 2, 1:1 + SIDE, 1:1 + SIDE],
                                      bank(h).rearrange("p (b y x) -> p b y x", b=2, y=SIDE),
                                      half(rstd, h).rearrange("p (b y x) -> p b y x", b=2, y=SIDE),
                                      ALU.mult).then_inc(s["normed"], 1)
                else:
                    dve.tensor_tensor(half(xn, h), bank(h), half(rstd, h), ALU.mult).then_inc(s["normed"], 1)

            def norm_low(n, h, split):
                dve.wait_ge(s["norm_hi"], split + h + 1)
                dve.wait_ge(s["normed"], 2 * n + h + 1)
                dve.tensor_tensor(half(xl, h), half(xn, h), f32(half(xh, h)), ALU.subtract).then_inc(s["norm_lo"], 1)

            norm(0)
            for h in range(2):
                dve.wait_ge(s["norm_hi"], h + 1)
                dve.wait_ge(s["normed"], h + 1)
                seg = [t[:, 2 * h:2 * h + 2].rearrange("p b y x -> p (b y x)") for t in (xpl, xp, xph)]
                dve.tensor_tensor(seg[0], seg[1], f32(seg[2]), ALU.subtract).then_inc(s["norm_lo"], 1)
            dve.wait_ge(s["params_loaded"], 16)
            for h in range(2):
                dve.wait_ge(s["proj_done"], 2 * h + 2)
                dve.tensor_scalar(half(cen, h), bank(2 + h, PAB), p("b_center", PAB), None, ALU.add).then_inc(s["center_ready"], 1)
            for b in range(B):
                dve.wait_ge(s["scores_done"], b + 1)
                dve.tensor_reduce(mx[:, b:b + 1], bank(b), AX.X, ALU.max).then_inc(s["score_max"], 1)
            dve.wait_ge(s["max_turned"], 1)
            step(dve.tensor_reduce(mx4, bank(6, B, C), AX.X, ALU.max))
            dve.tensor_scalar(mxd, ident[0:B, 0:B], mx4, -1.0, ALU.mult, ALU.mult).then_inc(s["max_diag"], 1)
            dve.wait_ge(s["max_spread"], 1)
            dve.tensor_copy(nmx, bank(6, cols=B, first=256)).then_inc(s["neg_max"], 1)
            dve.wait_ge(s["consts_loaded"], 16)
            dve.wait_ge(s["params_loaded"], 16)
            shifts = k("shift").rearrange("p (d i) -> p d i", d=3)
            woff = p("w_offset")
            for j in range(3):
                step(dve.tensor_scalar(shiftw[:, j, :], shifts[:, 0, :], woff[:, 3 * j:3 * j + 1], None, ALU.mult))
                for d in range(1, 3):
                    step(dve.scalar_tensor_tensor(shiftw[:, j, :], shifts[:, d, :], woff[:, 3 * j + d:3 * j + d + 1],
                                                  shiftw[:, j, :], ALU.mult, ALU.add))
            step(dve.tensor_scalar(neg_wf, p("wf"), -1.0, None, ALU.mult))
            step(dve.memset(pair, -BIG))
            step(dve.tensor_scalar(neg_b, p("b_deform"), -1.0, None, ALU.mult))

            for g in range(2):
                dve.wait_ge(s["bottom_turned"], g + 1)
                dve.tensor_copy(bot_t[:, 4 * g:4 * g + 4, :].rearrange("p t c -> p (t c)"), bank(6 + g)).then_inc(s["bottom_ready"], 1)
            dve.wait_ge(s["exp_summed"], 1)
            dve.reciprocal(rs, bank(4, cols=B)).then_inc(s["exp_recip"], 1)
            dve.wait_ge(s["exp_recip"], 1)
            dve.wait_ge(s["borders_zero"], 2)
            for b in range(B):
                dve.wait_ge(s["mixed"], b // 2 * 2 + 2)
                dve.scalar_tensor_tensor(inside(yp, b), bank(6 + b // 2, cols=PIX, first=b % 2 * PIX).rearrange("p (y x) -> p y x", y=SIDE),
                                         rs[:, b:b + 1], inside(xp, b), ALU.mult, ALU.add).then_inc(s["mix_added"], 1)
                if b % 2:
                    h = b // 2
                    dve.wait_ge(s["mix_hi"], h + 1)
                    dve.wait_ge(s["mix_added"], b + 1)
                    seg = [t[:, 2 * h:2 * h + 2].rearrange("p b y x -> p (b y x)") for t in (xpl, yp, xph)]
                    dve.tensor_tensor(seg[0], seg[1], f32(seg[2]), ALU.subtract).then_inc(s["mix_lo"], 1)
            for h in range(2):
                dve.wait_ge(s["out_conv_done"], h + 1)
                dve.scalar_tensor_tensor(half(x, h), bank(4 + h), p("b_out"), half(x, h), ALU.add, ALU.add).then_inc(s["x1_ready"], 1)
                if h == 1:
                    norm_low(1, 0, 2)
                norm_half(1, h)
            norm_low(1, 1, 2)

            dve.wait_ge(s["gates_done"], 1)
            dve.tensor_scalar(plan, bank(4, cols=64), 1e-10, None, ALU.max).then_inc(s["sink_in"], 1)
            plan3 = tiles(plan)
            for it in range(8):
                dve.wait_ge(s["sink_sum"], it + 1)
                dve.wait_ge(s["sink_in"], it + 1)
                step(dve.tensor_reduce(r8, bank(5, cols=64).rearrange("p (t e) -> p e t", e=E), AX.X, ALU.add))
                step(dve.reciprocal(r8b, r8))
                step(dve.tensor_tensor(plan3, plan3, again(r8b, TT), ALU.mult))
                step(dve.tensor_reduce(r8, plan3, AX.X, ALU.add))
                step(dve.reciprocal(r8b, r8))
                dve.tensor_tensor(plan3, plan3, over(r8b, E), ALU.mult).then_inc(s["sink_in"], 1)
            dve.wait_ge(s["sink_in"], 9)
            dve.tensor_scalar(gate, plan, 0.5, None, ALU.is_gt).then_inc(s["gate_ready"], 1)
            dve.wait_ge(s["gate_ready"], 1)
            step(dve.tensor_reduce(r8, tiles(gate), AX.X, ALU.add))
            step(dve.tensor_scalar(r8, r8, 1.0, None, ALU.max))
            step(dve.reciprocal(r8b, r8))
            step(dve.tensor_tensor(tiles(share), tiles(gate), over(r8b, E), ALU.mult))
            dve.wait_ge(s["plan_turned"], 1)
            src = ps[0:E, 2:4, :].rearrange("p g n -> p (g n)")
            for r in range(TOPK0 // 8):
                step(dve.max(top8, src))
                last = dve.match_replace(picked, top8, src, -1.0)
                if r < TOPK0 // 8 - 1:
                    step(last)
                src = picked
            last.then_inc(s["picked"], 1)
            dve.wait_ge(s["picked_turned"], 1)
            step(dve.tensor_scalar(pick_w, bank(4, cols=64, first=64), 0.0, None, ALU.is_lt))
            step(dve.tensor_reduce(cnt, tiles(pick_w), AX.X, ALU.add))
            step(dve.tensor_tensor(pick_w, pick_w, share, ALU.mult))
            step(dve.tensor_scalar(cnt, cnt, 1.0, None, ALU.add))
            step(dve.tensor_reduce(r8, tiles(pick_w), AX.X, ALU.add))
            step(dve.reciprocal(r8b, cnt))
            step(dve.tensor_tensor(r8, r8, r8b, ALU.mult))
            sqt = sq.rearrange("p (t c) -> p t c", c=C)
            dve.wait_ge(s["gated_sum"], 1)
            dve.tensor_tensor(sqt[:, 0:4, :], bank(0).rearrange("p (t c) -> p t c", c=C), over(r8[:, 0:4], C),
                              ALU.mult).then_inc(s["combined"], 1)
            dve.tensor_scalar(sqt[:, 4, :], bank(1, cols=C), r8[:, 4:5], None, ALU.mult).then_inc(s["combined"], 1)
            dve.wait_ge(s["pool_sum"], 3)
            dve.tensor_tensor(sqt[:, POOL_T:TT, :], sqt[:, POOL_T:TT, :], over(r8[:, POOL_T:TT], C),
                              ALU.mult).then_inc(s["combined"], 1)
            for h in range(2):
                dve.wait_ge(s["combined_turned"], h + 1)
                dve.tensor_tensor(half(x, h), bank(6 + h), half(x, h), ALU.add).then_inc(s["x2_ready"], 1)

            norm(2)
            for h in range(2):
                ims = slice(2 * h, 2 * h + 2)
                dve.wait_ge(s["keys_done"], h + 1)
                step(dve.tensor_reduce(kmx[:, ims], bank(4 + h, KK).rearrange("p (b n) -> p b n", b=2), AX.X, ALU.max))
                step(dve.tensor_scalar(kmx[:, ims], kmx[:, ims], p("K_b", KK), None, ALU.add))
                dve.tensor_scalar(kbias[:, ims], kmx[:, ims], -1.0, p("K_b", KK), ALU.mult, ALU.add).then_inc(s["key_max"], 1)
            dve.wait_ge(s["img_turned"], 2)
            dve.tensor_copy(img_t[:, 4:8, :].rearrange("p t c -> p (t c)"), bank(7)).then_inc(s["img_ready_dve"], 1)
            dve.wait_ge(s["key_exp"], B)
            step(dve.reciprocal(krs, kes))
            dve.tensor_tensor(key_d[:], again(ident[0:KK, 0:KK], B), over(krs, KK), ALU.mult).then_inc(s["key_diag"], 1)
            dve.wait_ge(s["key_turned"], 1)
            dve.tensor_copy(key_t.rearrange("p t k -> p (t k)"), bank(4, cols=TT * KK)).then_inc(s["key_ready"], 1)
            dve.wait_ge(s["filt_done"], 1)
            f0, f1, f2, f3 = [filt[:, j] for j in range(4)]

            def flat(t):
                return t.rearrange("p b k -> p (b k)")

            dve.tensor_copy(flat(f0), bank(5, cols=B * KK)).then_inc(s["filt_in"], 1)
            dve.wait_ge(s["filt0_done"], 1)
            step(dve.tensor_scalar(flat(f1), bank(6, cols=B * KK), p("conv0_b"), None, ALU.add))
            dve.tensor_reduce(st, f1, AX.X, ALU.add).then_inc(s["stat_in"], 1)
            dve.wait_ge(s["stat_sum"], 1)
            step(dve.scalar_tensor_tensor(f1, over(bank(7, cols=B), KK), 1.0 / (C * KK), f1, ALU.mult, ALU.subtract))
            step(dve.tensor_tensor(f2, f1, f1, ALU.mult))
            dve.tensor_reduce(st, f2, AX.X, ALU.add).then_inc(s["stat_in"], 1)
            step(dve.scalar_tensor_tensor(f0, f1, -1.0, again(p("ln_w"), B), ALU.mult, ALU.mult))
            dve.wait_ge(s["filt_rstd"], 1)
            for b in range(B):
                last = dve.scalar_tensor_tensor(f1[:, b], f0[:, b], st[:, b:b + 1], p("ln_b"), ALU.mult, ALU.add)
            step(last)
            dve.tensor_scalar(flat(f3), flat(f1), 0.0, None, ALU.max).then_inc(s["filt_act"], 1)
            dve.wait_ge(s["filt1_done"], 1)
            dve.tensor_tensor(filt_t.rearrange("p (b c) -> p b c", b=B), bank(4, KK).rearrange("p (b c) -> p b c", b=B),
                              again(p("conv1_b", KK), B), ALU.add).then_inc(s["filt1_ready"], 1)
            for q in range(QF):
                dve.wait_ge(s["filt_freq"], q + 1)
                dve.wait_ge(s["img_freq_kept"], q + 1)
                dve.tensor_tensor(prod_f[:, q, :], bank([5, 6, 7][q % 3]), img_f[:, q, :], ALU.mult).then_inc(s["freq_mult"], 1)
            for h in range(2):
                dve.wait_ge(s["img_back"], h + 1)
                dve.tensor_tensor(half(x, h).rearrange("p (b n) -> p b n", b=2), ps[:, 2 * h:2 * h + 2, 0:PIX],
                                  half(x, h).rearrange("p (b n) -> p b n", b=2), ALU.add).then_inc(s["x3_ready"], 1)

            def mixture(m):
                spec = MOE[m]
                q_n, n = spec["q"], spec["ln"]
                def front(e, h):
                    for f in range(q_n):
                        pair = e * q_n + (CHUNKS[m] // 2 + (q_n * h + f) // 2 + 1)
                        if f % 2 == 1:
                            dve.wait_ge(s["hidden"], e * (2 * q_n) + (CHUNKS[m] + q_n * h + f + 1))
                            dve.tensor_copy(hidh[:, h, f, :], hid[:, h, f, :]).then_inc(s["hidden_hi_dve"], 1)
                            dve.wait_ge(s["hidden_hi_dve"], pair)
                        else:
                            dve.wait_ge(s["hidden_hi_act"], pair)
                        dve.tensor_tensor(hidl[:, h, f, :], hid[:, h, f, :], f32(hidh[:, h, f, :]),
                                          ALU.subtract).then_inc(s["hidden_lo"], 1)

                norm(n, split=4 + 2 * m)
                dve.wait_ge(s["logits_done"], m + 1)
                if spec["layer"] == 3:
                    step(dve.tensor_tensor(tiles(lg), tiles(bank(4, cols=64)), again(p("bg3"), TT), ALU.add))
                else:
                    step(dve.tensor_copy(lg, bank(4, cols=64)))
                def largest():
                    for t in range(TT):
                        last = dve.max(tops[:, t * E:(t + 1) * E], lg[:, t * E:(t + 1) * E])
                        if t < TT - 1:
                            last.then_inc(s["dve_step"], 1)
                            steps[0] += 1
                    step(last)

                if spec["layer"] == 2:
                    step(dve.tensor_reduce(m8, tiles(lg), AX.X, ALU.max))
                else:
                    largest()
                first = m8 if spec["layer"] == 2 else tiles(tops)[:, :, 0]
                dve.tensor_tensor(tiles(lg2), tiles(lg), over(first, E), ALU.subtract).then_inc(s["exp_in"], 1)
                if spec["layer"] == 2:
                    dve.wait_ge(s["exp_out"], m + 1)
                    step(dve.tensor_reduce(r8, tiles(ew), AX.X, ALU.add))
                    step(dve.reciprocal(r8b, r8))
                    step(dve.tensor_tensor(tiles(lg), tiles(ew), over(r8b, E), ALU.mult))
                    largest()
                step(dve.tensor_copy(tiles(pair)[:, :, 0:2], tiles(tops)[:, :, 0:2]))
                for t in range(TT):
                    last = dve.match_replace(oh1[:, t * E:(t + 1) * E], pair[:, t * E:(t + 1) * E], lg[:, t * E:(t + 1) * E], BIG)
                    if t < TT - 1:
                        last.then_inc(s["dve_step"], 1)
                        steps[0] += 1
                step(last)
                dve.wait_ge(s["exp_out"], m + 1)
                values = lg if spec["layer"] == 2 else ew
                step(dve.scalar_tensor_tensor(wgt, oh1, BIG, values, ALU.is_equal, ALU.mult))
                step(dve.tensor_reduce(r8, tiles(wgt), AX.X, ALU.add))
                if spec["layer"] == 2:
                    step(dve.tensor_scalar(r8, r8, 1e-6, None, ALU.add))
                step(dve.reciprocal(r8b, r8))
                step(dve.tensor_tensor(tiles(wgt), tiles(wgt), over(r8b, E), ALU.mult))
                step(dve.tensor_copy(cparts[:, :, 0:E], tiles(wgt)))
                step(dve.tensor_tensor(tiles(rem), tiles(wgt), cparts[:, :, 0:E], ALU.subtract))
                step(dve.tensor_copy(cparts[:, :, E:2 * E], tiles(rem)))
                step(dve.tensor_tensor(tiles(rem), tiles(rem), cparts[:, :, E:2 * E], ALU.subtract))
                dve.tensor_copy(cparts[:, :, 2 * E:3 * E], tiles(rem)).then_inc(s["route_parts"], 1)
                front(0, 0)
                dve.wait_ge(s["route_turned"], m + 1)
                dve.wait_ge(s["routes_zero"], 1)
                dve.tensor_copy(routes[0:PARTS * E, :], ps[0:PARTS * E, 5, :].bitcast(BF16)).then_inc(s["route_ready"], 1)

                def back(e, h):
                    unit = e * 2 + (UNITS * m + h + 1)
                    dve.wait_ge(s["part_sums"], unit)
                    dve.wait_ge(s["score_kept"], unit)
                    wait_count(dve, "state_added", e * 2 + (UNITS * m + h - 1))
                    if spec["b2"]:
                        dve.scalar_tensor_tensor(half(parts, h), bank(6 + h), p(spec["b2"])[:, bass.ds(e, 1)], half(score, h),
                                                 ALU.add, ALU.mult).then_inc(s["scaled"], 1)
                    else:
                        dve.tensor_tensor(half(parts, h), bank(6 + h), half(score, h), ALU.mult).then_inc(s["scaled"], 1)

                def expert(e):
                    front(e, 1)
                    back(e, 0)
                    front(e + 1, 0)
                    back(e, 1)

                expert(0)
                with dve.Fori(0, E - 2) as i:
                    expert(i + 1)
                front(E - 1, 1)
                back(E - 1, 0)
                back(E - 1, 1)
                dve.wait_ge(s["scaled"], UNITS * (m + 1))
                dve.wait_ge(s["state_added"], UNITS * (m + 1) - 1)
                dve.tensor_tensor(half(x, 1), half(x, 1), half(parts, 1), ALU.add).then_inc(s["state_added"], 1)

            def norm_and_pool(n):
                for h in range(2):
                    norm_half(n, h)
                    dve.wait_ge(s["normed"], 2 * n + h + 1)
                    last = dve.tensor_reduce(pool4[:, 2 * h:2 * h + 2], half(xn, h).rearrange("p (b n) -> p b n", b=2), AX.X, ALU.add)
                    if h == 0:
                        last.then_inc(s["dve_step"], 1)
                        steps[0] += 1
                step(last)

            mixture(0)

            norm_and_pool(4)
            step(dve.tensor_scalar(pool4, pool4, 1.0 / PIX, None, ALU.mult))
            dve.tensor_copy(spread, over(pool4, C)).then_inc(s["pooled_in"], 1)
            step(dve.tensor_tensor(wpool.rearrange("p (b k) -> p b k", b=B), over(pool4, 3), again(p("w_deform"), B), ALU.mult))
            for b in range(B):
                dve.wait_ge(s["offset_done"], b + 1)
                seg = pos[:, 3 * b:3 * b + 3, :].rearrange("p a c -> p (a c)")
                step(dve.tensor_tensor(seg, bank(b, cols=3 * C), k("base"), ALU.add))
                dve.tensor_scalar(seg, seg, 0.0, C - 1.0, ALU.max, ALU.min).then_inc(s["pos_ready"], 1)
            dve.wait_ge(s["deform_exp"], 1)
            step(dve.tensor_scalar(gate4, gate4, 1.0, None, ALU.add))
            step(dve.reciprocal(gate4, gate4))
            for b in range(B):
                cols = slice(b * PIX, (b + 1) * PIX)
                last = dve.scalar_tensor_tensor(x[:, cols], xn[:, cols], gate4[:, b:b + 1], x[:, cols], ALU.mult, ALU.add)
                if b % 2:
                    last.then_inc(s["x5_ready"], 1)
            mixture(1)

            norm_and_pool(6)
            step(dve.tensor_scalar(pool4, pool4, 1.0 / SALIENCY_AREA, 1.0 / C, ALU.mult, ALU.mult))
            dve.tensor_tensor(spread, over(pool4, C), again(p("conv_w"), B), ALU.mult).then_inc(s["alpha_in"], 1)
            for h in range(2):
                dve.tensor_scalar(half(x, h), half(x, h), 1.0, None, ALU.add).then_inc(s["one_added"], 1)
            for h in range(2):
                dve.wait_ge(s["sal_rectified"], h + 1)
                dve.scalar_tensor_tensor(half(fm, h), half(fm, h), TH, half(fm, h), ALU.is_gt, ALU.mult).then_inc(s["sal_ready"], 1)
            for h in range(2):
                dve.wait_ge(s["sal_sig"], h + 1)
                dve.wait_ge(s["one_added"], h + 1)
                dve.scalar_tensor_tensor(half(x, h), half(fm, h), neg_wf, half(x, h), ALU.mult, ALU.add).then_inc(s["x7_ready"], 1)
            mixture(2)


def constants():
    cols = {
        "center": np.eye(C) - 1.0 / C, "mean": np.full((C, C), 1.0 / C), "ident": np.eye(C), "ones": np.ones((C, C)),
        "shift": np.concatenate([np.eye(C, k=1 - d) for d in range(3)], 1),
        "base": np.broadcast_to((np.arange(C)[None, :] + np.arange(3)[:, None] - 1).reshape(-1), (C, 3 * C)),
        "minus_i": -np.arange(C)[:, None],
        "eps6": np.full((C, 1), 1e-6), "eps5": np.full((C, 1), 1e-5),
    }
    packed = np.concatenate([cols[n] for n in CONST], 1).astype(np.float32)
    sel = np.zeros((C, E + 1, C), np.float32)
    for e in range(E):
        sel[e:PARTS * E:E, e, :] = 1.0
    sel[:, E, :] = np.eye(C)

    freqs = [(u, v) for u in range(GRID) for v in range(GRID)
             if (u, v) != (0, 0) and (u, v) < ((-u) % GRID, (-v) % GRID)]
    assert len(freqs) == FREQ
    fu, fv = (np.array([f[i] for f in freqs], np.float64) for i in range(2))
    y, xx = np.divmod(np.arange(PIX), SIDE)
    i, j = np.divmod(np.arange(KK), KW)
    angle = 2 * np.pi / GRID
    ta = angle * (np.outer(y, fu) + np.outer(xx, fv))
    tk = angle * (np.outer(i - KW // 2, fu) + np.outer(j - KW // 2, fv))
    ar, ai, br, bi = np.cos(ta), -np.sin(ta), np.cos(tk), np.sin(tk)
    pad = QF * C - 1 - 3 * FREQ

    def rows(first, a, b, c):
        n = first.shape[0]
        return np.concatenate([first, a, b, c, np.zeros((n, pad))], 1)

    to_x = rows(np.ones((PIX, 1)), ar + ai, ar, ai)
    to_k = rows(np.ones((KK, 1)), br, bi - br, br + bi)
    re, im = 2 * ar, 2 * ai
    back = rows(np.ones((PIX, 1)), re + im, im, -re).T / GRID ** 2
    f32 = np.float32
    return {
        "consts": packed,
        "sel": sel,
        "dft_x": np.ascontiguousarray(to_x.reshape(2, C, QF * C).transpose(1, 0, 2)).astype(f32),
        "dft_k": np.ascontiguousarray(to_k).astype(f32),
        "dft_o": np.ascontiguousarray(back.reshape(QF, C, PIX).transpose(1, 0, 2)).astype(f32),
    }


def laid_out(a):
    def col(v, rows=C):
        m = np.zeros((C, v.shape[-1] if v.ndim > 1 else 1), np.float32)
        m[:v.shape[0]] = v.reshape(v.shape[0], -1)
        return m

    def every(v):
        v = np.asarray(v).reshape(1, -1)
        return np.broadcast_to(v, (C, v.shape[1]))

    par = {
        "b_bottom": col(a["L0_conv_b_bottom"]), "b_out": col(a["L0_conv_b_out"]),
        "b_top": col(a["L0_conv_b_top"]), "b_center": col(a["L0_conv_b_center"]),
        "w_top": a["L0_conv_w_top"][:, :, 0, 0].T, "w_center": a["L0_conv_w_center"][:, :, 0, 0].T,
        "gate_w": a["L0_ffn_gate_w"][0], "K_w": a["L1_conv_K_w"].T, "K_b": col(a["L1_conv_K_b"]),
        "conv0_w": a["L1_conv_conv0_w"].T, "conv0_b": col(a["L1_conv_conv0_b"]),
        "ln_w": a["L1_conv_ln_w"].reshape(C, KK), "ln_b": a["L1_conv_ln_b"].reshape(C, KK),
        "conv1_w": a["L1_conv_conv1_w"].T, "conv1_b": every(a["L1_conv_conv1_b"]), "Wg1": a["L1_ffn_Wg"],
        "w_offset": every(a["L2_conv_w_offset"]), "w_deform": every(a["L2_conv_w_deform"]),
        "b_deform": every(a["L2_conv_b_deform"]), "Wg2": a["L2_ffn_Wg"],
        "L2_b1": a["L2_ffn_b1"].reshape(E * 4, C).T, "L2_b2": a["L2_ffn_b2"].T,
        "conv_w": every(a["L3_conv_conv_w"]), "scale": every(a["L3_conv_scale"]), "wf": every(a["L3_conv_wf"]),
        "wg3": a["L3_ffn_wg"], "bg3": every(a["L3_ffn_bg"]),
        "L3_b1": a["L3_ffn_b1"].reshape(E * 2, C).T, "L3_b2": a["L3_ffn_b2"].T,
    }

    def experts(w1, w2, q):
        return np.concatenate([w1.transpose(1, 0, 2), w2.reshape(E, q, C, C).transpose(2, 0, 1, 3).reshape(C, E, q * C)], 2)

    return {
        "x": a["x"].reshape(B, C, PIX),
        "params": np.concatenate([par[n] for n in PARAM], 1),
        "w_bottom": a["L0_conv_w_bottom"].transpose(1, 2, 3, 0).reshape(C, 9 * C),
        "w_out": a["L0_conv_w_out"].transpose(1, 2, 3, 0).reshape(C, 9 * C),
        "w_experts": a["L0_ffn_experts"].transpose(1, 0, 2).reshape(C, E * C),
        "moe1": experts(a["L1_ffn_W1"], a["L1_ffn_W2"], 4),
        "moe2": experts(a["L2_ffn_W1"], a["L2_ffn_W2"], 4),
        "moe3": experts(a["L3_ffn_w1"], a["L3_ffn_w2"], 2),
    }


def kernel(**inputs):
    import ml_dtypes
    import concourse.bacc as bacc
    from concourse.bass_utils import run_bass_kernel_spmd as run

    nc = bacc.Bacc("TRN2", target_bir_lowering=False, num_devices=1)
    arrays, dram = {}, {}
    given = {**laid_out({n: np.asarray(v) for n, v in inputs.items()}), **constants()}
    given["sel"] = given["sel"].astype(ml_dtypes.bfloat16)
    for name, v in given.items():
        v = np.ascontiguousarray(v)
        arrays[f"in_{name}"] = v
        dram[name] = nc.dram_tensor(f"in_{name}", v.shape, mybir.dt.from_np(v.dtype), kind="ExternalInput").ap()
    out = nc.dram_tensor("out_0", (B, C, PIX), F32, kind="ExternalOutput").ap()
    metaformer(nc, dram, out)
    r = run(nc, [arrays], core_ids=[0])
    return r.results[0]["out_0"].reshape(B, C, SIDE, SIDE)
```

```python
from contextlib import ExitStack

import numpy as np

import concourse.bass as bass
from concourse import mybir

F32 = mybir.dt.float32
F32R = mybir.dt.float32r
BF16 = mybir.dt.bfloat16
ALU = mybir.AluOpType
ACT = mybir.ActivationFunctionType
AX = mybir.AxisListType

C = 128
B = 4
SIDE = 16
PIX = SIDE * SIDE
N = B * PIX
HALF = N // 2
TT = N // C
PAD = SIDE + 2
PAB = 16
E = 8
TOPK0 = N // B // E
KW = 7
KK = KW * KW
POOL_T = 5
TH = 0.01
SALIENCY_AREA = 56 * 56
BIG = 3.0e38

GRID = SIDE + KW // 2
FREQ = (GRID * GRID - 1) // 2
QF = -(-(1 + 3 * FREQ) // C)

PARAM = {}
for _name, _cols in [
    ("b_bottom", 1), ("b_out", 1), ("b_top", 1), ("b_center", 1), ("w_top", PAB), ("w_center", PAB),
    ("gate_w", E), ("K_w", KK), ("K_b", 1), ("conv0_w", C), ("conv0_b", 1), ("ln_w", KK), ("ln_b", KK),
    ("conv1_w", C), ("conv1_b", C), ("Wg1", E), ("w_offset", 9), ("w_deform", 3), ("b_deform", 1),
    ("Wg2", E), ("L2_b1", E * 4), ("L2_b2", E), ("conv_w", C), ("scale", 1), ("wf", 1),
    ("wg3", E), ("bg3", E), ("L3_b1", E * 2), ("L3_b2", E),
]:
    PARAM[_name] = (sum(c for _, c in PARAM.values()), _cols)
PARAM_COLS = sum(c for _, c in PARAM.values())

CONST = {}
for _name, _cols in [("center", C), ("mean", C), ("eps6", 1), ("eps5", 1), ("ident", C), ("ones", C),
                     ("minus_i", 1), ("shift", 3 * C), ("base", 3 * C)]:
    CONST[_name] = (sum(c for _, c in CONST.values()), _cols)
NORM_CONSTS = CONST["ident"][0]
CONST_COLS = sum(c for _, c in CONST.values())

UNITS = 2 * E
MOE = [
    dict(layer=1, ln=3, q=4, act="Silu", router="Wg1", b1=None, b2=None),
    dict(layer=2, ln=5, q=4, act="Gelu", router="Wg2", b1="L2_b1", b2="L2_b2"),
    dict(layer=3, ln=7, q=2, act="Relu", router="wg3", b1="L3_b1", b2="L3_b2"),
]
START_CLOCK = 7
LAST_COLUMNS = (slice(0, HALF // 2), slice(HALF // 2, HALF))
LN_EPS = ["eps6", "eps5"] * 4

SIGNALS = [
    "x0_loaded", "x1_loaded", "params_loaded", "norm_consts_loaded", "consts_loaded", "wb_loaded", "wo_loaded", "we_loaded", "dft_loaded", "rows_stored", "scores0_in", "scores1_in",
    "moe1_loaded", "moe2_loaded", "moe3_loaded", "stored",
    "borders_zero", "quiet_zero", "wb_split", "wo_split", "we_split", "pool_step",
    "centered", "squared", "variance", "log_var", "rstd", "normed", "norm_hi", "norm_lo",
    "dve_step",
    "proj_done", "top_ready", "center_ready", "scores_done", "score_max", "max_turned", "max_diag", "max_spread",
    "neg_max", "exp_done", "exp_summed", "exp_recip",
    "bottom_done", "bottom_biased", "bottom_turned", "bottom_ready", "mixed", "mix_added", "mix_hi", "mix_lo",
    "out_conv_done", "x1_ready",
    "gates_done", "expert_out", "expert_kept", "sink_in", "sink_sum", "plan_turned", "plan_ready",
    "gate_ready", "gated", "gated_sum", "pool_gated", "pool_sum",
    "picked", "picked_turned", "combined", "combined_turned", "x2_ready",
    "keys_done", "key_max", "key_exp", "key_diag", "key_turned", "key_ready", "img_turned", "img_ready_act", "img_ready_dve",
    "filt_done", "filt_in", "filt0_done", "stat_in", "stat_sum", "filt_rstd_ln", "filt_rstd", "filt_act", "filt1_done", "filt1_ready",
    "img_freq", "img_freq_kept", "filt_freq", "freq_mult", "img_back", "x3_ready",
    "pooled_in", "offset_done", "pos_ready", "dist_done", "hat_ready", "deform_done", "deform_exp", "x5_ready",
    "alpha_in", "one_added", "sal_done", "sal_rectified", "sal_ready", "sal_sig", "x7_ready",
    "logits_done", "exp_in", "exp_out", "routed", "route_turned", "rows_ready",
    "w1_split", "w2_high", "w2_split", "hidden_sums", "bias_kept", "hidden", "hidden_hi_act", "hidden_hi_dve", "hidden_lo", "part_sums", "scaled",
    "state_added", "last_sums", "last_scaled", "last_added",
]


def metaformer(nc, dram, out):
    ctx = ExitStack()
    with ctx:
        def sb(name, shape, dt=F32, scope=ctx):
            return scope.enter_context(nc.sbuf_tensor(name, shape, dt))

        s = {name: ctx.enter_context(nc.semaphore(name)) for name in SIGNALS}

        x = sb("x", [C, N])
        xn = sb("xn", [C, N])
        xh = sb("xh", [C, N], F32R)
        xl = sb("xl", [C, N], F32R)
        sq = sb("sq", [C, N])
        rstd = sb("rstd", [C, N])
        par = sb("par", [C, PARAM_COLS])
        cst = sb("cst", [C, CONST_COLS])
        quiet = sb("quiet", [C, 512], BF16)
        wa = sb("wa", [C, E, 1024])
        wb = sb("wb", [C, E, 1024])
        dft_x = sb("dft_x", [C, 2, QF * C])
        dft_k = sb("dft_k", [KK, QF * C])
        dft_o = sb("dft_o", [C, QF, PIX])
        shiftw = sb("shiftw", [C, 3, C])
        small = sb("small", [C, 1024])
        ps = ctx.enter_context(nc.psum_tensor("ps", [C, 8, 512], F32))

        with ExitStack() as scope:
            xp = sb("xp", [C, B, PAD, PAD], scope=scope)
            xph = sb("xph", [C, B, PAD, PAD], F32R, scope)
            xpl = sb("xpl", [C, B, PAD, PAD], F32R, scope)
            yp = sb("yp", [C, B, PAD, PAD], scope=scope)
            w33 = sb("w33", [C, 2, 9 * C], scope=scope)
            w33h = sb("w33h", [C, 2, 9 * C], F32R, scope)
            w33l = sb("w33l", [C, 2, 9 * C], F32R, scope)
            expo = sb("expo", [C, B, 2, PIX], scope=scope)
            bot = sb("bot", [C, N], scope=scope)
            bot_t = sb("bot_t", [C, TT, C], scope=scope)
            top = sb("top", [PAB, N], scope=scope)
            cen = sb("cen", [PAB, N], scope=scope)
            we = sb("we", [C, E * C], scope=scope)
            weh = sb("weh", [C, E * C], F32R, scope)
            wel = sb("wel", [C, E * C], F32R, scope)
        picked = bot[0:E, :]
        with ExitStack() as scope:
            img_t = sb("img_t", [C, TT, C], scope=scope)
            key_d = sb("key_d", [KK, B, KK], scope=scope)
            keye = sb("keye", [KK, N], scope=scope)
            key_t = sb("key_t", [C, TT, KK], scope=scope)
            filt = sb("filt", [C, 4, B, KK], scope=scope)
            filt_t = sb("filt_t", [KK, B * C], scope=scope)
            img_f = sb("img_f", [C, QF, B * C], scope=scope)
            prod_f = sb("prod_f", [C, QF, B * C], scope=scope)
        pos = img_f[:, 0:3, :].rearrange("p a (b c) -> p (a b) c", b=4)
        hat = prod_f[:, 0:3, :].rearrange("p a (b c) -> p (a b) c", b=4)
        spread = img_t[:, 0:4, :]
        fm = sq
        with ExitStack() as scope:
            hid = sb("hid", [C, 2, 4, 512], scope=scope)
            hidh = sb("hidh", [C, 2, 4, 512], F32R, scope)
            hidl = sb("hidl", [C, 2, 4, 512], F32R, scope)
            rows = sb("rows", [E, N], scope=scope)
            scores_all = sb("scores_all", [C, 2, N], scope=scope)
            wst_h = sb("wst_h", [C, 2, 1024], F32R, scope)
            wst_l = sb("wst_l", [C, 2, 1024], F32R, scope)
        parts = rstd

        at = [0]

        def piece(cols, rows=C):
            at[0] += cols
            assert at[0] <= 1024
            return small[0:rows, at[0] - cols:at[0]]

        mx, mx4, mxd, nmx, es, rs = piece(4), piece(1, B), piece(4, B), piece(4), piece(4), piece(4)
        plan, r8, r8b, top8 = piece(64), piece(8), piece(8), piece(8, E)
        pick_w, cnt = piece(64), piece(8)
        kmx, kbias, kes, krs = [piece(4, KK) for _ in range(4)]
        st = piece(4)
        pool4, wpool, gate4 = piece(4), piece(12), piece(4)
        lg, lg2, ew, oh1, oh2, wgt, rem, tops, pair, m8 = [piece(64) for _ in range(9)] + [piece(8)]
        neg_wf, neg_b, bias1 = piece(1), piece(1), piece(4)
        gate, share = oh1, oh2

        def p(name, rows=C):
            at0, cols = PARAM[name]
            return par[0:rows, at0:at0 + cols]

        def k(name, rows=C):
            at0, cols = CONST[name]
            return cst[0:rows, at0:at0 + cols]

        ident = k("ident")

        def half(t, h):
            return t[:, h * HALF:(h + 1) * HALF]

        def bank(n, rows=C, cols=512, first=0):
            return ps[0:rows, n, first:first + cols]

        def f32(t):
            return t.bitcast(F32)

        def tiles(t):
            return t.rearrange("p (t e) -> p t e", e=E)

        def over(t, n):
            return t.unsqueeze(2).to_broadcast([t.shape[0], t.shape[1], n])

        def again(t, n):
            return t.unsqueeze(1).to_broadcast([t.shape[0], n, t.shape[1]])

        def inside(t, b):
            return t[:, b, 1:1 + SIDE, 1:1 + SIDE]

        def x_ready(eng, version, h):
            if version == 0:
                eng.wait_ge(s[f"x{h}_loaded"], 16)
            elif version in (4, 6, 8):
                eng.wait_ge(s["state_added"], UNITS * (version // 2 - 1) - 1 + h)
            else:
                eng.wait_ge(s[f"x{version}_ready"], h + 1)

        def wait_count(eng, name, value):
            if not isinstance(value, int) or value > 0:
                eng.wait_ge(s[name], value)

        CHUNKS = [sum(MOE[j]["q"] for j in range(m)) * UNITS for m in range(3)]

        block = ctx.enter_context(nc.Block())

        @block.sync
        def _(sp):
            def load_scores(m, e, q):
                sp.dma_start(scores_all[:, q, :], dram["rows"][m, bass.ds(e, 1), :].to_broadcast([C, N])).then_inc(s[f"scores{q}_in"], 16)

            def spread_scores(m):
                sp.wait_ge(s["rows_ready"], 2 * m + 2)
                sp.dma_start(dram["rows"][m], rows[:]).then_inc(s["rows_stored"], 16)
                sp.wait_ge(s["rows_stored"], 16 * (m + 1))
                for q in range(2):
                    wait_count(sp, "scaled", UNITS * m + 2 * (q - 1))
                    load_scores(m, q, q)
                with sp.Fori(0, E // 2 - 1) as i:
                    for q in range(2):
                        sp.wait_ge(s["scaled"], i * 4 + (UNITS * m + 2 * (q + 1)))
                        load_scores(m, i * 2 + (q + 2), q)

            sp.dma_start(cst[:, 0:NORM_CONSTS], dram["consts"][:, 0:NORM_CONSTS]).then_inc(s["norm_consts_loaded"], 16)
            for h in range(2):
                sp.dma_start(half(x, h).rearrange("p (b n) -> p b n", b=2),
                             dram["x"][2 * h:2 * h + 2].rearrange("b c n -> c b n")).then_inc(s[f"x{h}_loaded"], 16)
            sp.dma_start(par[:], dram["params"]).then_inc(s["params_loaded"], 16)
            sp.dma_start(w33[:, 0], dram["w_bottom"]).then_inc(s["wb_loaded"], 16)
            sp.dma_start(cst[:, NORM_CONSTS:], dram["consts"][:, NORM_CONSTS:]).then_inc(s["consts_loaded"], 16)
            sp.dma_start(w33[:, 1], dram["w_out"]).then_inc(s["wo_loaded"], 16)
            sp.dma_start(we[:], dram["w_experts"]).then_inc(s["we_loaded"], 16)
            sp.dma_start(wa[:], dram["moe1"]).then_inc(s["moe1_loaded"], 16)
            sp.dma_start(dft_x[:], dram["dft_x"]).then_inc(s["dft_loaded"], 16)
            sp.dma_start(dft_k[:], dram["dft_k"]).then_inc(s["dft_loaded"], 16)
            sp.dma_start(dft_o[:], dram["dft_o"]).then_inc(s["dft_loaded"], 16)
            sp.wait_ge(s["x2_ready"], 2)
            sp.dma_start(wb[:], dram["moe2"]).then_inc(s["moe2_loaded"], 16)
            spread_scores(0)
            sp.wait_ge(s["w2_split"], E)
            sp.dma_start(wa[:, :, 0:512], dram["moe3"]).then_inc(s["moe3_loaded"], 16)
            spread_scores(1)
            spread_scores(2)
            for h in range(2):
                x_ready(sp, 8, h)
                sp.dma_start(out[2 * h:2 * h + 2].rearrange("b c n -> c b n"),
                             half(x, h).rearrange("p (b n) -> p b n", b=2)).then_inc(s["stored"], 16)
            sp.wait_ge(s["stored"], 32)

        @block.gpsimd
        def _(pool):
            pool.memset(quiet[:], 0.0).then_inc(s["quiet_zero"], 1)
            pool.memset(xp[:], 0.0).then_inc(s["borders_zero"], 1)
            pool.memset(yp[:], 0.0).then_inc(s["borders_zero"], 1)

            def split(hi, lo, src, done, n):
                pool.tensor_copy(hi, src).then_inc(s["pool_step"], 1)
                pool.wait_ge(s["pool_step"], n)
                pool.tensor_tensor(lo, src, f32(hi), ALU.subtract).then_inc(done, 1)

            pool.wait_ge(s["wb_loaded"], 16)
            split(w33h[:, 0], w33l[:, 0], w33[:, 0], s["wb_split"], 1)
            pool.wait_ge(s["wo_loaded"], 16)
            split(w33h[:, 1], w33l[:, 1], w33[:, 1], s["wo_split"], 2)
            pool.wait_ge(s["we_loaded"], 16)
            split(weh[:], wel[:], we[:], s["we_split"], 3)

            gated = wb[:, POOL_T:TT]
            pool.wait_ge(s["expert_kept"], 2 * TT)
            pool.wait_ge(s["gate_ready"], 1)
            for t in range(POOL_T, TT):
                tile = wb[:, t, :].rearrange("p (e c) -> p e c", c=C)
                pool.tensor_tensor(tile, tile, over(gate[:, t * E:(t + 1) * E], C), ALU.mult).then_inc(s["pool_gated"], 1)
            pool.wait_ge(s["pool_gated"], TT - POOL_T)
            for i, w in enumerate((4 * C, 2 * C)):
                pool.tensor_tensor(gated[:, :, 0:w], gated[:, :, 0:w], gated[:, :, w:2 * w], ALU.add).then_inc(s["pool_sum"], 1)
                pool.wait_ge(s["pool_sum"], i + 1)
            pool.tensor_tensor(sq.rearrange("p (t c) -> p t c", c=C)[:, POOL_T:TT, :], gated[:, :, 0:C],
                               gated[:, :, C:2 * C], ALU.add).then_inc(s["pool_sum"], 1)

            for m, spec in enumerate(MOE):
                src = wb if spec["layer"] == 2 else wa
                unit0 = UNITS * m
                if m == 0:
                    x_ready(pool, 2, 1)
                pool.wait_ge(s[f"moe{spec['layer']}_loaded"], 16)

                def split_half(e, q, first, done):
                    at0, at1 = first * spec["q"] * C, (first + 1) * spec["q"] * C
                    pool.tensor_copy(wst_h[:, q, at0:at1], src[:, e, at0:at1])
                    pool.drain()
                    pool.tensor_tensor(wst_l[:, q, at0:at1], src[:, e, at0:at1], f32(wst_h[:, q, at0:at1]),
                                       ALU.subtract).then_inc(s[done], 1)

                def split_first(e, q):
                    wait_count(pool, "hidden_sums", e * (2 * spec["q"]) + (CHUNKS[m] - 2 * spec["q"]))
                    split_half(e, q, 0, "w1_split")

                def split_second(e, q, high_by_act=False):
                    if high_by_act:
                        at0, at1 = spec["q"] * C, 2 * spec["q"] * C
                        pool.tensor_tensor(wst_l[:, q, at0:at1], src[:, e, at0:at1], f32(wst_h[:, q, at0:at1]),
                                           ALU.subtract).then_inc(s["w2_split"], 1)
                        return
                    wait_count(pool, "part_sums", e * 2 + (unit0 - 2))
                    split_half(e, q, 1, "w2_split")

                def add_parts(e, halves=(0, 1), high_by_act=False):
                    for h in halves:
                        if high_by_act and h == 1:
                            pool.wait_ge(s["w2_high"], e + 1)
                        pool.wait_ge(s["scaled"], e * 2 + (unit0 + h + 1))
                        pool.tensor_tensor(half(x, h), half(x, h), half(parts, h), ALU.add).then_inc(s["state_added"], 1)

                for q in range(2):
                    split_first(q, q)
                    split_second(q, q)
                with pool.Fori(0, E // 2 - 1) as i:
                    for q in range(2):
                        split_first(i * 2 + (q + 2), q)
                        add_parts(i * 2 + q, high_by_act=spec["layer"] == 3)
                        split_second(i * 2 + (q + 2), q, spec["layer"] == 3)
                add_parts(E - 2)

        @block.tensor
        def _(pe):
            def mm3(o, wh, wl, xhi, xlo, start=True, stop=True):
                pe.matmul(o, wh, xhi, start=start, stop=False)
                pe.matmul(o, wl, xhi, start=False, stop=False)
                return pe.matmul(o, wh, xlo, start=False, stop=stop)

            def center(n, h):
                x_ready(pe, n, h)
                pe.matmul(bank(h), k("center"), half(x, h), start=True, stop=True).then_inc(s["centered"], 1)

            def variance(n, h):
                pe.wait_ge(s["squared"], 2 * n + h + 1)
                pe.matmul(bank(2 + h), k("mean"), half(sq, h), start=True, stop=True).then_inc(s["variance"], 1)

            def norm(n, halves=(0, 1)):
                for h in halves:
                    center(n, h)
                for h in halves:
                    variance(n, h)

            def keep_clock(n, b):
                for _ in range(n):
                    pe.matmul(bank(b), quiet[:, 0:C], quiet[:], start=True, stop=True)

            pe.wait_ge(s["quiet_zero"], 1)
            keep_clock(START_CLOCK, 7)
            pe.wait_ge(s["norm_consts_loaded"], 16)
            norm(0)
            pe.wait_ge(s["params_loaded"], 16)
            for h in range(2):
                pe.wait_ge(s["normed"], h + 1)
                window = xp[:, 2 * h:2 * h + 2, 1:1 + SIDE, 1:1 + SIDE]
                for w, b0 in (("w_top", 0), ("w_center", 2)):
                    pe.matmul(bank(b0 + h, PAB), p(w), window, start=True, stop=True).then_inc(s["proj_done"], 1)

            def conv33(which, hi, lo, hi_done, lo_done, n0, done, halves=(0, 1), between={}):
                for h in halves:
                    pe.wait_ge(hi_done, n0 + h + 1)
                    pe.wait_ge(lo_done, n0 + h + 1)
                    for t in range(9):
                        if (h, t) in between:
                            between[h, t]()
                        dy, dx = divmod(t, 3)
                        wh = w33h[:, which, t * C:(t + 1) * C]
                        wl = w33l[:, which, t * C:(t + 1) * C]
                        win = (slice(None), slice(2 * h, 2 * h + 2), slice(dy, dy + SIDE), slice(dx, dx + SIDE))
                        last = mm3(bank(4 + h), wh, wl, hi[win], lo[win], start=(t == 0), stop=(t == 8))
                    last.then_inc(done, 1)

            def scores(b):
                pe.wait_ge(s["top_ready"], b // 2 + 1)
                pe.wait_ge(s["center_ready"], b // 2 + 1)
                if b == 0:
                    pe.wait_ge(s["top_ready"], 2)
                    pe.wait_ge(s["center_ready"], 2)
                for j in range(2):
                    last = pe.matmul(bank(b, cols=PIX, first=j * PIX), top[:, b * PIX + j * C:b * PIX + (j + 1) * C],
                                     cen[:, b * PIX:(b + 1) * PIX], start=True, stop=True)
                last.then_inc(s["scores_done"], 1)

            def turn_max():
                pe.wait_ge(s["consts_loaded"], 16)
                pe.wait_ge(s["score_max"], B)
                pe.transpose(bank(6, B, C), mx, ident).then_inc(s["max_turned"], 1)

            def spread_max():
                pe.wait_ge(s["max_diag"], 1)
                pe.matmul(bank(6, cols=B, first=256), k("ones", B), mxd, start=True, stop=True).then_inc(s["max_spread"], 1)

            pe.wait_ge(s["wb_split"], 1)
            conv33(0, xph, xpl, s["norm_hi"], s["norm_lo"], 0, s["bottom_done"],
                   between={**{(0, 3 + b): lambda b=b: scores(b) for b in range(B)}, (1, 0): turn_max, (1, 1): spread_max})
            pe.wait_ge(s["neg_max"], 1)
            for t in range(TT):
                if t % 4 == 0:
                    pe.wait_ge(s["bottom_biased"], t // 4 + 1)
                last = pe.transpose(bank(6 + t // 4, cols=C, first=t % 4 * C), bot[:, t * C:(t + 1) * C], ident)
                if t % 4 == 3:
                    last.then_inc(s["bottom_turned"], 1)
            pe.wait_ge(s["exp_done"], B)
            pe.matmul(bank(4, cols=B), k("ones"), es, start=True, stop=True).then_inc(s["exp_summed"], 1)
            pe.wait_ge(s["bottom_ready"], 2)
            for b in range(B):
                for par_ in range(2):
                    for j in range(2):
                        last = pe.matmul(bank(6 + b // 2, cols=C, first=(b % 2) * PIX + par_ * C),
                                         expo[:, b, j, par_::2], bot_t[:, 2 * b + j, :], start=(j == 0), stop=(j == 1))
                last.then_inc(s["mixed"], 1)
            def gates(h):
                pe.wait_ge(s["normed"], 3 + h)
                if h == 0:
                    pe.wait_ge(s["x1_ready"], 1)
                for t in range(4 * h, 4 * h + 4):
                    last = pe.matmul(bank(4, cols=E, first=t * E), xn[:, t * C:(t + 1) * C], p("gate_w"), start=True, stop=True)
                return last

            pe.wait_ge(s["wo_split"], 1)
            pe.wait_ge(s["exp_recip"], 1)
            conv33(1, xph, xpl, s["mix_hi"], s["mix_lo"], 0, s["out_conv_done"],
                   between={(1, 2): lambda: center(1, 0), (1, 4): lambda: variance(1, 0)})

            gates(0)
            norm(1, halves=(1,))
            gates(1).then_inc(s["gates_done"], 1)
            pe.wait_ge(s["norm_hi"], 4)
            pe.wait_ge(s["norm_lo"], 4)
            pe.wait_ge(s["we_split"], 1)
            ring = [0, 1, 6, 7]

            def expert_rows(n):
                t, g = divmod(n, 2)
                if n >= 4:
                    pe.wait_ge(s["expert_kept"], n - 3)
                o = bank(ring[n % 4])
                cols, ecols = slice(t * C, (t + 1) * C), slice(g * 512, (g + 1) * 512)
                pe.matmul(o, xh[:, cols], weh[:, ecols], start=True, stop=False)
                pe.matmul(o, xh[:, cols], wel[:, ecols], start=False, stop=False)
                pe.matmul(o, xl[:, cols], weh[:, ecols], start=False, stop=True).then_inc(s["expert_out"], 1)

            for it in range(8):
                pe.wait_ge(s["sink_in"], it + 1)
                pe.matmul(bank(5, cols=64), k("ones"), plan, start=True, stop=True).then_inc(s["sink_sum"], 1)
                expert_rows(2 * it)
                expert_rows(2 * it + 1)
            pe.wait_ge(s["sink_in"], 9)
            for t in range(TT):
                last = pe.transpose(bank(2 + t // 4, E, C, t % 4 * C), plan[:, t * E:(t + 1) * E], ident)
            last.then_inc(s["plan_turned"], 1)
            pe.wait_ge(s["expert_kept"], 2 * TT)
            for e in range(E):
                if e == E - 1:
                    pe.wait_ge(s["picked"], 1)
                    for t in range(TT):
                        last = pe.transpose(bank(4, cols=E, first=64 + t * E), picked[:, t * C:(t + 1) * C], ident[0:E, 0:E])
                    last.then_inc(s["picked_turned"], 1)
                pe.wait_ge(s["gated"], e + 1)
                pe.matmul(bank(0), ident, wb[:, 0:4, e * C:(e + 1) * C], start=(e == 0), stop=(e == E - 1))
                last = pe.matmul(bank(1, cols=C), ident, wb[:, 4, e * C:(e + 1) * C], start=(e == 0), stop=(e == E - 1))
            last.then_inc(s["gated_sum"], 1)
            keep_clock(2, 5)
            for t in range(TT):
                if t % 4 == 0:
                    pe.wait_ge(s["combined"], 1 + t // 2)
                last = pe.transpose(bank(6 + t // 4, cols=C, first=t % 4 * C), sq[:, t * C:(t + 1) * C], ident)
                if t % 4 == 3:
                    last.then_inc(s["combined_turned"], 1)

            keep_clock(3, 5)
            norm(2)
            for h in range(2):
                pe.wait_ge(s["normed"], 5 + h)
                pe.matmul(bank(4 + h, KK), p("K_w"), half(xn, h), start=True, stop=True).then_inc(s["keys_done"], 1)
            for t in range(TT):
                last = pe.transpose(bank(6 + t // 4, cols=C, first=t % 4 * C), xn[:, t * C:(t + 1) * C], ident)
                if t % 4 == 3:
                    last.then_inc(s["img_turned"], 1)
            def img_pieces(*numbers):
                for n in numbers:
                    q, j = divmod(n, 2)
                    if n == 8:
                        pe.wait_ge(s["img_freq_kept"], 1)
                    ins = pe.matmul(bank(q % 4), dft_x[:, j, q * C:(q + 1) * C],
                                    img_t.rearrange("p (b j) c -> p j b c", j=2)[:, j], start=(j == 0), stop=(j == 1))
                    if j == 1:
                        ins.then_inc(s["img_freq"], 1)

            keep_clock(3, 3)
            pe.wait_ge(s["img_ready_act"], 1)
            pe.wait_ge(s["img_ready_dve"], 1)
            pe.wait_ge(s["dft_loaded"], 48)
            img_pieces(0)
            pe.wait_ge(s["key_diag"], 1)
            for t in range(TT):
                last = pe.matmul(bank(4, cols=KK, first=t * KK), keye[:, t * C:(t + 1) * C], key_d[:, t // 2, :],
                                 start=True, stop=True)
            last.then_inc(s["key_turned"], 1)
            img_pieces(1)
            pe.wait_ge(s["key_ready"], 1)
            for b in range(B):
                for j in range(2):
                    last = pe.matmul(bank(5, cols=KK, first=b * KK), img_t[:, 2 * b + j, :], key_t[:, 2 * b + j, :],
                                     start=(j == 0), stop=(j == 1))
            last.then_inc(s["filt_done"], 1)
            img_pieces(2)
            pe.wait_ge(s["filt_in"], 1)
            pe.matmul(bank(6, cols=B * KK), p("conv0_w"), filt[:, 0].rearrange("p b k -> p (b k)"),
                      start=True, stop=True).then_inc(s["filt0_done"], 1)
            for i, numbers in enumerate([(3,), (4, 5)]):
                img_pieces(*numbers)
                pe.wait_ge(s["stat_in"], i + 1)
                pe.matmul(bank(7, cols=B, first=B * i), k("ones"), st, start=True, stop=True).then_inc(s["stat_sum"], 1)
            img_pieces(6, 7)
            pe.wait_ge(s["filt_act"], 1)
            for b in range(B):
                last = pe.matmul(bank(4, KK, C, b * C), filt[:, 3, b, :], p("conv1_w"), start=True, stop=True)
            last.then_inc(s["filt1_done"], 1)
            img_pieces(8, 9)
            pe.wait_ge(s["filt1_ready"], 1)
            fring = [5, 6, 7]

            def filt_freq(q):
                if q >= 3:
                    pe.wait_ge(s["freq_mult"], q - 2)
                pe.matmul(bank(fring[q % 3]), dft_k[:, q * C:(q + 1) * C], filt_t[:], start=True, stop=True).then_inc(s["filt_freq"], 1)

            filt_freq(0)
            filt_freq(1)
            pe.wait_ge(s["img_freq_kept"], QF)
            for q in range(QF):
                if q + 2 < QF:
                    filt_freq(q + 2)
                pe.wait_ge(s["freq_mult"], q + 1)
                for b in range(B):
                    last = pe.matmul(bank(b, cols=PIX), prod_f[:, q, b * C:(b + 1) * C], dft_o[:, q, :],
                                     start=(q == 0), stop=(q == QF - 1))
                    if q == QF - 1 and b % 2:
                        last.then_inc(s["img_back"], 1)

            def mixture(m):
                spec = MOE[m]
                q_n, n = spec["q"], spec["ln"]
                sets = 4 // q_n
                norm(n)
                keep_clock(5, 7)
                for h in range(2):
                    pe.wait_ge(s["normed"], 2 * n + h + 1)
                    for t in range(4 * h, 4 * h + 4):
                        last = pe.matmul(bank(4, cols=E, first=t * E), xn[:, t * C:(t + 1) * C], p(spec["router"]),
                                         start=True, stop=True)
                last.then_inc(s["logits_done"], 1)

                def front(e, h, q, peeled=False):
                    if h == 0:
                        pe.wait_ge(s["w1_split"], e + (E * m + 1))
                    for f in range(q_n):
                        if not peeled and (sets == 1 or not isinstance(e, int) or e > 0):
                            wait_count(pe, "hidden", e * (2 * q_n) + (CHUNKS[m] + q_n * (h - sets) + f + 1))
                        mm3(bank(h % sets * q_n + f), wst_h[:, q, f * C:(f + 1) * C], wst_l[:, q, f * C:(f + 1) * C],
                            half(xh, h), half(xl, h)).then_inc(s["hidden_sums"], 1)

                def back(e, h, q, columns=(slice(0, HALF),)):
                    wait_count(pe, "scaled", e * 2 + (UNITS * m + h - (3 if m else 1)))
                    if h == 0:
                        pe.wait_ge(s["w2_split"], e + (E * m + 1))
                    for cols in columns:
                        o = bank(6 - 2 * q + h)
                        if cols is not columns[-1]:
                            pe.wait_ge(s["scaled"], UNITS * (m + 1) - 3)
                            o = bank(6)
                        for f in range(q_n):
                            pe.wait_ge(s["hidden_lo"], e * (2 * q_n) + (CHUNKS[m] + q_n * h + f + 1))
                            first = (q_n + f) * C
                            last = mm3(o[:, cols], wst_h[:, q, first:first + C], wst_l[:, q, first:first + C],
                                       hidh[:, h, f, cols], hidl[:, h, f, cols], start=(f == 0), stop=(f == q_n - 1))
                        last.then_inc(s["part_sums" if cols is columns[-1] else "last_sums"], 1)

                def expert(e, q):
                    front(e, 1, q)
                    back(e, 0, q)
                    front(e + 1, 0, 1 - q)
                    back(e, 1, q)

                pe.wait_ge(s["norm_hi"], 4 + 2 * m + 1)
                pe.wait_ge(s["norm_lo"], 4 + 2 * m + 1)
                front(0, 0, 0, peeled=True)
                pe.wait_ge(s["norm_hi"], 4 + 2 * m + 2)
                pe.wait_ge(s["norm_lo"], 4 + 2 * m + 2)
                front(0, 1, 0)
                pe.wait_ge(s["routed"], m + 1)
                for t in range(TT):
                    last = pe.transpose(bank(4 + t // 4, E, C, t % 4 * C), wgt[:, t * E:(t + 1) * E], ident)
                    if t % 4 == 3:
                        last.then_inc(s["route_turned"], 1)
                back(0, 0, 0)
                front(1, 0, 1)
                pe.wait_ge(s["rows_ready"], 2 * m + 2)
                back(0, 1, 0)
                with pe.Fori(0, E // 2 - 1) as i:
                    for q in range(2):
                        expert(i * 2 + (1 + q), 1 - q)
                front(E - 1, 1, 1)
                back(E - 1, 0, 1)
                back(E - 1, 1, 1, LAST_COLUMNS)

            mixture(0)

            norm(4)
            keep_clock(10, 7)
            for b in range(B):
                if b % 2 == 0:
                    pe.wait_ge(s["pooled_in"], b // 2 + 1)
                    if b:
                        pe.wait_ge(s["normed"], 10)
                pe.matmul(bank(b if b in (0, 3) else 7 - b, cols=3 * C), spread[:, b, :], shiftw.rearrange("p k i -> p (k i)"),
                          start=True, stop=True).then_inc(s["offset_done"], 1)
            for b in range(B):
                keep_clock(3, 7)
                pe.wait_ge(s["hat_ready"], b + 1)
                for j in range(3):
                    last = pe.matmul(bank(2 - b // 2, cols=1, first=b), hat[:, 3 * b + j, :], wpool[:, 3 * b + j:3 * b + j + 1],
                                     start=(j == 0), stop=(j == 2))
                if b % 2:
                    last.then_inc(s["deform_done"], 1)
            keep_clock(3, 7)
            mixture(1)

            norm(6)
            keep_clock(10, 7)
            for b in range(B):
                if b == 2:
                    keep_clock(1, 7)
                if b % 2 == 0:
                    pe.wait_ge(s["alpha_in"], b // 2 + 1)
                last = pe.matmul(bank(b // 2, cols=PIX, first=b % 2 * PIX), spread[:, b, :],
                                 xn[:, b * PIX:(b + 1) * PIX], start=True, stop=True)
                if b % 2:
                    last.then_inc(s["sal_done"], 1)
            keep_clock(4, 7)
            mixture(2)

        @block.scalar
        def _(act):
            def norm(n, split=None):
                if n == 0:
                    act.wait_ge(s["norm_consts_loaded"], 16)
                if n in (0, 4, 6):
                    act.preload_act_table_set("natural_log_exp_and_others")
                def square(h):
                    act.wait_ge(s["centered"], 2 * n + h + 1)
                    act.activation(half(sq, h), bank(h), ACT.Square).then_inc(s["squared"], 1)

                def inverse_root(h):
                    act.wait_ge(s["variance"], 2 * n + h + 1)
                    act.activation(half(rstd, h), bank(2 + h), ACT.Ln, bias=k(LN_EPS[n])).then_inc(s["log_var"], 1)
                    act.wait_ge(s["log_var"], 2 * n + h + 1)
                    act.activation(half(rstd, h), half(rstd, h), ACT.Exp, scale=-0.5).then_inc(s["rstd"], 1)

                def high_part(h):
                    if split is not None:
                        act.wait_ge(s["normed"], 2 * n + h + 1)
                        act.activation(half(xh, h), half(xn, h), ACT.Copy).then_inc(s["norm_hi"], 1)

                if n == 1:
                    for h in range(2):
                        square(h)
                        inverse_root(h)
                        high_part(h)
                else:
                    for work in (square, inverse_root, high_part):
                        for h in range(2):
                            work(h)
                            if n == 7 and work is square and h == 0:
                                act.preload_act_table_set("natural_log_exp_and_others")

            norm(0)
            for h in range(2):
                act.wait_ge(s["normed"], h + 1)
                act.activation(xph[:, 2 * h:2 * h + 2].rearrange("p b y x -> p (b y x)"),
                               xp[:, 2 * h:2 * h + 2].rearrange("p b y x -> p (b y x)"), ACT.Copy).then_inc(s["norm_hi"], 1)
            for h in range(2):
                act.wait_ge(s["proj_done"], 2 * h + 1)
                act.activation(half(top, h), bank(h, PAB), ACT.Identity, bias=p("b_top", PAB)).then_inc(s["top_ready"], 1)
            def bottom_bias(h):
                act.wait_ge(s["bottom_done"], h + 1)
                act.activation(half(bot, h), bank(4 + h), ACT.Identity, bias=p("b_bottom")).then_inc(s["bottom_biased"], 1)

            bottom_bias(0)
            for b in range(B):
                act.wait_ge(s["neg_max"], 1)
                act.activation(expo[:, b].rearrange("p j n -> p (j n)"), bank(b), ACT.Exp, bias=nmx[:, b:b + 1],
                               accum_out=es[:, b:b + 1]).then_inc(s["exp_done"], 1)
            bottom_bias(1)
            for h in range(2):
                act.wait_ge(s["mix_added"], 2 * h + 2)
                act.activation(xph[:, 2 * h:2 * h + 2].rearrange("p b y x -> p (b y x)"),
                               yp[:, 2 * h:2 * h + 2].rearrange("p b y x -> p (b y x)"), ACT.Copy).then_inc(s["mix_hi"], 1)
            norm(1, split=1)
            for n in range(2 * TT):
                act.wait_ge(s["expert_out"], n + 1)
                t, g = divmod(n, 2)
                act.activation(wb[:, t, g * 512:(g + 1) * 512], bank([0, 1, 6, 7][n % 4]), ACT.Copy).then_inc(s["expert_kept"], 1)
            act.wait_ge(s["expert_kept"], 2 * TT)
            act.wait_ge(s["gate_ready"], 1)
            for e in range(E):
                for t in range(POOL_T):
                    y = wb[:, t, e * C:(e + 1) * C]
                    last = act.activation(y, y, ACT.Copy, scale=gate[:, t * E + e:t * E + e + 1])
                last.then_inc(s["gated"], 1)
            norm(2)
            for b in range(B):
                if b % 2 == 0:
                    act.wait_ge(s["key_max"], b // 2 + 1)
                act.activation(keye[:, b * PIX:(b + 1) * PIX], bank(4 + b // 2, KK, PIX, b % 2 * PIX), ACT.Exp,
                               bias=kbias[:, b:b + 1], accum_out=kes[:, b:b + 1]).then_inc(s["key_exp"], 1)
                if b == 1:
                    act.wait_ge(s["img_turned"], 1)
                    act.activation(img_t[:, 0:4, :].rearrange("p t c -> p (t c)"), bank(6), ACT.Copy).then_inc(s["img_ready_act"], 1)
            for q in range(QF):
                act.wait_ge(s["img_freq"], q + 1)
                act.activation(img_f[:, q, :], bank(q % 4), ACT.Copy).then_inc(s["img_freq_kept"], 1)
                if q == 2:
                    act.wait_ge(s["stat_sum"], 2)
                    act.activation(st, bank(7, cols=B, first=B), ACT.Ln, bias=k("eps5"), scale=1.0 / (C * KK)).then_inc(s["filt_rstd_ln"], 1)
                    act.wait_ge(s["filt_rstd_ln"], 1)
                    act.activation(st, st, ACT.Exp, scale=-0.5).then_inc(s["filt_rstd"], 1)

            def mixture(m):
                spec = MOE[m]
                q_n, n = spec["q"], spec["ln"]
                func = {"Silu": ACT.Silu, "Gelu": ACT.Gelu, "Relu": ACT.Relu}[spec["act"]]
                norm(n, split=1)

                def route_exp():
                    act.wait_ge(s["exp_in"], m + 1)
                    act.activation(ew, lg2, ACT.Exp).then_inc(s["exp_out"], 1)

                if spec["act"] != "Relu":
                    route_exp()

                def hidden(e, h, after_first=None):
                    if spec["b1"] and h == 0:
                        act.wait_ge(s["hidden"], e * (2 * q_n) + CHUNKS[m])
                        act.activation(bias1[:, 0:q_n], p(spec["b1"]).rearrange("p (e f) -> p e f", f=q_n)[:, e, :],
                                       ACT.Copy).then_inc(s["bias_kept"], 1)
                        act.wait_ge(s["bias_kept"], e + (E * (m - 1) + 1))
                    wait_count(act, "part_sums", e * 2 + (UNITS * m + h - 1))
                    for f in range(q_n):
                        chunk = e * (2 * q_n) + (CHUNKS[m] + q_n * h + f + 1)
                        act.wait_ge(s["hidden_sums"], chunk)
                        bias = 0.0
                        if spec["b1"]:
                            bias = bias1[:, f:f + 1]
                        act.activation(hid[:, h, f, :], bank(h % (4 // q_n) * q_n + f), func, bias=bias).then_inc(s["hidden"], 1)
                        if f == 0 and after_first:
                            after_first()
                        if f % 2 == 0:
                            act.wait_ge(s["hidden"], chunk)
                            act.activation(hidh[:, h, f, :], hid[:, h, f, :], ACT.Copy).then_inc(s["hidden_hi_act"], 1)

                hidden(0, 0, after_first=route_exp if spec["act"] == "Relu" else None)
                hidden(0, 1)
                if spec["layer"] == 3:
                    for h in range(2):
                        act.wait_ge(s["route_turned"], 2 * m + h + 1)
                        act.activation(half(rows, h), bank(4 + h, E), ACT.Copy).then_inc(s["rows_ready"], 1)

                def second_high(e, q):
                    at0, at1 = q_n * C, 2 * q_n * C
                    act.wait_ge(s["part_sums"], e * 2 + (UNITS * m - 2))
                    act.activation(wst_h[:, q, at0:at1], wa[:, e, at0:at1], ACT.Copy).then_inc(s["w2_high"], 1)

                with act.Fori(0, E // 2 - 1) as i:
                    for q in range(2):
                        for h in range(2):
                            hidden(i * 2 + (1 + q), h)
                        if spec["layer"] == 3:
                            second_high(i * 2 + (2 + q), q)
                for h in range(2):
                    hidden(E - 1, h)

            mixture(0)
            norm(4)
            def gate_exp(h):
                act.wait_ge(s["deform_done"], h + 1)
                act.activation(gate4[:, 2 * h:2 * h + 2], bank(2 - h, cols=2, first=2 * h), ACT.Exp, bias=neg_b,
                               scale=-1.0).then_inc(s["deform_exp"], 1)

            for b in range(B):
                act.wait_ge(s["pos_ready"], b + 1)
                seg = pos[:, 3 * b:3 * b + 3, :].rearrange("p a c -> p (a c)")
                act.activation(seg, seg, ACT.Abs, bias=k("minus_i")).then_inc(s["dist_done"], 1)
                act.wait_ge(s["dist_done"], b + 1)
                act.activation(hat[:, 3 * b:3 * b + 3, :].rearrange("p a c -> p (a c)"), seg, ACT.Relu,
                               bias=1.0, scale=-1.0).then_inc(s["hat_ready"], 1)
                if b >= 2:
                    gate_exp(b - 2)
            mixture(1)
            norm(6)
            act.preload_act_table_set("sigmoid_and_others")
            for h in range(2):
                act.wait_ge(s["sal_done"], h + 1)
                act.activation(half(fm, h), bank(h), ACT.Relu).then_inc(s["sal_rectified"], 1)
                act.wait_ge(s["sal_ready"], h + 1)
                act.activation(half(fm, h), half(fm, h), ACT.Sigmoid, scale=p("scale")).then_inc(s["sal_sig"], 1)
            mixture(2)

        @block.vector
        def _(dve):
            steps = [0]

            def step(ins):
                steps[0] += 1
                ins.then_inc(s["dve_step"], 1)
                dve.wait_ge(s["dve_step"], steps[0])

            def norm(n, split=None):
                for h in range(2):
                    norm_half(n, h)
                if split is not None:
                    for h in range(2):
                        norm_low(n, h, split)

            def norm_half(n, h):
                dve.wait_ge(s["rstd"], 2 * n + h + 1)
                if n == 0:
                    dve.wait_ge(s["borders_zero"], 1)
                    dve.tensor_tensor(xp[:, 2 * h:2 * h + 2, 1:1 + SIDE, 1:1 + SIDE],
                                      bank(h).rearrange("p (b y x) -> p b y x", b=2, y=SIDE),
                                      half(rstd, h).rearrange("p (b y x) -> p b y x", b=2, y=SIDE),
                                      ALU.mult).then_inc(s["normed"], 1)
                else:
                    dve.tensor_tensor(half(xn, h), bank(h), half(rstd, h), ALU.mult).then_inc(s["normed"], 1)

            def norm_low(n, h, split):
                dve.wait_ge(s["norm_hi"], split + h + 1)
                dve.wait_ge(s["normed"], 2 * n + h + 1)
                dve.tensor_tensor(half(xl, h), half(xn, h), f32(half(xh, h)), ALU.subtract).then_inc(s["norm_lo"], 1)

            norm(0)
            for h in range(2):
                dve.wait_ge(s["norm_hi"], h + 1)
                dve.wait_ge(s["normed"], h + 1)
                seg = [t[:, 2 * h:2 * h + 2].rearrange("p b y x -> p (b y x)") for t in (xpl, xp, xph)]
                dve.tensor_tensor(seg[0], seg[1], f32(seg[2]), ALU.subtract).then_inc(s["norm_lo"], 1)
            dve.wait_ge(s["params_loaded"], 16)
            for h in range(2):
                dve.wait_ge(s["proj_done"], 2 * h + 2)
                dve.tensor_scalar(half(cen, h), bank(2 + h, PAB), p("b_center", PAB), None, ALU.add).then_inc(s["center_ready"], 1)
            for b in range(B):
                dve.wait_ge(s["scores_done"], b + 1)
                dve.tensor_reduce(mx[:, b:b + 1], bank(b), AX.X, ALU.max).then_inc(s["score_max"], 1)
            dve.wait_ge(s["max_turned"], 1)
            step(dve.tensor_reduce(mx4, bank(6, B, C), AX.X, ALU.max))
            dve.tensor_scalar(mxd, ident[0:B, 0:B], mx4, -1.0, ALU.mult, ALU.mult).then_inc(s["max_diag"], 1)
            dve.wait_ge(s["max_spread"], 1)
            dve.tensor_copy(nmx, bank(6, cols=B, first=256)).then_inc(s["neg_max"], 1)
            dve.wait_ge(s["consts_loaded"], 16)
            dve.wait_ge(s["params_loaded"], 16)
            shifts = k("shift").rearrange("p (d i) -> p d i", d=3)
            woff = p("w_offset")
            for j in range(3):
                step(dve.tensor_scalar(shiftw[:, j, :], shifts[:, 0, :], woff[:, 3 * j:3 * j + 1], None, ALU.mult))
                for d in range(1, 3):
                    step(dve.scalar_tensor_tensor(shiftw[:, j, :], shifts[:, d, :], woff[:, 3 * j + d:3 * j + d + 1],
                                                  shiftw[:, j, :], ALU.mult, ALU.add))
            step(dve.tensor_scalar(neg_wf, p("wf"), -1.0, None, ALU.mult))
            step(dve.memset(pair, -BIG))
            step(dve.tensor_scalar(neg_b, p("b_deform"), -1.0, None, ALU.mult))

            for g in range(2):
                dve.wait_ge(s["bottom_turned"], g + 1)
                dve.tensor_copy(bot_t[:, 4 * g:4 * g + 4, :].rearrange("p t c -> p (t c)"), bank(6 + g)).then_inc(s["bottom_ready"], 1)
            dve.wait_ge(s["exp_summed"], 1)
            dve.reciprocal(rs, bank(4, cols=B)).then_inc(s["exp_recip"], 1)
            dve.wait_ge(s["exp_recip"], 1)
            dve.wait_ge(s["borders_zero"], 2)
            for b in range(B):
                dve.wait_ge(s["mixed"], b // 2 * 2 + 2)
                dve.scalar_tensor_tensor(inside(yp, b), bank(6 + b // 2, cols=PIX, first=b % 2 * PIX).rearrange("p (y x) -> p y x", y=SIDE),
                                         rs[:, b:b + 1], inside(xp, b), ALU.mult, ALU.add).then_inc(s["mix_added"], 1)
                if b % 2:
                    h = b // 2
                    dve.wait_ge(s["mix_hi"], h + 1)
                    dve.wait_ge(s["mix_added"], b + 1)
                    seg = [t[:, 2 * h:2 * h + 2].rearrange("p b y x -> p (b y x)") for t in (xpl, yp, xph)]
                    dve.tensor_tensor(seg[0], seg[1], f32(seg[2]), ALU.subtract).then_inc(s["mix_lo"], 1)
            for h in range(2):
                dve.wait_ge(s["out_conv_done"], h + 1)
                dve.scalar_tensor_tensor(half(x, h), bank(4 + h), p("b_out"), half(x, h), ALU.add, ALU.add).then_inc(s["x1_ready"], 1)
                if h == 1:
                    norm_low(1, 0, 2)
                norm_half(1, h)
            norm_low(1, 1, 2)

            dve.wait_ge(s["gates_done"], 1)
            dve.tensor_scalar(plan, bank(4, cols=64), 1e-10, None, ALU.max).then_inc(s["sink_in"], 1)
            plan3 = tiles(plan)
            for it in range(8):
                dve.wait_ge(s["sink_sum"], it + 1)
                dve.wait_ge(s["sink_in"], it + 1)
                step(dve.tensor_reduce(r8, bank(5, cols=64).rearrange("p (t e) -> p e t", e=E), AX.X, ALU.add))
                step(dve.reciprocal(r8b, r8))
                step(dve.tensor_tensor(plan3, plan3, again(r8b, TT), ALU.mult))
                step(dve.tensor_reduce(r8, plan3, AX.X, ALU.add))
                step(dve.reciprocal(r8b, r8))
                dve.tensor_tensor(plan3, plan3, over(r8b, E), ALU.mult).then_inc(s["sink_in"], 1)
            dve.wait_ge(s["sink_in"], 9)
            dve.tensor_scalar(gate, plan, 0.5, None, ALU.is_gt).then_inc(s["gate_ready"], 1)
            dve.wait_ge(s["gate_ready"], 1)
            step(dve.tensor_reduce(r8, tiles(gate), AX.X, ALU.add))
            step(dve.tensor_scalar(r8, r8, 1.0, None, ALU.max))
            step(dve.reciprocal(r8b, r8))
            step(dve.tensor_tensor(tiles(share), tiles(gate), over(r8b, E), ALU.mult))
            dve.wait_ge(s["plan_turned"], 1)
            src = ps[0:E, 2:4, :].rearrange("p g n -> p (g n)")
            for r in range(TOPK0 // 8):
                step(dve.max(top8, src))
                last = dve.match_replace(picked, top8, src, -1.0)
                if r < TOPK0 // 8 - 1:
                    step(last)
                src = picked
            last.then_inc(s["picked"], 1)
            dve.wait_ge(s["picked_turned"], 1)
            step(dve.tensor_scalar(pick_w, bank(4, cols=64, first=64), 0.0, None, ALU.is_lt))
            step(dve.tensor_reduce(cnt, tiles(pick_w), AX.X, ALU.add))
            step(dve.tensor_tensor(pick_w, pick_w, share, ALU.mult))
            step(dve.tensor_scalar(cnt, cnt, 1.0, None, ALU.add))
            step(dve.tensor_reduce(r8, tiles(pick_w), AX.X, ALU.add))
            step(dve.reciprocal(r8b, cnt))
            step(dve.tensor_tensor(r8, r8, r8b, ALU.mult))
            sqt = sq.rearrange("p (t c) -> p t c", c=C)
            dve.wait_ge(s["gated_sum"], 1)
            dve.tensor_tensor(sqt[:, 0:4, :], bank(0).rearrange("p (t c) -> p t c", c=C), over(r8[:, 0:4], C),
                              ALU.mult).then_inc(s["combined"], 1)
            dve.tensor_scalar(sqt[:, 4, :], bank(1, cols=C), r8[:, 4:5], None, ALU.mult).then_inc(s["combined"], 1)
            dve.wait_ge(s["pool_sum"], 3)
            dve.tensor_tensor(sqt[:, POOL_T:TT, :], sqt[:, POOL_T:TT, :], over(r8[:, POOL_T:TT], C),
                              ALU.mult).then_inc(s["combined"], 1)
            for h in range(2):
                dve.wait_ge(s["combined_turned"], h + 1)
                dve.tensor_tensor(half(x, h), bank(6 + h), half(x, h), ALU.add).then_inc(s["x2_ready"], 1)

            norm(2)
            for h in range(2):
                ims = slice(2 * h, 2 * h + 2)
                dve.wait_ge(s["keys_done"], h + 1)
                step(dve.tensor_reduce(kmx[:, ims], bank(4 + h, KK).rearrange("p (b n) -> p b n", b=2), AX.X, ALU.max))
                step(dve.tensor_scalar(kmx[:, ims], kmx[:, ims], p("K_b", KK), None, ALU.add))
                dve.tensor_scalar(kbias[:, ims], kmx[:, ims], -1.0, p("K_b", KK), ALU.mult, ALU.add).then_inc(s["key_max"], 1)
            dve.wait_ge(s["img_turned"], 2)
            dve.tensor_copy(img_t[:, 4:8, :].rearrange("p t c -> p (t c)"), bank(7)).then_inc(s["img_ready_dve"], 1)
            dve.wait_ge(s["key_exp"], B)
            step(dve.reciprocal(krs, kes))
            dve.tensor_tensor(key_d[:], again(ident[0:KK, 0:KK], B), over(krs, KK), ALU.mult).then_inc(s["key_diag"], 1)
            dve.wait_ge(s["key_turned"], 1)
            dve.tensor_copy(key_t.rearrange("p t k -> p (t k)"), bank(4, cols=TT * KK)).then_inc(s["key_ready"], 1)
            dve.wait_ge(s["filt_done"], 1)
            f0, f1, f2, f3 = [filt[:, j] for j in range(4)]

            def flat(t):
                return t.rearrange("p b k -> p (b k)")

            dve.tensor_copy(flat(f0), bank(5, cols=B * KK)).then_inc(s["filt_in"], 1)
            dve.wait_ge(s["filt0_done"], 1)
            step(dve.tensor_scalar(flat(f1), bank(6, cols=B * KK), p("conv0_b"), None, ALU.add))
            dve.tensor_reduce(st, f1, AX.X, ALU.add).then_inc(s["stat_in"], 1)
            dve.wait_ge(s["stat_sum"], 1)
            step(dve.scalar_tensor_tensor(f1, over(bank(7, cols=B), KK), 1.0 / (C * KK), f1, ALU.mult, ALU.subtract))
            step(dve.tensor_tensor(f2, f1, f1, ALU.mult))
            dve.tensor_reduce(st, f2, AX.X, ALU.add).then_inc(s["stat_in"], 1)
            step(dve.scalar_tensor_tensor(f0, f1, -1.0, again(p("ln_w"), B), ALU.mult, ALU.mult))
            dve.wait_ge(s["filt_rstd"], 1)
            for b in range(B):
                last = dve.scalar_tensor_tensor(f1[:, b], f0[:, b], st[:, b:b + 1], p("ln_b"), ALU.mult, ALU.add)
            step(last)
            dve.tensor_scalar(flat(f3), flat(f1), 0.0, None, ALU.max).then_inc(s["filt_act"], 1)
            dve.wait_ge(s["filt1_done"], 1)
            dve.tensor_tensor(filt_t.rearrange("p (b c) -> p b c", b=B), bank(4, KK).rearrange("p (b c) -> p b c", b=B),
                              again(p("conv1_b", KK), B), ALU.add).then_inc(s["filt1_ready"], 1)
            for q in range(QF):
                dve.wait_ge(s["filt_freq"], q + 1)
                dve.wait_ge(s["img_freq_kept"], q + 1)
                dve.tensor_tensor(prod_f[:, q, :], bank([5, 6, 7][q % 3]), img_f[:, q, :], ALU.mult).then_inc(s["freq_mult"], 1)
            for h in range(2):
                dve.wait_ge(s["img_back"], h + 1)
                dve.tensor_tensor(half(x, h).rearrange("p (b n) -> p b n", b=2), ps[:, 2 * h:2 * h + 2, 0:PIX],
                                  half(x, h).rearrange("p (b n) -> p b n", b=2), ALU.add).then_inc(s["x3_ready"], 1)

            def mixture(m):
                spec = MOE[m]
                q_n, n = spec["q"], spec["ln"]
                def front(e, h, chunks=range(q_n)):
                    for f in chunks:
                        pair = e * q_n + (CHUNKS[m] // 2 + (q_n * h + f) // 2 + 1)
                        if f % 2 == 1:
                            dve.wait_ge(s["hidden"], e * (2 * q_n) + (CHUNKS[m] + q_n * h + f + 1))
                            dve.tensor_copy(hidh[:, h, f, :], hid[:, h, f, :]).then_inc(s["hidden_hi_dve"], 1)
                            dve.wait_ge(s["hidden_hi_dve"], pair)
                        else:
                            dve.wait_ge(s["hidden_hi_act"], pair)
                        dve.tensor_tensor(hidl[:, h, f, :], hid[:, h, f, :], f32(hidh[:, h, f, :]),
                                          ALU.subtract).then_inc(s["hidden_lo"], 1)

                norm(n, split=4 + 2 * m)
                dve.wait_ge(s["logits_done"], m + 1)
                if spec["layer"] == 3:
                    step(dve.tensor_tensor(tiles(lg), tiles(bank(4, cols=64)), again(p("bg3"), TT), ALU.add))
                else:
                    step(dve.tensor_copy(lg, bank(4, cols=64)))
                def largest():
                    for t in range(TT):
                        last = dve.max(tops[:, t * E:(t + 1) * E], lg[:, t * E:(t + 1) * E])
                        if t < TT - 1:
                            last.then_inc(s["dve_step"], 1)
                            steps[0] += 1
                    step(last)

                if spec["layer"] == 2:
                    step(dve.tensor_reduce(m8, tiles(lg), AX.X, ALU.max))
                else:
                    largest()
                first = m8 if spec["layer"] == 2 else tiles(tops)[:, :, 0]
                dve.tensor_tensor(tiles(lg2), tiles(lg), over(first, E), ALU.subtract).then_inc(s["exp_in"], 1)
                if spec["layer"] == 2:
                    dve.wait_ge(s["exp_out"], m + 1)
                    step(dve.tensor_reduce(r8, tiles(ew), AX.X, ALU.add))
                    step(dve.reciprocal(r8b, r8))
                    step(dve.tensor_tensor(tiles(lg), tiles(ew), over(r8b, E), ALU.mult))
                    largest()
                step(dve.tensor_copy(tiles(pair)[:, :, 0:2], tiles(tops)[:, :, 0:2]))
                for t in range(TT):
                    last = dve.match_replace(oh1[:, t * E:(t + 1) * E], pair[:, t * E:(t + 1) * E], lg[:, t * E:(t + 1) * E], BIG)
                    if t < TT - 1:
                        last.then_inc(s["dve_step"], 1)
                        steps[0] += 1
                step(last)
                dve.wait_ge(s["exp_out"], m + 1)
                values = lg if spec["layer"] == 2 else ew
                step(dve.scalar_tensor_tensor(wgt, oh1, BIG, values, ALU.is_equal, ALU.mult))
                step(dve.tensor_reduce(r8, tiles(wgt), AX.X, ALU.add))
                if spec["layer"] == 2:
                    step(dve.tensor_scalar(r8, r8, 1e-6, None, ALU.add))
                step(dve.reciprocal(r8b, r8))
                dve.tensor_tensor(tiles(wgt), tiles(wgt), over(r8b, E), ALU.mult).then_inc(s["routed"], 1)
                front(0, 0, range(q_n // 2))
                if spec["layer"] != 3:
                    for h in range(2):
                        dve.wait_ge(s["route_turned"], 2 * m + h + 1)
                        dve.tensor_copy(half(rows, h), bank(4 + h, E)).then_inc(s["rows_ready"], 1)
                front(0, 0, range(q_n // 2, q_n))

                def back(e, h, q, loads):
                    score = scores_all[:, q, :]
                    unit = e * 2 + (UNITS * m + h + 1)
                    dve.wait_ge(s["part_sums"], unit)
                    dve.wait_ge(s[f"scores{q}_in"], loads)
                    wait_count(dve, "state_added", e * 2 + (UNITS * m + h - 1))
                    if spec["b2"]:
                        dve.scalar_tensor_tensor(half(parts, h), bank(6 - 2 * q + h), p(spec["b2"])[:, bass.ds(e, 1)], half(score, h),
                                                 ALU.add, ALU.mult).then_inc(s["scaled"], 1)
                    else:
                        dve.tensor_tensor(half(parts, h), bank(6 - 2 * q + h), half(score, h), ALU.mult).then_inc(s["scaled"], 1)

                def expert(e, q, loads):
                    front(e, 1)
                    back(e, 0, q, loads)
                    front(e + 1, 0)
                    back(e, 1, q, loads)

                loads0 = 16 * (E // 2 * m + 1)
                front(0, 1)
                front(1, 0)
                back(0, 0, 0, loads0)
                back(0, 1, 0, loads0)
                with dve.Fori(0, E // 2 - 1) as i:
                    expert(i * 2 + 1, 1, i * 16 + loads0)
                    expert(i * 2 + 2, 0, i * 16 + (loads0 + 16))
                loads = 16 * (E // 2) * (m + 1)
                front(E - 1, 1)
                back(E - 1, 0, 1, loads)
                dve.wait_ge(s["state_added"], UNITS * (m + 1) - 2)
                dve.wait_ge(s["scaled"], UNITS * (m + 1) - 1)
                dve.tensor_tensor(half(x, 0), half(x, 0), half(parts, 0), ALU.add).then_inc(s["state_added"], 1)
                for cols in LAST_COLUMNS:
                    last = cols is LAST_COLUMNS[-1]
                    if last:
                        dve.wait_ge(s["part_sums"], UNITS * (m + 1))
                    else:
                        dve.wait_ge(s["last_sums"], m + 1)
                    sums, part = bank(5 if last else 6)[:, cols], half(parts, 1)[:, cols]
                    weight, state = half(scores_all[:, 1, :], 1)[:, cols], half(x, 1)[:, cols]
                    if spec["b2"]:
                        ins = dve.scalar_tensor_tensor(part, sums, p(spec["b2"])[:, E - 1:E], weight, ALU.add, ALU.mult)
                    else:
                        ins = dve.tensor_tensor(part, sums, weight, ALU.mult)
                    if last:
                        ins.then_inc(s["scaled"], 1)
                        dve.wait_ge(s["scaled"], UNITS * (m + 1))
                        dve.wait_ge(s["last_added"], m + 1)
                    else:
                        ins.then_inc(s["last_scaled"], 1)
                        dve.wait_ge(s["last_scaled"], m + 1)
                    dve.tensor_tensor(state, state, part, ALU.add).then_inc(s["state_added" if last else "last_added"], 1)

            def norm_and_pool(n, h):
                norm_half(n, h)
                dve.wait_ge(s["normed"], 2 * n + h + 1)
                step(dve.tensor_reduce(pool4[:, 2 * h:2 * h + 2], half(xn, h).rearrange("p (b n) -> p b n", b=2), AX.X, ALU.add))
                return pool4[:, 2 * h:2 * h + 2], spread[:, 2 * h:2 * h + 2, :]

            mixture(0)

            for h in range(2):
                pooled, spread_h = norm_and_pool(4, h)
                step(dve.tensor_scalar(pooled, pooled, 1.0 / PIX, None, ALU.mult))
                dve.tensor_copy(spread_h, over(pooled, C)).then_inc(s["pooled_in"], 1)
                step(dve.tensor_tensor(wpool[:, 6 * h:6 * h + 6].rearrange("p (b k) -> p b k", b=2), over(pooled, 3),
                                       again(p("w_deform"), 2), ALU.mult))
            for b in range(B):
                dve.wait_ge(s["offset_done"], b + 1)
                seg = pos[:, 3 * b:3 * b + 3, :].rearrange("p a c -> p (a c)")
                step(dve.tensor_tensor(seg, bank(b if b in (0, 3) else 7 - b, cols=3 * C), k("base"), ALU.add))
                dve.tensor_scalar(seg, seg, 0.0, C - 1.0, ALU.max, ALU.min).then_inc(s["pos_ready"], 1)
            for h in range(2):
                dve.wait_ge(s["deform_exp"], h + 1)
                g = gate4[:, 2 * h:2 * h + 2]
                step(dve.tensor_scalar(g, g, 1.0, None, ALU.add))
                step(dve.reciprocal(g, g))
                for b in (2 * h, 2 * h + 1):
                    cols = slice(b * PIX, (b + 1) * PIX)
                    last = dve.scalar_tensor_tensor(x[:, cols], xn[:, cols], gate4[:, b:b + 1], x[:, cols], ALU.mult, ALU.add)
                last.then_inc(s["x5_ready"], 1)
            mixture(1)

            for h in range(2):
                pooled, spread_h = norm_and_pool(6, h)
                step(dve.tensor_scalar(pooled, pooled, 1.0 / SALIENCY_AREA, 1.0 / C, ALU.mult, ALU.mult))
                dve.tensor_tensor(spread_h, over(pooled, C), again(p("conv_w"), 2), ALU.mult).then_inc(s["alpha_in"], 1)
            for h in range(2):
                dve.wait_ge(s["sal_rectified"], h + 1)
                dve.scalar_tensor_tensor(half(fm, h), half(fm, h), TH, half(fm, h), ALU.is_gt, ALU.mult).then_inc(s["sal_ready"], 1)
                dve.tensor_scalar(half(x, h), half(x, h), 1.0, None, ALU.add).then_inc(s["one_added"], 1)
                dve.wait_ge(s["sal_sig"], h + 1)
                dve.wait_ge(s["one_added"], h + 1)
                dve.scalar_tensor_tensor(half(x, h), half(fm, h), neg_wf, half(x, h), ALU.mult, ALU.add).then_inc(s["x7_ready"], 1)
            mixture(2)


def constants():
    cols = {
        "center": np.eye(C) - 1.0 / C, "mean": np.full((C, C), 1.0 / C), "ident": np.eye(C), "ones": np.ones((C, C)),
        "shift": np.concatenate([np.eye(C, k=1 - d) for d in range(3)], 1),
        "base": np.broadcast_to((np.arange(C)[None, :] + np.arange(3)[:, None] - 1).reshape(-1), (C, 3 * C)),
        "minus_i": -np.arange(C)[:, None],
        "eps6": np.full((C, 1), 1e-6), "eps5": np.full((C, 1), 1e-5),
    }
    packed = np.concatenate([cols[n] for n in CONST], 1).astype(np.float32)
    freqs = [(u, v) for u in range(GRID) for v in range(GRID)
             if (u, v) != (0, 0) and (u, v) < ((-u) % GRID, (-v) % GRID)]
    assert len(freqs) == FREQ
    fu, fv = (np.array([f[i] for f in freqs], np.float64) for i in range(2))
    y, xx = np.divmod(np.arange(PIX), SIDE)
    i, j = np.divmod(np.arange(KK), KW)
    angle = 2 * np.pi / GRID
    ta = angle * (np.outer(y, fu) + np.outer(xx, fv))
    tk = angle * (np.outer(i - KW // 2, fu) + np.outer(j - KW // 2, fv))
    ar, ai, br, bi = np.cos(ta), -np.sin(ta), np.cos(tk), np.sin(tk)
    pad = QF * C - 1 - 3 * FREQ

    def rows(first, a, b, c):
        n = first.shape[0]
        return np.concatenate([first, a, b, c, np.zeros((n, pad))], 1)

    to_x = rows(np.ones((PIX, 1)), ar + ai, ar, ai)
    to_k = rows(np.ones((KK, 1)), br, bi - br, br + bi)
    re, im = 2 * ar, 2 * ai
    back = rows(np.ones((PIX, 1)), re + im, im, -re).T / GRID ** 2
    f32 = np.float32
    return {
        "consts": packed,
        "dft_x": np.ascontiguousarray(to_x.reshape(2, C, QF * C).transpose(1, 0, 2)).astype(f32),
        "dft_k": np.ascontiguousarray(to_k).astype(f32),
        "dft_o": np.ascontiguousarray(back.reshape(QF, C, PIX).transpose(1, 0, 2)).astype(f32),
    }


def laid_out(a):
    def col(v, rows=C):
        m = np.zeros((C, v.shape[-1] if v.ndim > 1 else 1), np.float32)
        m[:v.shape[0]] = v.reshape(v.shape[0], -1)
        return m

    def every(v):
        v = np.asarray(v).reshape(1, -1)
        return np.broadcast_to(v, (C, v.shape[1]))

    par = {
        "b_bottom": col(a["L0_conv_b_bottom"]), "b_out": col(a["L0_conv_b_out"]),
        "b_top": col(a["L0_conv_b_top"]), "b_center": col(a["L0_conv_b_center"]),
        "w_top": a["L0_conv_w_top"][:, :, 0, 0].T, "w_center": a["L0_conv_w_center"][:, :, 0, 0].T,
        "gate_w": a["L0_ffn_gate_w"][0], "K_w": a["L1_conv_K_w"].T, "K_b": col(a["L1_conv_K_b"]),
        "conv0_w": a["L1_conv_conv0_w"].T, "conv0_b": col(a["L1_conv_conv0_b"]),
        "ln_w": a["L1_conv_ln_w"].reshape(C, KK), "ln_b": a["L1_conv_ln_b"].reshape(C, KK),
        "conv1_w": a["L1_conv_conv1_w"].T, "conv1_b": every(a["L1_conv_conv1_b"]), "Wg1": a["L1_ffn_Wg"],
        "w_offset": every(a["L2_conv_w_offset"]), "w_deform": every(a["L2_conv_w_deform"]),
        "b_deform": every(a["L2_conv_b_deform"]), "Wg2": a["L2_ffn_Wg"],
        "L2_b1": a["L2_ffn_b1"].reshape(E * 4, C).T, "L2_b2": a["L2_ffn_b2"].T,
        "conv_w": every(a["L3_conv_conv_w"]), "scale": every(a["L3_conv_scale"]), "wf": every(a["L3_conv_wf"]),
        "wg3": a["L3_ffn_wg"], "bg3": every(a["L3_ffn_bg"]),
        "L3_b1": a["L3_ffn_b1"].reshape(E * 2, C).T, "L3_b2": a["L3_ffn_b2"].T,
    }

    def experts(w1, w2, q):
        return np.concatenate([w1.transpose(1, 0, 2), w2.reshape(E, q, C, C).transpose(2, 0, 1, 3).reshape(C, E, q * C)], 2)

    return {
        "x": a["x"].reshape(B, C, PIX),
        "params": np.concatenate([par[n] for n in PARAM], 1),
        "w_bottom": a["L0_conv_w_bottom"].transpose(1, 2, 3, 0).reshape(C, 9 * C),
        "w_out": a["L0_conv_w_out"].transpose(1, 2, 3, 0).reshape(C, 9 * C),
        "w_experts": a["L0_ffn_experts"].transpose(1, 0, 2).reshape(C, E * C),
        "moe1": experts(a["L1_ffn_W1"], a["L1_ffn_W2"], 4),
        "moe2": experts(a["L2_ffn_W1"], a["L2_ffn_W2"], 4),
        "moe3": experts(a["L3_ffn_w1"], a["L3_ffn_w2"], 2),
    }


def kernel(**inputs):
    import concourse.bacc as bacc
    from concourse.bass_utils import run_bass_kernel_spmd as run

    nc = bacc.Bacc("TRN2", target_bir_lowering=False, num_devices=1)
    arrays, dram = {}, {}
    given = {**laid_out({n: np.asarray(v) for n, v in inputs.items()}), **constants()}
    for name, v in given.items():
        v = np.ascontiguousarray(v)
        arrays[f"in_{name}"] = v
        dram[name] = nc.dram_tensor(f"in_{name}", v.shape, mybir.dt.from_np(v.dtype), kind="ExternalInput").ap()
    dram["rows"] = nc.dram_tensor("rows_scratch", (len(MOE), E, N), F32, kind="Internal").ap()
    out = nc.dram_tensor("out_0", (B, C, PIX), F32, kind="ExternalOutput").ap()
    metaformer(nc, dram, out)
    r = run(nc, [arrays], core_ids=[0])
    return r.results[0]["out_0"].reshape(B, C, SIDE, SIDE)
```
